# Optimizing a Trainium2 kernel written in Bass

```python
import numpy as np
import jax
import jax.numpy as jnp

def _softmax(x, axis=-1):
    return jax.nn.softmax(x, axis=axis)

def _gelu(x):
    return jax.nn.gelu(x, approximate=True)

def _silu(x):
    return jax.nn.silu(x)

def _sigmoid(x):
    return jax.nn.sigmoid(x)

def _layernorm(x, axis=-1, eps=1e-05):
    m = jnp.mean(x, axis=axis, keepdims=True)
    v = jnp.var(x, axis=axis, keepdims=True)
    return (x - m) / jnp.sqrt(v + eps)

def _scatter_add(tgt, idx, src, axis=0):
    return tgt.at[idx].add(src)

def _segment_sum(src, seg, n):
    return jax.ops.segment_sum(src, seg, n)
kernel_name = 'mk_seq_preln_d2_jaxref_r8_d3adbd'

def setup_inputs(seed: int=0):
    np.random.seed(seed)
    _w = jnp.asarray

    def _L0_attn_setup():
        import jax, jax.numpy as jnp
        import numpy as np
        B, L, D, H = (2, 512, 128, 4)
        DK = D // H
        DV = D // H
        CONV_K = 4
        FIR_S, FIR_L = (5, 64)
        GATE_HID = D * 2 // 2
        CHUNK = 32
        FLOOR_EPS = 0.08
        GATE_BIAS = np.array([-0.5, -0.5, 1.0, 3.0], np.float32)
        GATE_LOGIT_INIT = float(np.log(np.expm1(0.7)))
        CONV_RES_INIT = float(np.log(0.1 / 0.9))

        def _l2norm(x):
            return x / jnp.sqrt(jnp.sum(x * x, -1, keepdims=True) + 1e-12)

        def _causal_dwconv(x, w):
            k = w.shape[-1]
            xp = jnp.pad(x, ((0, 0), (k - 1, 0), (0, 0))).transpose(0, 2, 1)
            y = jax.lax.conv_general_dilated(xp, w[:, None, :], (1,), 'VALID', feature_group_count=w.shape[0], dimension_numbers=('NCH', 'OIH', 'NCH'))
            return y.transpose(0, 2, 1)

        def _delta_chunkwise(q, k, v, beta):
            b, h, Lq, dk = q.shape
            dv = v.shape[-1]
            c = CHUNK
            n = Lq // c
            q = _l2norm(q)
            k = _l2norm(k)
            v = v * beta[..., None]
            kb = k * beta[..., None]
            rs = lambda t: t.reshape(b, h, n, c, t.shape[-1])
            q, k, v, kb = map(rs, (q, k, v, kb))
            tri_lo_strict = jnp.tril(jnp.ones((c, c), bool), -1)
            tri_lo = jnp.tril(jnp.ones((c, c), bool), 0)
            A = jnp.where(tri_lo_strict, kb @ jnp.swapaxes(k, -1, -2), 0.0)
            eye = jnp.eye(c, dtype=q.dtype)
            inv = jax.scipy.linalg.solve_triangular(eye + A, jnp.broadcast_to(eye, A.shape), lower=True, unit_diagonal=True)
            u = inv @ v
            w = inv @ kb

            def step(S, xs):
                qi, ki, ui, wi = xs
                attn = jnp.where(tri_lo, qi @ jnp.swapaxes(ki, -1, -2), 0.0)
                u_i = ui - wi @ S
                o = qi @ S + attn @ u_i
                return (S + jnp.swapaxes(ki, -1, -2) @ u_i, o)
            mv = lambda t: jnp.moveaxis(t, 2, 0)
            S0 = jnp.zeros((b, h, dk, dv), q.dtype)
            _, out = jax.lax.scan(step, S0, (mv(q), mv(k), mv(u), mv(w)))
            return jnp.moveaxis(out, 0, 2).reshape(b, h, Lq, dv)

        def _stats(x):
            mean = jnp.mean(x, -1, keepdims=True)
            var = jnp.var(x, -1, keepdims=True)
            am = jnp.mean(jnp.abs(x), -1, keepdims=True)
            l2 = jnp.linalg.norm(x, axis=-1, keepdims=True)
            return jnp.concatenate([mean, var, am, l2], -1)
        key = jax.random.key(seed)
        ks = jax.random.split(key, 20)
        rn = lambda i, shape, sc: jax.random.normal(ks[i], shape, jnp.float32) * sc
        fir_s = jnp.zeros((H, DV, FIR_S), jnp.float32).at[..., 0].set(1.0) + rn(8, (H, DV, FIR_S), 0.02)
        fir_l = jnp.zeros((H, DV, FIR_L), jnp.float32).at[..., 0].set(1.0) + rn(9, (H, DV, FIR_L), 0.02)
        return {'hidden_states': rn(0, (B, L, D), 1.0), 'Wq': rn(1, (D, D), 0.02), 'Wk': rn(2, (D, D), 0.02), 'Wv': rn(3, (D, D), 0.02), 'Wb': rn(4, (D, H), 0.02), 'conv_w_q': rn(5, (D, CONV_K), 0.3), 'conv_w_k': rn(6, (D, CONV_K), 0.3), 'conv_w_v': rn(7, (D, CONV_K), 0.3), 'fir_short_w': fir_s, 'fir_long_w': fir_l, 'mlp_w1': rn(10, (D + 16, GATE_HID), 0.02), 'mlp_b1': jnp.zeros((GATE_HID,), jnp.float32), 'mlp_w2': rn(11, (GATE_HID, 4), 0.02), 'mlp_b2': jnp.asarray(GATE_BIAS), 'logit_temp': jnp.full((1,), GATE_LOGIT_INIT, jnp.float32), 'conv_res_logit': jnp.full((H,), CONV_RES_INIT, jnp.float32), 'rms_w': jnp.ones((DV,), jnp.float32), 'Wo': rn(12, (D, D), 0.02)}
    _L0_attn_in = _L0_attn_setup()

    def _L0_ffn_setup():
        import jax, jax.numpy as jnp
        import numpy as np
        DIM = 128

        def _reference_tuple_inner(x, W_r, W_k, W_v, mu_r, mu_k):
            B, T, C = x.shape
            x_prev = jnp.concatenate([jnp.zeros((B, 1, C), x.dtype), x[:, :-1, :]], axis=1)
            xr = mu_r * x + (1.0 - mu_r) * x_prev
            xk = mu_k * x + (1.0 - mu_k) * x_prev
            r = jax.nn.sigmoid(jnp.einsum('btc,dc->btd', xr, W_r))
            k = jnp.einsum('btc,dc->btd', xk, W_k)
            k_act = jnp.square(jax.nn.relu(k))
            out = r * jnp.einsum('btc,dc->btd', k_act, W_v)
            new_state = x[:, -1, :]
            return (out, new_state)
        key = jax.random.key(seed)
        ks = jax.random.split(key, 6)
        B, T, C = (8, 256, DIM)
        x = jax.random.normal(ks[0], (B, T, C), dtype=jnp.float32)
        s = 1.0 / np.sqrt(C)
        W_r = jax.random.uniform(ks[1], (C, C), jnp.float32, -s, s)
        W_k = jax.random.uniform(ks[2], (C, C), jnp.float32, -s, s)
        W_v = jax.random.uniform(ks[3], (C, C), jnp.float32, -s, s)
        mu_r = jax.random.uniform(ks[4], (C,), jnp.float32)
        mu_k = jax.random.uniform(ks[5], (C,), jnp.float32)
        return {'x': x, 'W_r': W_r, 'W_k': W_k, 'W_v': W_v, 'mu_r': mu_r, 'mu_k': mu_k}
    _L0_ffn_in = _L0_ffn_setup()

    def _L1_attn_setup():
        import jax, jax.numpy as jnp
        from jax import lax
        import numpy as np

        def _causal_dwconv(x, w, b):
            k = w.shape[-1]
            y = lax.conv_general_dilated(x, w, (1,), [(k - 1, 0)], feature_group_count=w.shape[0], dimension_numbers=('NCH', 'OIH', 'NCH'))
            return y + b[None, :, None]

        def _mamba_branch(xz, conv_w, conv_b, xproj_w, dtproj_w, dt_bias, A_log, Dp):
            x, z = jnp.split(xz, 2, axis=1)
            x = jax.nn.silu(_causal_dwconv(x, conv_w, conv_b))
            r = dtproj_w.shape[1]
            n = A_log.shape[1]
            x_dbl = jnp.einsum('bdl,ed->bel', x, xproj_w)
            dt, Bm, Cm = (x_dbl[:, :r], x_dbl[:, r:r + n], x_dbl[:, r + n:])
            delta = jax.nn.softplus(jnp.einsum('brl,dr->bdl', dt, dtproj_w) + dt_bias[None, :, None])
            A = -jnp.exp(A_log)
            dA = jnp.exp(jnp.einsum('bdl,dn->lbdn', delta, A))
            dBu = jnp.einsum('bdl,bnl,bdl->lbdn', delta, Bm, x)

            def step(h, ab):
                h = ab[0] * h + ab[1]
                return (h, h)
            _, hs = lax.scan(step, jnp.zeros_like(dA[0]), (dA, dBu))
            y = jnp.einsum('lbdn,bnl->bdl', hs, Cm) + Dp[None, :, None] * x
            return y * jax.nn.silu(z)
        key = jax.random.key(seed)
        ks = jax.random.split(key, 20)
        B, L, DM = (2, 128, 128)
        DI, DS, DR, K = (256, 16, 64, 4)
        f = lambda i, shape, s=1.0: jax.random.normal(ks[i], shape, jnp.float32) * s
        return {'hidden_states': f(0, (B, L, DM)), 'in_proj_w': f(1, (2 * DI, DM), 0.02), 'conv1d_w': f(2, (DI, 1, K), 0.2), 'conv1d_bias': f(3, (DI,), 0.1), 'x_proj_w': f(4, (DR + 2 * DS, DI), 0.02), 'dt_proj_w': f(5, (DI, DR), 0.05), 'dt_proj_b': f(6, (DI,), 0.1), 'A_log': f(7, (DI, DS), 0.5), 'D': f(8, (DI,), 1.0), 'conv1db_w': f(9, (DI, 1, K), 0.2), 'conv1db_bias': f(10, (DI,), 0.1), 'x_projb_w': f(11, (DR + 2 * DS, DI), 0.02), 'dt_projb_w': f(12, (DI, DR), 0.05), 'dt_projb_b': f(13, (DI,), 0.1), 'A_b_log': f(14, (DI, DS), 0.5), 'D_b': f(15, (DI,), 1.0), 'out_proj_w': f(16, (DM, DI), 0.02), 'fft_conv_w': f(17, (2 * DI, 2 * DI, 5), 0.01), 'fft_conv_b': f(18, (2 * DI,), 0.1)}
    _L1_attn_in = _L1_attn_setup()

    def _L1_ffn_setup():
        import jax, jax.numpy as jnp
        import numpy as np
        B, N, D = (4, 512, 128)
        E, K, H, ITERS = (8, 2, 64, 2)
        DT = 0.1
        C = 2 * D

        def _gelu(x):
            return jax.nn.gelu(x, approximate=False)

        def _inl(ctrl, xs, vs, mu):
            a, b, g = jnp.split(ctrl, 3, axis=-1)
            v_next = jax.nn.sigmoid(a) * vs - jax.nn.softplus(b) * (xs - mu)
            x_next = xs + DT * jax.nn.sigmoid(g) * v_next
            return (x_next, v_next)

        def _experts(ctx, idx, w1, b1, w2, b2):
            out = jnp.zeros((ctx.shape[0], w2.shape[2]), ctx.dtype)
            for e in range(E):
                h = _gelu(ctx @ w1[e] + b1[e])
                o = h @ w2[e] + b2[e]
                out = out + jnp.where((idx == e)[:, None], o, jnp.float32(0))
            return out

        def _forward(x, integration_weight, mu, router_w1, router_b1, router_w2, router_b2, halt_w1, halt_b1, halt_w2, halt_b2, expert_w1, expert_b1, expert_w2, expert_b2, shared_w1, shared_b1, shared_w2, shared_b2, shared_weight, refine_w1, refine_b1, refine_w2, refine_b2):
            b, n, d = x.shape
            xf = x.reshape(b * n, d)
            logits = _gelu(xf @ router_w1 + router_b1) @ router_w2 + router_b2
            probs = jax.nn.softmax(logits, axis=-1)
            topk_p, topk_i = jax.lax.top_k(probs, K)
            topk_p = topk_p / jnp.sum(topk_p, axis=-1, keepdims=True)
            flat_idx = topk_i.reshape(-1)
            flat_w = topk_p.reshape(-1, 1)
            v = jnp.zeros_like(xf)
            integrated = xf
            for _ in range(ITERS):
                ctx = jnp.concatenate([integrated, v], axis=-1)
                shared_ctrl = _gelu(ctx @ shared_w1 + shared_b1) @ shared_w2 + shared_b2
                x_sh, v_sh = _inl(shared_ctrl, integrated, v, mu)
                sw = jax.nn.sigmoid(shared_weight)
                ctx_e = jnp.repeat(ctx, K, axis=0)
                x_e = jnp.repeat(integrated, K, axis=0)
                v_e = jnp.repeat(v, K, axis=0)
                ctrl = _experts(ctx_e, flat_idx, expert_w1, expert_b1, expert_w2, expert_b2)
                x_r, v_r = _inl(ctrl, x_e, v_e, mu)
                x_r = (x_r * flat_w).reshape(-1, K, d).sum(axis=1)
                v_r = (v_r * flat_w).reshape(-1, K, d).sum(axis=1)
                x_next = sw * x_sh + (1.0 - sw) * x_r
                v_next = sw * v_sh + (1.0 - sw) * v_r
                halt = jax.nn.sigmoid(_gelu(integrated @ halt_w1 + halt_b1) @ halt_w2 + halt_b2)
                integrated = integrated + halt * (x_next - integrated)
                v = v + halt * (v_next - v)
            refined = _gelu(integrated @ refine_w1 + refine_b1) @ refine_w2 + refine_b2
            out = xf + integration_weight * refined
            return out.reshape(b, n, d)
        key = jax.random.key(seed)
        ks = jax.random.split(key, 12)
        rn = lambda k, s, sc=0.02: jax.random.normal(k, s, dtype=jnp.float32) * sc
        z = lambda s: jnp.zeros(s, jnp.float32)
        return {'x': jax.random.normal(ks[0], (B, N, D), dtype=jnp.float32), 'integration_weight': jnp.full((D,), 0.5, jnp.float32), 'mu': z((D,)), 'router_w1': rn(ks[1], (D, D // 4)), 'router_b1': z((D // 4,)), 'router_w2': rn(ks[2], (D // 4, E)), 'router_b2': z((E,)), 'halt_w1': rn(ks[3], (D, D // 4)), 'halt_b1': z((D // 4,)), 'halt_w2': rn(ks[4], (D // 4, 1)), 'halt_b2': z((1,)), 'expert_w1': rn(ks[5], (E, C, H)), 'expert_b1': z((E, H)), 'expert_w2': rn(ks[6], (E, H, 3 * D)), 'expert_b2': z((E, 3 * D)), 'shared_w1': rn(ks[7], (C, H)), 'shared_b1': z((H,)), 'shared_w2': rn(ks[8], (H, 3 * D)), 'shared_b2': z((3 * D,)), 'shared_weight': jnp.float32(0.5), 'refine_w1': rn(ks[9], (D, 2 * D)), 'refine_b1': z((2 * D,)), 'refine_w2': rn(ks[10], (2 * D, D)), 'refine_b2': z((D,))}
    _L1_ffn_in = _L1_ffn_setup()
    _d = {'L0_attn_hidden_states': _L0_attn_in['hidden_states'], 'L0_attn_Wq': _L0_attn_in['Wq'], 'L0_attn_Wk': _L0_attn_in['Wk'], 'L0_attn_Wv': _L0_attn_in['Wv'], 'L0_attn_Wb': _L0_attn_in['Wb'], 'L0_attn_conv_w_q': _L0_attn_in['conv_w_q'], 'L0_attn_conv_w_k': _L0_attn_in['conv_w_k'], 'L0_attn_conv_w_v': _L0_attn_in['conv_w_v'], 'L0_attn_fir_short_w': _L0_attn_in['fir_short_w'], 'L0_attn_fir_long_w': _L0_attn_in['fir_long_w'], 'L0_attn_mlp_w1': _L0_attn_in['mlp_w1'], 'L0_attn_mlp_b1': _L0_attn_in['mlp_b1'], 'L0_attn_mlp_w2': _L0_attn_in['mlp_w2'], 'L0_attn_mlp_b2': _L0_attn_in['mlp_b2'], 'L0_attn_logit_temp': _L0_attn_in['logit_temp'], 'L0_attn_conv_res_logit': _L0_attn_in['conv_res_logit'], 'L0_attn_rms_w': _L0_attn_in['rms_w'], 'L0_attn_Wo': _L0_attn_in['Wo'], 'L0_ffn_W_r': _L0_ffn_in['W_r'], 'L0_ffn_W_k': _L0_ffn_in['W_k'], 'L0_ffn_W_v': _L0_ffn_in['W_v'], 'L0_ffn_mu_r': _L0_ffn_in['mu_r'], 'L0_ffn_mu_k': _L0_ffn_in['mu_k'], 'L1_attn_in_proj_w': _L1_attn_in['in_proj_w'], 'L1_attn_conv1d_w': _L1_attn_in['conv1d_w'], 'L1_attn_conv1d_bias': _L1_attn_in['conv1d_bias'], 'L1_attn_x_proj_w': _L1_attn_in['x_proj_w'], 'L1_attn_dt_proj_w': _L1_attn_in['dt_proj_w'], 'L1_attn_dt_proj_b': _L1_attn_in['dt_proj_b'], 'L1_attn_A_log': _L1_attn_in['A_log'], 'L1_attn_D': _L1_attn_in['D'], 'L1_attn_conv1db_w': _L1_attn_in['conv1db_w'], 'L1_attn_conv1db_bias': _L1_attn_in['conv1db_bias'], 'L1_attn_x_projb_w': _L1_attn_in['x_projb_w'], 'L1_attn_dt_projb_w': _L1_attn_in['dt_projb_w'], 'L1_attn_dt_projb_b': _L1_attn_in['dt_projb_b'], 'L1_attn_A_b_log': _L1_attn_in['A_b_log'], 'L1_attn_D_b': _L1_attn_in['D_b'], 'L1_attn_out_proj_w': _L1_attn_in['out_proj_w'], 'L1_attn_fft_conv_w': _L1_attn_in['fft_conv_w'], 'L1_attn_fft_conv_b': _L1_attn_in['fft_conv_b'], 'L1_ffn_integration_weight': _L1_ffn_in['integration_weight'], 'L1_ffn_mu': _L1_ffn_in['mu'], 'L1_ffn_router_w1': _L1_ffn_in['router_w1'], 'L1_ffn_router_b1': _L1_ffn_in['router_b1'], 'L1_ffn_router_w2': _L1_ffn_in['router_w2'], 'L1_ffn_router_b2': _L1_ffn_in['router_b2'], 'L1_ffn_halt_w1': _L1_ffn_in['halt_w1'], 'L1_ffn_halt_b1': _L1_ffn_in['halt_b1'], 'L1_ffn_halt_w2': _L1_ffn_in['halt_w2'], 'L1_ffn_halt_b2': _L1_ffn_in['halt_b2'], 'L1_ffn_expert_w1': _L1_ffn_in['expert_w1'], 'L1_ffn_expert_b1': _L1_ffn_in['expert_b1'], 'L1_ffn_expert_w2': _L1_ffn_in['expert_w2'], 'L1_ffn_expert_b2': _L1_ffn_in['expert_b2'], 'L1_ffn_shared_w1': _L1_ffn_in['shared_w1'], 'L1_ffn_shared_b1': _L1_ffn_in['shared_b1'], 'L1_ffn_shared_w2': _L1_ffn_in['shared_w2'], 'L1_ffn_shared_b2': _L1_ffn_in['shared_b2'], 'L1_ffn_shared_weight': _L1_ffn_in['shared_weight'], 'L1_ffn_refine_w1': _L1_ffn_in['refine_w1'], 'L1_ffn_refine_b1': _L1_ffn_in['refine_b1'], 'L1_ffn_refine_w2': _L1_ffn_in['refine_w2'], 'L1_ffn_refine_b2': _L1_ffn_in['refine_b2']}
    _x0 = _d['L0_attn_hidden_states']
    _d['L0_attn_hidden_states'] = jax.random.normal(jax.random.fold_in(jax.random.key(seed), 1), (8, 512, 128), dtype=_x0.dtype)
    del _x0
    return _d

def reference(L0_attn_hidden_states, L0_attn_Wq, L0_attn_Wk, L0_attn_Wv, L0_attn_Wb, L0_attn_conv_w_q, L0_attn_conv_w_k, L0_attn_conv_w_v, L0_attn_fir_short_w, L0_attn_fir_long_w, L0_attn_mlp_w1, L0_attn_mlp_b1, L0_attn_mlp_w2, L0_attn_mlp_b2, L0_attn_logit_temp, L0_attn_conv_res_logit, L0_attn_rms_w, L0_attn_Wo, L0_ffn_W_r, L0_ffn_W_k, L0_ffn_W_v, L0_ffn_mu_r, L0_ffn_mu_k, L1_attn_in_proj_w, L1_attn_conv1d_w, L1_attn_conv1d_bias, L1_attn_x_proj_w, L1_attn_dt_proj_w, L1_attn_dt_proj_b, L1_attn_A_log, L1_attn_D, L1_attn_conv1db_w, L1_attn_conv1db_bias, L1_attn_x_projb_w, L1_attn_dt_projb_w, L1_attn_dt_projb_b, L1_attn_A_b_log, L1_attn_D_b, L1_attn_out_proj_w, L1_attn_fft_conv_w, L1_attn_fft_conv_b, L1_ffn_integration_weight, L1_ffn_mu, L1_ffn_router_w1, L1_ffn_router_b1, L1_ffn_router_w2, L1_ffn_router_b2, L1_ffn_halt_w1, L1_ffn_halt_b1, L1_ffn_halt_w2, L1_ffn_halt_b2, L1_ffn_expert_w1, L1_ffn_expert_b1, L1_ffn_expert_w2, L1_ffn_expert_b2, L1_ffn_shared_w1, L1_ffn_shared_b1, L1_ffn_shared_w2, L1_ffn_shared_b2, L1_ffn_shared_weight, L1_ffn_refine_w1, L1_ffn_refine_b1, L1_ffn_refine_w2, L1_ffn_refine_b2):

    def _L0_attn_ref(hidden_states, Wq, Wk, Wv, Wb, conv_w_q, conv_w_k, conv_w_v, fir_short_w, fir_long_w, mlp_w1, mlp_b1, mlp_w2, mlp_b2, logit_temp, conv_res_logit, rms_w, Wo):
        import jax, jax.numpy as jnp
        import numpy as np
        B, L, D, H = (2, 512, 128, 4)
        DK = D // H
        DV = D // H
        CONV_K = 4
        FIR_S, FIR_L = (5, 64)
        GATE_HID = D * 2 // 2
        CHUNK = 32
        FLOOR_EPS = 0.08
        GATE_BIAS = np.array([-0.5, -0.5, 1.0, 3.0], np.float32)
        GATE_LOGIT_INIT = float(np.log(np.expm1(0.7)))
        CONV_RES_INIT = float(np.log(0.1 / 0.9))

        def _l2norm(x):
            return x / jnp.sqrt(jnp.sum(x * x, -1, keepdims=True) + 1e-12)

        def _causal_dwconv(x, w):
            k = w.shape[-1]
            xp = jnp.pad(x, ((0, 0), (k - 1, 0), (0, 0))).transpose(0, 2, 1)
            y = jax.lax.conv_general_dilated(xp, w[:, None, :], (1,), 'VALID', feature_group_count=w.shape[0], dimension_numbers=('NCH', 'OIH', 'NCH'))
            return y.transpose(0, 2, 1)

        def _delta_chunkwise(q, k, v, beta):
            b, h, Lq, dk = q.shape
            dv = v.shape[-1]
            c = CHUNK
            n = Lq // c
            q = _l2norm(q)
            k = _l2norm(k)
            v = v * beta[..., None]
            kb = k * beta[..., None]
            rs = lambda t: t.reshape(b, h, n, c, t.shape[-1])
            q, k, v, kb = map(rs, (q, k, v, kb))
            tri_lo_strict = jnp.tril(jnp.ones((c, c), bool), -1)
            tri_lo = jnp.tril(jnp.ones((c, c), bool), 0)
            A = jnp.where(tri_lo_strict, kb @ jnp.swapaxes(k, -1, -2), 0.0)
            eye = jnp.eye(c, dtype=q.dtype)
            inv = jax.scipy.linalg.solve_triangular(eye + A, jnp.broadcast_to(eye, A.shape), lower=True, unit_diagonal=True)
            u = inv @ v
            w = inv @ kb

            def step(S, xs):
                qi, ki, ui, wi = xs
                attn = jnp.where(tri_lo, qi @ jnp.swapaxes(ki, -1, -2), 0.0)
                u_i = ui - wi @ S
                o = qi @ S + attn @ u_i
                return (S + jnp.swapaxes(ki, -1, -2) @ u_i, o)
            mv = lambda t: jnp.moveaxis(t, 2, 0)
            S0 = jnp.zeros((b, h, dk, dv), q.dtype)
            _, out = jax.lax.scan(step, S0, (mv(q), mv(k), mv(u), mv(w)))
            return jnp.moveaxis(out, 0, 2).reshape(b, h, Lq, dv)

        def _stats(x):
            mean = jnp.mean(x, -1, keepdims=True)
            var = jnp.var(x, -1, keepdims=True)
            am = jnp.mean(jnp.abs(x), -1, keepdims=True)
            l2 = jnp.linalg.norm(x, axis=-1, keepdims=True)
            return jnp.concatenate([mean, var, am, l2], -1)
        hs = hidden_states
        b, l, _ = hs.shape
        silu = jax.nn.silu
        q = silu(_causal_dwconv(hs @ Wq, conv_w_q))
        k = silu(_causal_dwconv(hs @ Wk, conv_w_k))
        v = silu(_causal_dwconv(hs @ Wv, conv_w_v))
        qh = q.reshape(b, l, H, DK)
        kh = k.reshape(b, l, H, DK)
        vh = v.reshape(b, l, H, DV)
        beta = jax.nn.sigmoid(hs @ Wb)
        tr = lambda t: jnp.transpose(t, (0, 2, 1, 3))
        delta_out = tr(_delta_chunkwise(tr(qh), tr(kh), tr(vh), jnp.transpose(beta, (0, 2, 1))))
        fir = lambda x, w: _causal_dwconv(x.reshape(b, l, H * DV), w.reshape(H * DV, -1)).reshape(b, l, H, DV)
        local_short = fir(vh, fir_short_w)
        local_long = fir(vh, fir_long_w)
        stats = jnp.concatenate([_stats(local_short), _stats(local_long), _stats(delta_out), _stats(vh)], -1)
        hs_exp = jnp.broadcast_to(hs[:, :, None, :], (b, l, H, hs.shape[-1]))
        gate_in = jnp.concatenate([hs_exp, stats], -1)
        hgate = jax.nn.gelu(gate_in @ mlp_w1 + mlp_b1, approximate=False)
        logits = hgate @ mlp_w2 + mlp_b2
        temp = jax.nn.softplus(logit_temp) + 1e-06
        probs = jax.nn.softmax(logits / temp, -1)
        floor = jnp.array([FLOOR_EPS, FLOOR_EPS, 0.0, 0.0], probs.dtype)
        probs = probs * (1.0 - 2.0 * FLOOR_EPS) + floor
        o = probs[..., 0:1] * local_short + probs[..., 1:2] * local_long + probs[..., 2:3] * delta_out + probs[..., 3:4] * vh
        o = o + jax.nn.sigmoid(conv_res_logit)[None, None, :, None] * local_short
        o = o * jax.lax.rsqrt(jnp.mean(o * o, -1, keepdims=True) + 1e-05) * rms_w
        return o.reshape(b, l, H * DV) @ Wo

    def _L0_ffn_ref(x, W_r, W_k, W_v, mu_r, mu_k):
        import jax, jax.numpy as jnp
        import numpy as np
        DIM = 128

        def _reference_tuple_inner(x, W_r, W_k, W_v, mu_r, mu_k):
            B, T, C = x.shape
            x_prev = jnp.concatenate([jnp.zeros((B, 1, C), x.dtype), x[:, :-1, :]], axis=1)
            xr = mu_r * x + (1.0 - mu_r) * x_prev
            xk = mu_k * x + (1.0 - mu_k) * x_prev
            r = jax.nn.sigmoid(jnp.einsum('btc,dc->btd', xr, W_r))
            k = jnp.einsum('btc,dc->btd', xk, W_k)
            k_act = jnp.square(jax.nn.relu(k))
            out = r * jnp.einsum('btc,dc->btd', k_act, W_v)
            new_state = x[:, -1, :]
            return (out, new_state)
        return _reference_tuple_inner(x, W_r, W_k, W_v, mu_r, mu_k)[0]

    def _L1_attn_ref(hidden_states, in_proj_w, conv1d_w, conv1d_bias, x_proj_w, dt_proj_w, dt_proj_b, A_log, D, conv1db_w, conv1db_bias, x_projb_w, dt_projb_w, dt_projb_b, A_b_log, D_b, out_proj_w, fft_conv_w, fft_conv_b):
        import jax, jax.numpy as jnp
        from jax import lax
        import numpy as np

        def _causal_dwconv(x, w, b):
            k = w.shape[-1]
            y = lax.conv_general_dilated(x, w, (1,), [(k - 1, 0)], feature_group_count=w.shape[0], dimension_numbers=('NCH', 'OIH', 'NCH'))
            return y + b[None, :, None]

        def _mamba_branch(xz, conv_w, conv_b, xproj_w, dtproj_w, dt_bias, A_log, Dp):
            x, z = jnp.split(xz, 2, axis=1)
            x = jax.nn.silu(_causal_dwconv(x, conv_w, conv_b))
            r = dtproj_w.shape[1]
            n = A_log.shape[1]
            x_dbl = jnp.einsum('bdl,ed->bel', x, xproj_w)
            dt, Bm, Cm = (x_dbl[:, :r], x_dbl[:, r:r + n], x_dbl[:, r + n:])
            delta = jax.nn.softplus(jnp.einsum('brl,dr->bdl', dt, dtproj_w) + dt_bias[None, :, None])
            A = -jnp.exp(A_log)
            dA = jnp.exp(jnp.einsum('bdl,dn->lbdn', delta, A))
            dBu = jnp.einsum('bdl,bnl,bdl->lbdn', delta, Bm, x)

            def step(h, ab):
                h = ab[0] * h + ab[1]
                return (h, h)
            _, hs = lax.scan(step, jnp.zeros_like(dA[0]), (dA, dBu))
            y = jnp.einsum('lbdn,bnl->bdl', hs, Cm) + Dp[None, :, None] * x
            return y * jax.nn.silu(z)
        xz = jnp.einsum('bld,ed->bel', hidden_states, in_proj_w)
        out = _mamba_branch(xz, conv1d_w, conv1d_bias, x_proj_w, dt_proj_w, dt_proj_b, A_log, D)
        out_b = _mamba_branch(xz[:, :, ::-1], conv1db_w, conv1db_bias, x_projb_w, dt_projb_w, dt_projb_b, A_b_log, D_b)
        x, z = jnp.split(xz, 2, axis=1)
        xf = jnp.fft.fftn(x, axes=(-2, -1))
        xc = jnp.concatenate([xf.real, xf.imag], axis=1)
        xc = lax.conv_general_dilated(xc, fft_conv_w, (1,), [(2, 2)], dimension_numbers=('NCH', 'OIH', 'NCH'))
        xc = jax.nn.silu(xc + fft_conv_b[None, :, None])
        re, im = jnp.split(xc, 2, axis=1)
        x_out = jnp.fft.ifftn(lax.complex(re, im), axes=(-2, -1))
        z_out = jnp.max(jax.nn.silu(z), axis=-1, keepdims=True)
        v = jnp.abs(x_out * z_out)
        mu = jnp.mean(v, axis=-1, keepdims=True)
        var = jnp.var(v, axis=-1, keepdims=True)
        out_f = (v - mu) / jnp.sqrt(var + 1e-05)
        y = out + out_b[:, :, ::-1] + out_f
        return jnp.einsum('bdl,od->blo', y, out_proj_w)

    def _L1_ffn_ref(x, integration_weight, mu, router_w1, router_b1, router_w2, router_b2, halt_w1, halt_b1, halt_w2, halt_b2, expert_w1, expert_b1, expert_w2, expert_b2, shared_w1, shared_b1, shared_w2, shared_b2, shared_weight, refine_w1, refine_b1, refine_w2, refine_b2):
        import jax, jax.numpy as jnp
        import numpy as np
        B, N, D = (4, 512, 128)
        E, K, H, ITERS = (8, 2, 64, 2)
        DT = 0.1
        C = 2 * D

        def _gelu(x):
            return jax.nn.gelu(x, approximate=False)

        def _inl(ctrl, xs, vs, mu):
            a, b, g = jnp.split(ctrl, 3, axis=-1)
            v_next = jax.nn.sigmoid(a) * vs - jax.nn.softplus(b) * (xs - mu)
            x_next = xs + DT * jax.nn.sigmoid(g) * v_next
            return (x_next, v_next)

        def _experts(ctx, idx, w1, b1, w2, b2):
            out = jnp.zeros((ctx.shape[0], w2.shape[2]), ctx.dtype)
            for e in range(E):
                h = _gelu(ctx @ w1[e] + b1[e])
                o = h @ w2[e] + b2[e]
                out = out + jnp.where((idx == e)[:, None], o, jnp.float32(0))
            return out

        def _forward(x, integration_weight, mu, router_w1, router_b1, router_w2, router_b2, halt_w1, halt_b1, halt_w2, halt_b2, expert_w1, expert_b1, expert_w2, expert_b2, shared_w1, shared_b1, shared_w2, shared_b2, shared_weight, refine_w1, refine_b1, refine_w2, refine_b2):
            b, n, d = x.shape
            xf = x.reshape(b * n, d)
            logits = _gelu(xf @ router_w1 + router_b1) @ router_w2 + router_b2
            probs = jax.nn.softmax(logits, axis=-1)
            topk_p, topk_i = jax.lax.top_k(probs, K)
            topk_p = topk_p / jnp.sum(topk_p, axis=-1, keepdims=True)
            flat_idx = topk_i.reshape(-1)
            flat_w = topk_p.reshape(-1, 1)
            v = jnp.zeros_like(xf)
            integrated = xf
            for _ in range(ITERS):
                ctx = jnp.concatenate([integrated, v], axis=-1)
                shared_ctrl = _gelu(ctx @ shared_w1 + shared_b1) @ shared_w2 + shared_b2
                x_sh, v_sh = _inl(shared_ctrl, integrated, v, mu)
                sw = jax.nn.sigmoid(shared_weight)
                ctx_e = jnp.repeat(ctx, K, axis=0)
                x_e = jnp.repeat(integrated, K, axis=0)
                v_e = jnp.repeat(v, K, axis=0)
                ctrl = _experts(ctx_e, flat_idx, expert_w1, expert_b1, expert_w2, expert_b2)
                x_r, v_r = _inl(ctrl, x_e, v_e, mu)
                x_r = (x_r * flat_w).reshape(-1, K, d).sum(axis=1)
                v_r = (v_r * flat_w).reshape(-1, K, d).sum(axis=1)
                x_next = sw * x_sh + (1.0 - sw) * x_r
                v_next = sw * v_sh + (1.0 - sw) * v_r
                halt = jax.nn.sigmoid(_gelu(integrated @ halt_w1 + halt_b1) @ halt_w2 + halt_b2)
                integrated = integrated + halt * (x_next - integrated)
                v = v + halt * (v_next - v)
            refined = _gelu(integrated @ refine_w1 + refine_b1) @ refine_w2 + refine_b2
            out = xf + integration_weight * refined
            return out.reshape(b, n, d)
        return _forward(x, integration_weight, mu, router_w1, router_b1, router_w2, router_b2, halt_w1, halt_b1, halt_w2, halt_b2, expert_w1, expert_b1, expert_w2, expert_b2, shared_w1, shared_b1, shared_w2, shared_b2, shared_weight, refine_w1, refine_b1, refine_w2, refine_b2)
    x = L0_attn_hidden_states
    x = x + _L0_attn_ref(_layernorm(x, axis=-1), L0_attn_Wq, L0_attn_Wk, L0_attn_Wv, L0_attn_Wb, L0_attn_conv_w_q, L0_attn_conv_w_k, L0_attn_conv_w_v, L0_attn_fir_short_w, L0_attn_fir_long_w, L0_attn_mlp_w1, L0_attn_mlp_b1, L0_attn_mlp_w2, L0_attn_mlp_b2, L0_attn_logit_temp, L0_attn_conv_res_logit, L0_attn_rms_w, L0_attn_Wo)
    x = x + _L0_ffn_ref(_layernorm(x, axis=-1), L0_ffn_W_r, L0_ffn_W_k, L0_ffn_W_v, L0_ffn_mu_r, L0_ffn_mu_k)
    x = x + _L1_attn_ref(_layernorm(x, axis=-1), L1_attn_in_proj_w, L1_attn_conv1d_w, L1_attn_conv1d_bias, L1_attn_x_proj_w, L1_attn_dt_proj_w, L1_attn_dt_proj_b, L1_attn_A_log, L1_attn_D, L1_attn_conv1db_w, L1_attn_conv1db_bias, L1_attn_x_projb_w, L1_attn_dt_projb_w, L1_attn_dt_projb_b, L1_attn_A_b_log, L1_attn_D_b, L1_attn_out_proj_w, L1_attn_fft_conv_w, L1_attn_fft_conv_b)
    x = x + _L1_ffn_ref(_layernorm(x, axis=-1), L1_ffn_integration_weight, L1_ffn_mu, L1_ffn_router_w1, L1_ffn_router_b1, L1_ffn_router_w2, L1_ffn_router_b2, L1_ffn_halt_w1, L1_ffn_halt_b1, L1_ffn_halt_w2, L1_ffn_halt_b2, L1_ffn_expert_w1, L1_ffn_expert_b1, L1_ffn_expert_w2, L1_ffn_expert_b2, L1_ffn_shared_w1, L1_ffn_shared_b1, L1_ffn_shared_w2, L1_ffn_shared_b2, L1_ffn_shared_weight, L1_ffn_refine_w1, L1_ffn_refine_b1, L1_ffn_refine_w2, L1_ffn_refine_b2)
    return x

_drawn_inputs = setup_inputs


def setup_inputs(seed=0):
    import zlib

    import numpy as np

    out = dict(_drawn_inputs(seed))
    spreads = {'L0_attn_mlp_b1': (0.0, 0.8),
     'L0_attn_conv_res_logit': (-2.1972246170043945, 0.6),
     'L0_attn_rms_w': (1.0, 0.2),
     'L1_ffn_integration_weight': (0.5, 0.6),
     'L1_ffn_mu': (0.0, 0.8),
     'L1_ffn_router_b1': (0.0, 0.8),
     'L1_ffn_router_b2': (0.0, 0.8),
     'L1_ffn_halt_b1': (0.0, 0.8),
     'L1_ffn_expert_b1': (0.0, 0.8),
     'L1_ffn_expert_b2': (0.0, 0.8),
     'L1_ffn_shared_b1': (0.0, 0.8),
     'L1_ffn_shared_b2': (0.0, 0.8),
     'L1_ffn_refine_b1': (0.0, 0.8),
     'L1_ffn_refine_b2': (0.0, 0.302)}
    factors = {'L0_attn_Wq': 6.929,
     'L0_attn_Wk': 6.882,
     'L0_attn_Wb': 8.0,
     'L0_attn_conv_w_q': 7.011,
     'L0_attn_conv_w_k': 6.856,
     'L0_attn_mlp_w1': 8.0,
     'L0_attn_mlp_w2': 8.0,
     'L0_ffn_W_r': 2.945,
     'L0_ffn_mu_r': 5.794,
     'L1_attn_conv1d_w': 8.0,
     'L1_attn_conv1d_bias': 8.0,
     'L1_attn_x_proj_w': 8.0,
     'L1_attn_dt_proj_w': 8.0,
     'L1_attn_dt_proj_b': 8.0,
     'L1_attn_A_log': 8.0,
     'L1_attn_D': 8.0,
     'L1_attn_conv1db_w': 8.0,
     'L1_attn_conv1db_bias': 8.0,
     'L1_attn_x_projb_w': 8.0,
     'L1_attn_dt_projb_w': 8.0,
     'L1_attn_dt_projb_b': 8.0,
     'L1_attn_A_b_log': 8.0,
     'L1_attn_D_b': 8.0,
     'L1_attn_fft_conv_b': 8.0,
     'L1_ffn_router_w1': 8.0,
     'L1_ffn_router_w2': 8.0,
     'L1_ffn_halt_w1': 8.0,
     'L1_ffn_halt_w2': 8.0,
     'L1_ffn_expert_w1': 8.0,
     'L1_ffn_expert_w2': 8.0,
     'L1_ffn_shared_w1': 8.0,
     'L1_ffn_shared_w2': 8.0,
     'L1_ffn_refine_w1': 6.233,
     'L1_ffn_refine_w2': 5.675}
    for name, (base, spread) in spreads.items():
        noise = np.random.default_rng([zlib.crc32(name.encode()), seed]).standard_normal(out[name].shape)
        drawn = base * np.exp(spread * noise) if base else spread * noise
        out[name] = jnp.asarray(drawn.astype(out[name].dtype))
    for name, factor in factors.items():
        out[name] = (out[name] * factor).astype(out[name].dtype)
    return out
```

```python
import concourse.bass as bass
from concourse import mybir
from contextlib import ExitStack
import numpy as np

F32 = mybir.dt.float32
BF16 = mybir.dt.bfloat16
ALU = mybir.AluOpType
ACT = mybir.ActivationFunctionType
AXX = mybir.AxisListType.X

B, L, D = 8, 512, 128
H, DK, CH = 4, 32, 32
NCH = L // CH
FIR_S, FIR_L = 5, 64
FIR_PE = 16
NS = 16
NT = L // 128
TAPS = 5
NE, HE = 8, 64
PAD = 4
SP_CAP = 40.0


def shape_tables():
    p = np.arange(128)
    blk = (p[:, None] // 32 == p[None, :] // 32).astype(np.float32)
    i, j = p[:, None] % 32, np.arange(32)[None, :]
    t = {"ident": np.eye(128), "ones_mean": np.full((128, 128), 1 / 128), "head_ones": blk, "head_mean": blk / 32,
         "neg_blk": -blk, "ident_st": (i == j)}
    for s in (1, 2, 4, 8, 16):
        off = ((i // (2 * s) == j // (2 * s)) & (i // s % 2 == 1) & (j // s % 2 == 0)).astype(np.float32)
        t["neg_level1" if s == 1 else f"level{s}"] = -off if s == 1 else off
    t["causal_bd"] = (blk.reshape(128, 4, 32) * (i <= j)[:, None, :]).reshape(128, 128)
    sel = np.zeros((128, 4, 16))
    for s in range(4):
        for h in range(4):
            sel[32 * h:32 * h + 32, s, 4 * s + h] = 1 / 32
    t["stat_sel"] = sel.reshape(128, 64)
    prob = np.zeros((128, 4, 128))
    for h in range(4):
        for k in range(4):
            prob[4 * h + k, k, 32 * h:32 * h + 32] = 1
    t["prob_sel"] = prob.reshape(128, 512)
    t["floor"] = np.tile(np.array([0.08, 0.08, 0, 0]), (128, 4))
    t["dec"] = np.tile(np.arange(8, 0, -1.0), (128, 1))
    wsel = np.zeros((128, 2, 128))
    wsel[16, 0], wsel[17, 1] = 1, 1
    t["wsel"] = wsel.reshape(128, 256)
    return {k: np.asarray(v, np.float32).reshape(128, -1) for k, v in t.items()}


def selector_tables():
    s = np.zeros((128, 32, 128), np.float32)
    for n in range(32):
        s[[n, 32 + n, 64 + n], n] = 1
    m = np.zeros((128, 2, 4, 128), np.float32)
    for r in range(2):
        for t in range(4):
            for e in range(2):
                m[8 * r + 2 * t + e, r, t, 64 * e:64 * e + 64] = 1
    return np.concatenate([s.reshape(128, -1), m.reshape(128, -1)], 1)


def dft_tables():
    k = np.arange(L)
    a = 2 * np.pi * ((k[:, None] * k[None]) % L) / L
    time = np.stack([np.cos(a), np.sin(a)]).reshape(2, NT, 128, L).transpose(2, 0, 1, 3)
    k = np.arange(256)
    a = 2 * np.pi * ((k[:, None] * k[None]) % 256) / 256
    c, s = np.cos(a), np.sin(a)
    fwd = np.block([[c, s], [-s, c]])
    inv = np.block([[c, s], [-s, c]]) / (256 * L)
    lay = lambda m: m.reshape(4, 128, 512).transpose(1, 0, 2)
    return (np.ascontiguousarray(time.reshape(128, -1), np.float32),
            np.ascontiguousarray(lay(fwd).reshape(128, -1), np.float32),
            np.ascontiguousarray(lay(inv).reshape(128, -1), np.float32))


WEIGHTS = [
    ("Wb", 128), ("fir_s", 5), ("fir_l", 64),
    ("W1x", 128), ("W1s", 512), ("b1", 1), ("W2", 4), ("b2", 4), ("temp", 1), ("res", 4), ("rms", 1), ("Wo", 128),
    ("Wvf", 128), ("mur", 1), ("muk", 1),
    ("inp", 512), ("mconv", 16), ("mconvb", 4), ("xproj", 512), ("dtproj", 512), ("dtb", 4), ("Alog", 64), ("Dp", 4),
    ("outp", 256), ("fftb", 4),
    ("iw", 1), ("mu", 1), ("m1", 256), ("m1b", 1), ("rw2", 8), ("rb2", 8), ("hw2", 128), ("hb2", 1),
    ("e1", 1024), ("e1b", 4), ("e2", 1536), ("e2b", 768), ("s2", 384), ("s2b", 3), ("sw", 1),
    ("r1", 256), ("r1b", 2), ("r2", 256), ("r2b", 1),
]
WAT, _n = {}, 0
for _name, _c in WEIGHTS:
    WAT[_name] = (_n, _c)
    _n += _c
WCOLS = _n
TAT, _n = {}, 0
for _name, _v in shape_tables().items():
    TAT[_name] = (_n, _v.shape[1])
    _n += _v.shape[1]
TCOLS = _n


class Sems(dict):

    def __init__(self, nc, stack, stage):
        self.nc, self.stack, self.stage = nc, stack, stage

    def __missing__(self, name):
        self[name] = self.stack.enter_context(self.nc.semaphore(f"{self.stage}_{name}"))
        return self[name]


def linker(eng, sem):
    n = [0]

    def link(ins):
        n[0] += 1
        ins.then_inc(sem, 1)
        eng.wait_ge(sem, n[0])
    return link


class Mem:

    def __init__(self, nc, ctx):
        sb = lambda n, s, d=F32: ctx.enter_context(nc.sbuf_tensor(n, s, d))
        self.w = sb("weights", [128, WCOLS])
        self.t = sb("tables", [128, TCOLS])
        self.sel = sb("selectors", [128, 40, 128], BF16)
        self.dft = sb("dft_time", [128, 2, NT, L])
        self.inv = sb("dft_chan_inv", [128, 4, 512])
        self.fw = sb("freq_conv_w", [128, TAPS, 4, 512])
        self.qkvw = sb("qkv_tap_w", [128, 3, 4, 128])
        self.firw = sb("fir_diag", [128, FIR_S + FIR_PE, 128])
        self.mixw = sb("token_mix_w", [128, 4, 128])
        self.small = sb("small", [128, 128])
        self.x = sb("x", [128, L])
        self.hp = sb("h_padded", [128, PAD + L])
        self.work = sb("work", [128, 39, L])
        self.ps = [ctx.enter_context(nc.psum_tensor(f"ps{i}", [128, 512], F32)) for i in range(8)]

    def W(self, name):
        a, n = WAT[name]
        return self.w[:, a:a + n]

    def T(self, name):
        a, n = TAT[name]
        return self.t[:, a:a + n]

    def s(self, i):
        return self.work[:, i, :]

    @property
    def h(self):
        return self.hp[:, PAD:PAD + L]


SM = {"temp": 0, "res": 1, "pconst": 5, "sw": 21, "omsw": 22, "A": 23, "one_mu_r": 87, "one_mu_k": 88, "tmp": 89}


def run_block(nc, stage, programs):
    with ExitStack() as st:
        S = Sems(nc, st, stage)
        with nc.Block() as block:
            if "sync" in programs:
                block.sync(lambda eng: programs["sync"](eng, S))
            if "tensor" in programs:
                block.tensor(lambda eng: programs["tensor"](eng, S))
            if "vector" in programs:
                block.vector(lambda eng: programs["vector"](eng, S))
            if "scalar" in programs:
                block.scalar(lambda eng: programs["scalar"](eng, S))
            if "gpsimd" in programs:
                block.gpsimd(lambda eng: programs["gpsimd"](eng, S))
        nums = [s.num for s in S.values()]
        nc.gpsimd.sem_clear(range(min(nums), max(nums) + 1))
        nc.all_engine_barrier()


def ln_tensor(nc, pe, S, m, loaded=0):
    if loaded:
        pe.wait_ge(S["x_loaded"], loaded)
    nc.tensor.matmul(m.ps[0][:, :], m.T("ones_mean"), m.x[:, :], start=True, stop=True).then_inc(S["ln_mean"], 1)
    pe.wait_ge(S["ln_squared"], 1)
    nc.tensor.matmul(m.ps[1][:, :], m.T("ones_mean"), m.s(1), start=True, stop=True).then_inc(S["ln_var"], 1)


def ln_vector(nc, v, S, m):
    v.wait_ge(S["ln_mean"], 1)
    nc.vector.tensor_tensor(m.s(0), m.x[:, :], m.ps[0][:, :], ALU.subtract).then_inc(S["ln_centred"], 1)
    v.wait_ge(S["ln_centred"], 1)
    v.wait_ge(S["ln_rstd"], 1)
    nc.vector.tensor_tensor(m.h, m.s(0), m.s(2), ALU.mult).then_inc(S["h_ready"], 1)


def ln_scalar(nc, a, S, m):
    a.wait_ge(S["ln_centred"], 1)
    nc.scalar.activation(m.s(1), m.s(0), ACT.Square).then_inc(S["ln_squared"], 1)
    a.wait_ge(S["ln_var"], 1)
    nc.scalar.activation(m.s(2), m.ps[1][:, :], ACT.Ln, bias=m.small[:, 120:121]).then_inc(S["ln_log"], 1)
    a.wait_ge(S["ln_log"], 1)
    nc.scalar.activation(m.s(2), m.s(2), ACT.Exp, scale=-0.5).then_inc(S["ln_rstd"], 1)


def setup(nc, m, d):
    raw = m.work[:, 0:20, :].rearrange("p (t k) n -> p t k n", t=TAPS)
    fwd = m.work[:, 20:24, :]
    taps = m.work[:, 24:27, :]
    sel32 = m.work[:, 27:37, :]
    prep = m.work[:, 37:39, :].rearrange("p a n -> p (a n)")
    sm = m.small

    def sync(sp, S):
        sp.dma_start(m.w[:, :], d["w"]).then_inc(S["weights"], 16)
        sp.dma_start(m.t[:, :], d["tab"]).then_inc(S["weights"], 16)
        sp.dma_start(taps, d["taps"].rearrange("p (a n) -> p a n", a=3)).then_inc(S["weights"], 16)
        sp.dma_start(prep[:, 0:640], d["prep"]).then_inc(S["weights"], 16)
        sp.dma_start(sel32, d["sel"].rearrange("p (a n) -> p a n", a=10)).then_inc(S["selectors"], 16)
        sp.dma_start(fwd, d["fwd"].rearrange("p (a n) -> p a n", a=4)).then_inc(S["freq"], 16)
        sp.dma_start(raw, d["fw"].rearrange("p (t k n) -> p t k n", t=TAPS, k=4)).then_inc(S["freq"], 16)
        sp.dma_start(m.dft[:, :, :, :], d["time"].rearrange("p (a t n) -> p a t n", a=2, t=NT)).then_inc(S["dft"], 16)
        sp.dma_start(m.inv[:, :, :], d["inv"].rearrange("p (a n) -> p a n", a=4)).then_inc(S["dft"], 16)
        sp.wait_ge(S["dft"], 32)

    def tensor(pe, S):
        pe.wait_ge(S["freq"], 32)
        n = 0
        for t in range(TAPS):
            for yc in range(4):
                if n >= 4:
                    pe.wait_ge(S["folded_copied"], n - 3)
                for j in range(4):
                    last = nc.tensor.matmul(m.ps[n % 4][:, :], fwd[:, j, 128 * yc:128 * yc + 128], raw[:, t, j, :],
                                            start=(j == 0), stop=(j == 3))
                last.then_inc(S["folded"], 1)
                n += 1

    def vector(v, S):
        link = linker(v, S["chain"])
        link(nc.vector.memset(m.hp[:, 0:PAD], 0.0))
        link(nc.vector.memset(sm[:, 119:128], 0.0))
        link(nc.vector.memset(sm[:, 120:121], 1e-5))
        link(nc.vector.memset(sm[:, 121:122], 1e-12))
        link(nc.vector.memset(sm[:, 122:123], 1.0))
        v.wait_ge(S["weights"], 64)
        for p in range(3):
            for j in range(4):
                nc.vector.tensor_tensor(m.qkvw[:, p, j, :], prep[:, 128 * p:128 * p + 128], taps[:, p, 128 * j:128 * j + 128], ALU.mult)
        for k in range(FIR_S):
            nc.vector.tensor_scalar(m.firw[:, k, :], m.T("ident"), m.W("fir_s")[:, k:k + 1], None, ALU.mult)
        for k in range(FIR_PE):
            nc.vector.tensor_scalar(m.firw[:, FIR_S + k, :], m.T("ident"), m.W("fir_l")[:, k:k + 1], None, ALU.mult)
        for i, (w, mu, one_mu) in enumerate(((prep[:, 384:512], "mur", "one_mu_r"), (prep[:, 512:640], "muk", "one_mu_k"))):
            c = SM[one_mu]
            nc.vector.tensor_scalar(m.mixw[:, 2 * i, :], w, m.W(mu)[:, 0:1], None, ALU.mult)
            link(nc.vector.tensor_scalar(sm[:, c:c + 1], m.W(mu)[:, 0:1], -1.0, 1.0, ALU.mult, ALU.add))
            nc.vector.tensor_scalar(m.mixw[:, 2 * i + 1, :], w, sm[:, c:c + 1], None, ALU.mult)
        link(nc.vector.tensor_scalar(sm[:, 89:90], m.W("temp"), SP_CAP, None, ALU.min))
        nc.vector.tensor_scalar(sm[:, 90:91], m.W("temp"), 1.0, None, ALU.mult).then_inc(S["sp_in"], 1)
        v.wait_ge(S["exps"], 6)
        link(nc.vector.tensor_tensor(sm[:, 92:93], m.W("temp"), sm[:, 91:92], ALU.max))
        link(nc.vector.tensor_scalar(sm[:, 92:93], sm[:, 92:93], 1e-6, None, ALU.add))
        link(nc.vector.reciprocal(sm[:, 0:1], sm[:, 92:93]))
        link(nc.vector.tensor_scalar(sm[:, 93:98], sm[:, 93:98], 1.0, None, ALU.add))
        link(nc.vector.reciprocal(sm[:, 93:98], sm[:, 93:98]))
        link(nc.vector.tensor_copy(sm[:, 1:5], sm[:, 93:97]))
        link(nc.vector.tensor_copy(sm[:, 21:22], sm[:, 97:98]))
        link(nc.vector.tensor_scalar(sm[:, 22:23], sm[:, 21:22], -1.0, 1.0, ALU.mult, ALU.add))
        link(nc.vector.tensor_copy(sm[:, 5:21], m.T("floor")))
        pc = sm[:, 5:21].rearrange("p (h k) -> p h k", k=4)[:, :, 0]
        link(nc.vector.tensor_tensor(pc, pc, sm[:, 1:5], ALU.add))
        link(nc.vector.tensor_scalar(sm[:, 23:87], sm[:, 23:87], -1.0, None, ALU.mult))
        v.wait_ge(S["selectors"], 16)
        nc.vector.tensor_copy(m.sel[:, :, :].rearrange("p a n -> p (a n)"), sel32.rearrange("p a n -> p (a n)"))
        for n in range(20):
            v.wait_ge(S["folded"], n + 1)
            nc.vector.tensor_copy(m.fw[:, n // 4, n % 4, :], m.ps[n % 4][:, :]).then_inc(S["folded_copied"], 1)

    def scalar(a, S):
        a.wait_ge(S["sp_in"], 1)
        nc.scalar.activation(sm[:, 90:91], sm[:, 89:90], ACT.Exp).then_inc(S["exps"], 1)
        nc.scalar.activation(sm[:, 93:97], m.W("res"), ACT.Exp, scale=-1.0).then_inc(S["exps"], 1)
        nc.scalar.activation(sm[:, 97:98], m.W("sw"), ACT.Exp, scale=-1.0).then_inc(S["exps"], 1)
        nc.scalar.activation(sm[:, 23:87], m.W("Alog"), ACT.Exp).then_inc(S["exps"], 1)
        a.wait_ge(S["exps"], 4)
        nc.scalar.activation(sm[:, 91:92], sm[:, 90:91], ACT.Ln, bias=sm[:, 122:123]).then_inc(S["exps"], 2)

    run_block(nc, "setup", {"sync": sync, "tensor": tensor, "vector": vector, "scalar": scalar})


QN, KN, KB, VS, VB, BETA = 3, 4, 5, 6, 8, 9
RQ, RK, VT, KT, KBT = 10, 11, 12, 13, 14
KBD, QBD, KTBD, KBTBD = 15, 19, 23, 27
NATBD, XTBD = 31, 35
ATTBD, WTBD = 31, 15
XST, ZST, XTST, UST, FL, SCR = 0, 1, 2, 9, 14, 10
SHORT, DELTA = 8, 5


def bd(m, slot):
    return m.work[:, slot:slot + 4, :].rearrange("p a n -> p (a n)").rearrange("p (c h t) -> p c h t", c=NCH, h=H)


def spread(ap2d):
    return ap2d.rearrange("p (c t) -> p c t", t=32).unsqueeze(2).to_broadcast([128, NCH, H, 32])


def over_chunks(mask):
    return mask.rearrange("p (h t) -> p h t", h=H).unsqueeze(1).to_broadcast([128, NCH, H, 32])


def st_over_chunks(mask):
    return mask.unsqueeze(1).to_broadcast([128, NCH, 32])


def l0_inputs(nc, m, x_dram, b):
    vs = m.work[:, VS:VS + 2, :].rearrange("p a n -> p (a n)")[:, 64:64 + L]

    def sync(sp, S):
        sp.dma_start(m.x[:, :], x_dram[bass.ds(b, 1), :, :].rearrange("o c t -> (o c) t")).then_inc(S["x_loaded"], 16)

    def tensor(pe, S):
        ln_tensor(nc, pe, S, m, loaded=16)
        pe.wait_ge(S["h_ready"], 1)
        for p in range(3):
            for j in range(4):
                last = nc.tensor.matmul(m.ps[2 + p][:, :], m.qkvw[:, p, j, :], m.hp[:, PAD - 3 + j:PAD - 3 + j + L],
                                        start=(j == 0), stop=(j == 3))
            last.then_inc(S["qkv"], 1)
        nc.tensor.matmul(m.ps[5][:, :], m.W("Wb"), m.h, start=True, stop=True).then_inc(S["qkv"], 1)
        for i, slot in enumerate((0, 1)):
            pe.wait_ge(S["squares"], i + 1)
            nc.tensor.matmul(m.ps[6 + i][:, :], m.T("head_ones"), m.s(slot), start=True, stop=True).then_inc(S["norms"], 1)

    def scalar(a, S):
        ln_scalar(nc, a, S, m)
        for p, out in enumerate((m.s(QN), m.s(KN), vs)):
            a.wait_ge(S["qkv"], p + 1)
            nc.scalar.activation(out, m.ps[2 + p][:, :], ACT.Silu).then_inc(S["silu"], 1)
        a.wait_ge(S["qkv"], 4)
        nc.scalar.activation(m.s(BETA), m.ps[5][:, :], ACT.Tanh, scale=0.5).then_inc(S["tanh"], 1)
        a.wait_ge(S["silu"], 2)
        a.wait_ge(S["h_ready"], 1)
        nc.scalar.activation(m.s(0), m.s(QN), ACT.Square).then_inc(S["squares"], 1)
        nc.scalar.activation(m.s(1), m.s(KN), ACT.Square).then_inc(S["squares"], 1)
        for i, slot in enumerate((RQ, RK)):
            a.wait_ge(S["norms"], i + 1)
            nc.scalar.activation(m.s(slot), m.ps[6 + i][:, :], ACT.Ln, bias=m.small[:, 121:122]).then_inc(S["logs"], 1)
        for i, slot in enumerate((RQ, RK)):
            a.wait_ge(S["logs"], i + 1)
            nc.scalar.activation(m.s(slot), m.s(slot), ACT.Exp, scale=-0.5).then_inc(S["rnorm"], 1)

    def vector(v, S):
        ln_vector(nc, v, S, m)
        link = linker(v, S["chain"])
        nc.vector.memset(m.work[:, VS, 0:64], 0.0)
        v.wait_ge(S["tanh"], 1)
        link(nc.vector.tensor_scalar(m.s(BETA), m.s(BETA), 0.5, 0.5, ALU.mult, ALU.add))
        v.wait_ge(S["silu"], 3)
        link(nc.vector.tensor_tensor(m.s(VB), vs, m.s(BETA), ALU.mult))
        nc.vector.transpose(m.s(VT), m.s(VB))
        v.wait_ge(S["rnorm"], 1)
        v.wait_ge(S["squares"], 2)
        nc.vector.tensor_tensor(m.s(QN), m.s(QN), m.s(RQ), ALU.mult).then_inc(S["qn"], 1)
        v.wait_ge(S["rnorm"], 2)
        link(nc.vector.tensor_tensor(m.s(KN), m.s(KN), m.s(RK), ALU.mult))
        link(nc.vector.tensor_tensor(m.s(KB), m.s(KN), m.s(BETA), ALU.mult))
        nc.vector.transpose(m.s(KT), m.s(KN)).then_inc(S["kt"], 1)
        nc.vector.transpose(m.s(KBT), m.s(KB)).then_inc(S["kt"], 1)
        nc.vector.tensor_tensor(bd(m, KBD), spread(m.s(KN)), over_chunks(m.T("head_ones")), ALU.mult)
        v.wait_ge(S["qn"], 1)
        nc.vector.tensor_tensor(bd(m, QBD), spread(m.s(QN)), over_chunks(m.T("head_ones")), ALU.mult)
        v.wait_ge(S["kt"], 2)
        nc.vector.tensor_tensor(bd(m, KBTBD), spread(m.s(KBT)), over_chunks(m.T("head_ones")), ALU.mult)

    def gpsimd(g, S):
        g.wait_ge(S["kt"], 1)
        nc.gpsimd.tensor_tensor(bd(m, KTBD), spread(m.s(KT)), over_chunks(m.T("head_ones")), ALU.mult)

    run_block(nc, "qkv", {"sync": sync, "tensor": tensor, "vector": vector, "scalar": scalar, "gpsimd": gpsimd})


def l0_delta(nc, m):
    vp = m.work[:, VS:VS + 2, :].rearrange("p a n -> p (a n)")
    cols = lambda n: slice(32 * n, 32 * n + 32)
    A_PS, ATT_PS, Z_PS, Y_PS, W_PS = 0, 1, 2, 3, 1
    U_PS, S_PS, O_PS, FL_PS, FS_PS = 2, 3, 4, 5, 6
    state = lambda n: m.work[:, QN + n % 2, 0:32]
    LEVELS = (2, 4, 8, 16)

    def tensor(pe, S):
        for n in range(NCH):
            last = nc.tensor.matmul(m.ps[A_PS][:, cols(n)], bd(m, KBD)[:, n, :, :].rearrange("p h t -> p (h t)"),
                                    m.s(KB)[:, cols(n)], start=True, stop=True)
        last.then_inc(S["gram"], 1)
        for n in range(NCH):
            last = nc.tensor.matmul(m.ps[ATT_PS][:, cols(n)], bd(m, KBD)[:, n, :, :].rearrange("p h t -> p (h t)"),
                                    m.s(QN)[:, cols(n)], start=True, stop=True)
        last.then_inc(S["attn"], 1)
        for k in range(FIR_S):
            last = nc.tensor.matmul(m.ps[FS_PS][:, :], m.firw[:, k, :], vp[:, 64 - (FIR_S - 1) + k:64 - (FIR_S - 1) + k + L],
                                    start=(k == 0), stop=(k == FIR_S - 1))
        last.then_inc(S["fir_short"], 1)
        for i in range(len(LEVELS)):
            pe.wait_ge(S["xt_bd"], i + 1)
            for n in range(NCH):
                last = nc.tensor.matmul(m.ps[Z_PS][:, cols(n)], bd(m, NATBD)[:, n, :, :].rearrange("p h t -> p (h t)"),
                                        m.s(XST)[:, cols(n)], start=True, stop=True)
            last.then_inc(S["z"], 1)
            pe.wait_ge(S["z_plus"], i + 1)
            for n in range(NCH):
                last = nc.tensor.matmul(m.ps[Y_PS][:, cols(n)], bd(m, XTBD)[:, n, :, :].rearrange("p h t -> p (h t)"),
                                        m.s(ZST)[:, cols(n)], start=True, stop=True)
            last.then_inc(S["y"], 1)
        pe.wait_ge(S["inv_t"], len(LEVELS))
        pe.wait_ge(S["attn_bd"], 1)
        for n in range(NCH):
            last = nc.tensor.matmul(m.ps[W_PS][:, cols(n)], bd(m, KBTBD)[:, n, :, :].rearrange("p h t -> p (h t)"),
                                    m.s(XTST)[:, cols(n)], start=True, stop=True)
        last.then_inc(S["wt"], 1)
        pe.wait_ge(S["wt_bd"], 1)
        pe.wait_ge(S["xt_bd"], 5)
        flat = lambda slot, n: bd(m, slot)[:, n, :, :].rearrange("p h t -> p (h t)")
        tap = 0
        for n in range(NCH):
            if n:
                pe.wait_ge(S["state"], n)
            nc_last = nc.tensor.matmul(m.ps[U_PS][:, cols(n)], flat(XTBD, n), m.s(VT)[:, cols(n)], start=True, stop=(n == 0))
            if n:
                nc_last = nc.tensor.matmul(m.ps[U_PS][:, cols(n)], flat(WTBD, n), state(n), start=False, stop=True)
            nc_last.then_inc(S["u"], 1)
            if n:
                nc.tensor.matmul(m.ps[O_PS][:, cols(n)], flat(QBD, n), state(n), start=True, stop=False)
            pe.wait_ge(S["u_copied"], n + 1)
            if n < NCH - 1:
                nc.tensor.matmul(m.ps[S_PS][:, cols(n)], flat(KTBD, n), m.s(UST)[:, cols(n)], start=True, stop=True).then_inc(S["ku"], 1)
            nc.tensor.matmul(m.ps[O_PS][:, cols(n)], flat(ATTBD, n), m.s(UST)[:, cols(n)], start=(n == 0), stop=True).then_inc(S["o"], 1)
            for _ in range(FIR_PE // NCH):
                last = nc.tensor.matmul(m.ps[FL_PS][:, :], m.firw[:, FIR_S + tap, :], vp[:, 1 + tap:1 + tap + L],
                                        start=(tap == 0), stop=(tap == FIR_PE - 1))
                tap += 1
        last.then_inc(S["fir_long"], 1)

    def vector(v, S):
        link = linker(v, S["chain"])
        v.wait_ge(S["gram"], 1)
        nc.vector.tensor_tensor(bd(m, NATBD), spread(m.ps[A_PS][:, :]), over_chunks(m.T("neg_blk")), ALU.mult).then_inc(S["nat"], 1)
        link(nc.vector.transpose(m.s(SCR), m.ps[A_PS][:, :]))
        ch = lambda ap: ap.rearrange("p (c t) -> p c t", t=32)
        link(nc.vector.tensor_tensor(ch(m.s(SCR)), ch(m.s(SCR)), st_over_chunks(m.T("neg_level1")), ALU.mult))
        link(nc.vector.tensor_tensor(ch(m.s(XST)), ch(m.s(SCR)), st_over_chunks(m.T("ident_st")), ALU.add))
        link(nc.vector.transpose(m.s(XTST), m.s(XST)))
        nc.vector.tensor_tensor(bd(m, XTBD), spread(m.s(XTST)), over_chunks(m.T("head_ones")), ALU.mult).then_inc(S["xt_bd"], 1)
        for i, s in enumerate(LEVELS):
            v.wait_ge(S["z"], i + 1)
            link(nc.vector.tensor_tensor(ch(m.s(SCR)), ch(m.ps[Z_PS][:, :]), st_over_chunks(m.T(f"level{s}")), ALU.mult))
            nc.vector.tensor_tensor(ch(m.s(ZST)), ch(m.s(SCR)), st_over_chunks(m.T("ident_st")), ALU.add).then_inc(S["z_plus"], 1)
            v.wait_ge(S["y"], i + 1)
            if s < 16:
                link(nc.vector.tensor_copy(m.s(XST), m.ps[Y_PS][:, :]))
            nc.vector.transpose(m.s(XTST), m.ps[Y_PS][:, :]).then_inc(S["inv_t"], 1)
            v.wait_ge(S["inv_t"], i + 1)
            nc.vector.tensor_tensor(bd(m, XTBD), spread(m.s(XTST)), over_chunks(m.T("head_ones")), ALU.mult).then_inc(S["xt_bd"], 1)
        nc.vector.tensor_tensor(bd(m, ATTBD), spread(m.ps[ATT_PS][:, :]), over_chunks(m.T("causal_bd")), ALU.mult).then_inc(S["attn_bd"], 1)
        v.wait_ge(S["wt"], 1)
        nc.vector.tensor_tensor(bd(m, WTBD), spread(m.ps[W_PS][:, :]), over_chunks(m.T("neg_blk")), ALU.mult).then_inc(S["wt_bd"], 1)
        tap = FIR_PE
        for n in range(NCH):
            v.wait_ge(S["u"], n + 1)
            nc.vector.tensor_copy(m.s(UST)[:, cols(n)], m.ps[U_PS][:, cols(n)]).then_inc(S["u_copied"], 1)
            if n < NCH - 1:
                v.wait_ge(S["ku"], n + 1)
                if n:
                    v.wait_ge(S["state"], n)
                    nc.vector.tensor_tensor(state(n + 1), state(n), m.ps[S_PS][:, cols(n)], ALU.add).then_inc(S["state"], 1)
                else:
                    nc.vector.tensor_copy(state(1), m.ps[S_PS][:, cols(0)]).then_inc(S["state"], 1)
            for _ in range((FIR_L - FIR_PE) // NCH):
                w = m.W("fir_l")[:, tap:tap + 1]
                if tap > FIR_PE:
                    v.wait_ge(S["fir_acc"], tap - FIR_PE)
                    nc.vector.scalar_tensor_tensor(m.s(FL), vp[:, 1 + tap:1 + tap + L], w, m.s(FL), ALU.mult, ALU.add).then_inc(S["fir_acc"], 1)
                else:
                    nc.vector.tensor_scalar(m.s(FL), vp[:, 1 + tap:1 + tap + L], w, None, ALU.mult).then_inc(S["fir_acc"], 1)
                tap += 1
        v.wait_ge(S["fir_acc"], FIR_L - FIR_PE)
        v.wait_ge(S["fir_long"], 1)
        nc.vector.tensor_tensor(m.s(FL), m.s(FL), m.ps[FL_PS][:, :], ALU.add)
        v.wait_ge(S["o"], NCH)
        nc.vector.transpose(m.s(DELTA), m.ps[O_PS][:, :])

    def scalar(a, S):
        a.wait_ge(S["fir_short"], 1)
        nc.scalar.activation(m.s(SHORT), m.ps[FS_PS][:, :], ACT.Copy)

    run_block(nc, "delta", {"tensor": tensor, "vector": vector, "scalar": scalar})


def l0_gate(nc, m):
    vs = m.work[:, VS:VS + 2, :].rearrange("p a n -> p (a n)")[:, 64:64 + L]
    streams = (m.s(SHORT), m.s(FL), m.s(DELTA), vs)
    ABS, SQ, ST, M2, HG = 15, 19, 23, 24, 25
    PRT, O, T1, T2 = 29, 30, 31, 32
    tok = m.work[:, 33, :]
    lg, mx, pr = tok[:, 0:64], tok[:, 64:80], tok[:, 80:144]
    rs = tok[:, 144:160]
    j4 = lambda ap: ap.rearrange("p (g k) -> p g k", k=4)
    b16 = lambda ap: ap.unsqueeze(2).to_broadcast([128, 16, 4])

    def tensor(pe, S):
        sel = m.T("stat_sel")
        for s in range(4):
            nc.tensor.matmul(m.ps[0][0:16, :], sel[:, 16 * s:16 * s + 16], streams[s], start=(s == 0), stop=(s == 3))
        for s in range(4):
            pe.wait_ge(S["abs_sq"], 2 * s + 1)
            nc.tensor.matmul(m.ps[1][0:16, :], sel[:, 16 * s:16 * s + 16], m.s(ABS + s), start=(s == 0), stop=(s == 3))
            pe.wait_ge(S["abs_sq"], 2 * s + 2)
            last = nc.tensor.matmul(m.ps[2][0:16, :], sel[:, 16 * s:16 * s + 16], m.s(SQ + s), start=(s == 0), stop=(s == 3))
        last.then_inc(S["sums"], 1)
        pe.wait_ge(S["stats"], 4)
        for h in range(4):
            bank = m.ps[3 + h % 2]
            if h >= 2:
                pe.wait_ge(S["gelu"], h - 1)
            nc.tensor.matmul(bank[:, :], m.W("W1x"), m.h, start=True, stop=False)
            nc.tensor.matmul(bank[:, :], m.W("W1s")[:, 128 * h:128 * h + 128], m.s(ST), start=False, stop=True).then_inc(S["hid"], 1)
        for h in range(4):
            pe.wait_ge(S["gelu"], h + 1)
            for t in range(NT):
                c = 16 * t + 4 * h
                last = nc.tensor.matmul(m.ps[5][:, c:c + 4], m.s(HG + h)[:, 128 * t:128 * t + 128], m.W("W2"), start=True, stop=True)
        last.then_inc(S["logits"], 1)
        pe.wait_ge(S["probs"], 1)
        for t in range(NT):
            last = nc.tensor.transpose(m.ps[6][0:16, 128 * t:128 * t + 128], pr[:, 16 * t:16 * t + 16], m.T("ident"))
        last.then_inc(S["probs_t"], 1)
        pe.wait_ge(S["probs_sb"], 1)
        for k in range(4):
            nc.tensor.matmul(m.ps[k][:, :], m.T("prob_sel")[0:16, 128 * k:128 * k + 128], m.s(PRT)[0:16, :], start=True, stop=True).then_inc(S["prob_bc"], 1)
        pe.wait_ge(S["o_sq"], 1)
        nc.tensor.matmul(m.ps[7][:, :], m.T("head_mean"), m.s(T1), start=True, stop=True).then_inc(S["o_ms"], 1)
        pe.wait_ge(S["o_norm"], 1)
        nc.tensor.matmul(m.ps[5][:, :], m.W("Wo"), m.s(T2), start=True, stop=True).then_inc(S["proj"], 1)

    def scalar(a, S):
        for s in range(4):
            nc.scalar.activation(m.s(ABS + s), streams[s], ACT.Abs).then_inc(S["abs_sq"], 1)
            nc.scalar.activation(m.s(SQ + s), streams[s], ACT.Square).then_inc(S["abs_sq"], 1)
        a.wait_ge(S["sums"], 1)
        a.wait_ge(S["st_zero"], 1)
        nc.scalar.activation(m.s(M2)[0:16, :], m.ps[0][0:16, :], ACT.Square).then_inc(S["mean_sq"], 1)
        nc.scalar.activation(m.s(ST)[0:16, :], m.ps[0][0:16, :], ACT.Copy).then_inc(S["stats"], 1)
        nc.scalar.activation(m.s(ST)[64:80, :], m.ps[1][0:16, :], ACT.Copy).then_inc(S["stats"], 1)
        nc.scalar.activation(m.s(ST)[96:112, :], m.ps[2][0:16, :], ACT.Sqrt, scale=32.0).then_inc(S["stats"], 1)
        for h in range(4):
            a.wait_ge(S["hid"], h + 1)
            nc.scalar.activation(m.s(HG + h), m.ps[3 + h % 2][:, :], ACT.Gelu, bias=m.W("b1")).then_inc(S["gelu"], 1)
        a.wait_ge(S["shifted"], 1)
        nc.scalar.activation(pr, lg, ACT.Exp).then_inc(S["exp"], 1)
        a.wait_ge(S["probs_t"], 1)
        nc.scalar.activation(m.s(PRT)[0:16, :], m.ps[6][0:16, :], ACT.Copy).then_inc(S["probs_sb"], 1)
        a.wait_ge(S["o"], 1)
        nc.scalar.activation(m.s(T1), m.s(O), ACT.Square).then_inc(S["o_sq"], 1)
        a.wait_ge(S["o_ms"], 1)
        nc.scalar.activation(m.s(T2), m.ps[7][:, :], ACT.Ln, bias=m.small[:, 120:121]).then_inc(S["o_ln"], 1)
        a.wait_ge(S["o_ln"], 1)
        nc.scalar.activation(m.s(T2), m.s(T2), ACT.Exp, scale=-0.5).then_inc(S["o_rstd"], 1)

    def vector(v, S):
        link = linker(v, S["chain"])
        nc.vector.memset(m.s(ST), 0.0).then_inc(S["st_zero"], 1)
        v.wait_ge(S["st_zero"], 1)
        v.wait_ge(S["mean_sq"], 1)
        v.wait_ge(S["stats"], 3)
        nc.vector.tensor_tensor(m.s(ST)[32:48, :], m.ps[2][0:16, :], m.s(M2)[0:16, :], ALU.subtract).then_inc(S["stats"], 1)
        v.wait_ge(S["logits"], 1)
        link(nc.vector.tensor_tensor(j4(lg), j4(m.ps[5][:, 0:64]), m.W("b2").unsqueeze(1).to_broadcast([128, 16, 4]), ALU.add))
        link(nc.vector.tensor_scalar(lg, lg, m.small[:, 0:1], None, ALU.mult))
        link(nc.vector.tensor_reduce(mx, j4(lg), AXX, ALU.max))
        nc.vector.tensor_tensor(j4(lg), j4(lg), b16(mx), ALU.subtract).then_inc(S["shifted"], 1)
        v.wait_ge(S["exp"], 1)
        link(nc.vector.tensor_reduce(rs, j4(pr), AXX, ALU.add))
        link(nc.vector.reciprocal(rs, rs))
        link(nc.vector.tensor_tensor(j4(pr), j4(pr), b16(rs), ALU.mult))
        pc = m.small[:, 5:21].unsqueeze(1).to_broadcast([128, 4, 16])
        t16 = lambda ap: ap.rearrange("p (t k) -> p t k", t=4)
        nc.vector.scalar_tensor_tensor(t16(pr), t16(pr), 1.0 - 2.0 * 0.08, pc, ALU.mult, ALU.add).then_inc(S["probs"], 1)
        v.wait_ge(S["prob_bc"], 1)
        link(nc.vector.tensor_tensor(m.s(O), streams[0], m.ps[0][:, :], ALU.mult))
        for k in range(1, 4):
            v.wait_ge(S["prob_bc"], k + 1)
            link(nc.vector.tensor_tensor(m.s(T2), streams[k], m.ps[k][:, :], ALU.mult))
            add = nc.vector.tensor_tensor(m.s(O), m.s(O), m.s(T2), ALU.add)
            if k < 3:
                link(add)
        add.then_inc(S["o"], 1)
        v.wait_ge(S["o"], 1)
        v.wait_ge(S["o_rstd"], 1)
        nc.vector.scalar_tensor_tensor(m.s(T2), m.s(O), m.W("rms"), m.s(T2), ALU.mult, ALU.mult).then_inc(S["o_norm"], 1)
        v.wait_ge(S["proj"], 1)
        nc.vector.tensor_tensor(m.x[:, :], m.x[:, :], m.ps[5][:, :], ALU.add)

    run_block(nc, "gate", {"tensor": tensor, "vector": vector, "scalar": scalar})


def l0_ffn(nc, m):
    R, K, K2 = 3, 4, 5

    def tensor(pe, S):
        ln_tensor(nc, pe, S, m)
        pe.wait_ge(S["h_ready"], 1)
        for i in range(2):
            nc.tensor.matmul(m.ps[2 + i][:, :], m.mixw[:, 2 * i, :], m.h, start=True, stop=False)
            nc.tensor.matmul(m.ps[2 + i][:, :], m.mixw[:, 2 * i + 1, :], m.hp[:, PAD - 1:PAD - 1 + L], start=False, stop=True).then_inc(S["rk"], 1)
        pe.wait_ge(S["k_act"], 1)
        nc.tensor.matmul(m.ps[4][:, :], m.W("Wvf"), m.s(K2), start=True, stop=True).then_inc(S["kv"], 1)

    def scalar(a, S):
        ln_scalar(nc, a, S, m)
        a.wait_ge(S["rk"], 1)
        nc.scalar.activation(m.s(R), m.ps[2][:, :], ACT.Sigmoid).then_inc(S["r"], 1)
        a.wait_ge(S["rk"], 2)
        nc.scalar.activation(m.s(K), m.ps[3][:, :], ACT.Relu).then_inc(S["relu"], 1)

    def vector(v, S):
        ln_vector(nc, v, S, m)
        v.wait_ge(S["relu"], 1)
        nc.vector.tensor_tensor(m.s(K2), m.s(K), m.s(K), ALU.mult).then_inc(S["k_act"], 1)
        v.wait_ge(S["kv"], 1)
        v.wait_ge(S["r"], 1)
        nc.vector.tensor_tensor(m.s(R), m.s(R), m.ps[4][:, :], ALU.mult).then_inc(S["rv"], 1)
        v.wait_ge(S["rv"], 1)
        nc.vector.tensor_tensor(m.x[:, :], m.x[:, :], m.s(R), ALU.add)

    run_block(nc, "ffn", {"tensor": tensor, "vector": vector, "scalar": scalar})


C_PC = 3
C_X1, C_ZS, C_DEL, C_DU = 4, 8, 10, 14
C_XT, C_XP, C_T = 18, 20, 23
C_ACC = 33
C_DA, C_DBU, C_HS, C_HC, C_CS = 4, 30, (0, 28), 35, 37
C_XC = (18, 19, 20, 21)
C_YP, C_U = 22, 22
C_TH = (2, 32)


def l1_inputs(nc, m):
    xp = m.work[:, C_XP:C_XP + 3, :].rearrange("p a n -> p (a n)")[:, 0:2 * (L + 8)].rearrange("p (k n) -> p k n", k=2)
    xt = m.work[:, C_XT:C_XT + 2, :].rearrange("p a n -> p (a n)")
    pc = m.work[:, C_PC, :].bitcast(BF16).rearrange("p (e n) -> p e n", e=2)
    i4 = [(e, k) for e in range(2) for k in range(2)]

    def tensor(pe, S):
        ln_tensor(nc, pe, S, m)
        pe.wait_ge(S["h_ready"], 1)
        for k in range(4):
            nc.tensor.matmul(m.ps[2 + k][:, :], m.W("inp")[:, 128 * k:128 * k + 128], m.h, start=True, stop=True).then_inc(S["xz"], 1)
        for t in range(NT):
            last = nc.tensor.matmul(m.ps[6 + t // 2][:, 256 * (t % 2):256 * (t % 2) + 256], m.h[:, 128 * t:128 * t + 128],
                                    m.W("inp")[:, 0:256], start=True, stop=True)
        last.then_inc(S["xt"], 1)
        for e in range(2):
            for k in range(2):
                pe.wait_ge(S["x1"], 2 * e + k + 1)
                last = nc.tensor.matmul(m.ps[e][:, :], m.W("xproj")[:, 256 * e + 128 * k:256 * e + 128 * k + 128], m.s(C_X1 + 2 * e + k),
                                        start=(k == 0), stop=(k == 1))
            last.then_inc(S["xdbl"], 1)
        for i, (e, k) in enumerate(i4):
            pe.wait_ge(S["xd"], e + 1)
            if i == 0:
                pe.wait_ge(S["xz_used"], 4)
            nc.tensor.matmul(m.ps[2 + i][:, :], m.W("dtproj")[:, 256 * e + 128 * k:256 * e + 128 * k + 128], m.s(C_T + 8 + e),
                             start=True, stop=True).then_inc(S["dt"], 1)

    def scalar(a, S):
        ln_scalar(nc, a, S, m)
        for k in range(2):
            a.wait_ge(S["xz"], k + 1)
            nc.scalar.activation(xp[:, k, 4:4 + L], m.ps[2 + k][:, :], ACT.Copy).then_inc(S["xz_used"], 1)
        for k in range(2):
            a.wait_ge(S["xz"], k + 3)
            nc.scalar.activation(m.s(C_ZS + k), m.ps[4 + k][:, :], ACT.Silu).then_inc(S["xz_used"], 1)
        a.wait_ge(S["xt"], 1)
        for t in range(2):
            nc.scalar.activation(xt[:, 512 * t:512 * t + 512], m.ps[6 + t][:, :], ACT.Copy).then_inc(S["xt_sb"], 1)
        for i in range(4):
            a.wait_ge(S["conv"], i + 1)
            nc.scalar.activation(m.s(C_X1 + i), m.s(C_T + i), ACT.Silu).then_inc(S["x1"], 1)
        for e in range(2):
            a.wait_ge(S["xdbl"], e + 1)
            nc.scalar.activation(m.s(C_T + 8 + e), m.ps[e][:, :], ACT.Copy).then_inc(S["xd"], 1)
        for i in range(4):
            a.wait_ge(S["sp_in"], i + 1)
            nc.scalar.activation(m.s(C_T + i), m.s(C_T + i), ACT.Exp).then_inc(S["sp_exp"], 1)
        for i in range(4):
            a.wait_ge(S["sp_exp"], i + 1)
            nc.scalar.activation(m.s(C_T + i), m.s(C_T + i), ACT.Ln, bias=m.small[:, 122:123]).then_inc(S["sp_ln"], 1)

    def vector(v, S):
        link = linker(v, S["chain"])
        nc.vector.memset(xp[:, :, 0:4], 0.0)
        link(nc.vector.memset(xp[:, :, 4 + L:8 + L], 0.0))
        ln_vector(nc, v, S, m)
        v.wait_ge(S["xz_used"], 2)
        for i, (e, k) in enumerate(i4):
            w = m.W("mconv")[:, 4 * i:4 * i + 4]
            src = lambda j: xp[:, k, 1 + j:1 + j + L] if e == 0 else xp[:, k, 7 - j:7 - j + L]
            link(nc.vector.tensor_scalar(m.s(C_T + i), src(0), w[:, 0:1], m.W("mconvb")[:, i:i + 1], ALU.mult, ALU.add))
            for j in range(1, 4):
                last = nc.vector.scalar_tensor_tensor(m.s(C_T + i), src(j), w[:, j:j + 1], m.s(C_T + i), ALU.mult, ALU.add)
                if j < 3:
                    link(last)
            last.then_inc(S["conv"], 1)
        v.wait_ge(S["xz_used"], 4)
        for k in range(2):
            link(nc.vector.tensor_reduce(m.small[:, 100 + k:101 + k], m.s(C_ZS + k), AXX, ALU.max))
        r1, md = m.s(C_T + 5)[0:32, :], m.s(C_T + 6).bitcast(BF16)[0:32, 0:L]
        for e in range(2):
            v.wait_ge(S["xd"], e + 1)
            full = m.s(C_T + 8 + e)[0:32, :]
            link(nc.vector.tensor_copy(pc[0:32, e, :], full))
            link(nc.vector.tensor_tensor(r1, full, pc[0:32, e, :], ALU.subtract))
            link(nc.vector.tensor_copy(md, r1))
            link(nc.vector.tensor_tensor(r1, r1, md, ALU.subtract))
            nc.vector.tensor_copy(pc[32:64, e, :], md)
            link(nc.vector.tensor_copy(pc[64:96, e, :], r1))
        for i in range(4):
            v.wait_ge(S["dt"], i + 1)
            v.wait_ge(S["x1"], 4)
            nc.vector.tensor_scalar(m.s(C_T + i), m.ps[2 + i][:, :], m.W("dtb")[:, i:i + 1], SP_CAP, ALU.add, ALU.min).then_inc(S["sp_in"], 1)
        for i in range(4):
            v.wait_ge(S["sp_ln"], i + 1)
            link(nc.vector.scalar_tensor_tensor(m.s(C_DEL + i), m.ps[2 + i][:, :], m.W("dtb")[:, i:i + 1], m.s(C_T + i), ALU.add, ALU.max))
            nc.vector.tensor_tensor(m.s(C_DU + i), m.s(C_DEL + i), m.s(C_X1 + i), ALU.mult)
        for k in range(2):
            link(nc.vector.tensor_scalar(m.s(C_ACC + k), m.s(C_X1 + k), m.W("Dp")[:, k:k + 1], None, ALU.mult))
            nc.vector.scalar_tensor_tensor(m.s(C_ACC + k), m.s(C_X1 + 2 + k), m.W("Dp")[:, 2 + k:3 + k], m.s(C_ACC + k), ALU.mult, ALU.add)

    run_block(nc, "proj", {"tensor": tensor, "vector": vector, "scalar": scalar})


def l1_core(nc, m):
    xt = m.work[:, C_XT:C_XT + 2, :].rearrange("p a n -> p (a n)").rearrange("p (t c) -> p t c", t=NT)
    yp = m.work[:, C_YP:C_YP + 5, :].rearrange("p a n -> p (a n)")[:, 0:4 * 520].rearrange("p (k n) -> p k n", k=4)
    pc = m.work[:, C_PC, :].bitcast(BF16).rearrange("p (e n) -> p e n", e=2)
    u = m.work[:, C_U:C_U + 6, :].rearrange("p a n -> p (a n)").rearrange("p (t n) -> p t n", t=NT)
    xc = lambda o: m.s(C_XC[o])
    sq = xc
    two = lambda slot: m.work[:, slot:slot + 2, :]
    STEPS = [(e, n) for e in range(2) for n in range(NS)]

    units = ([("dft", c, r) for r in range(2) for c in range(2)] + [("conv", o, 0) for o in range(4)]
             + [("chan", t, 0) for t in range(4)] + [("time", c, r) for c in range(2) for r in range(2)])
    slices = [(i, k) for i, u_ in enumerate(units) for k in range({"dft": 1, "conv": 5, "chan": 1, "time": 2}[u_[0]])]
    plan = [slices[i * len(slices) // (len(STEPS) - 1):(i + 1) * len(slices) // (len(STEPS) - 1)] for i in range(len(STEPS) - 1)] + [[]]
    ends = [[i for i, k in p if k == {"dft": 1, "conv": 5, "chan": 1, "time": 2}[units[i][0]] - 1] for p in plan]
    bank = lambda i: m.ps[4 + i % 4]

    def products(i):
        kind, a, b = units[i]
        if kind == "dft":
            return [(xt[:, t, 128 * a:128 * a + 128], m.dft[:, b, t, :]) for t in range(NT)]
        if kind == "conv":
            return [(m.fw[:, t, k, 128 * a:128 * a + 128], yp[:, k, 2 + t:2 + t + L]) for t in range(TAPS) for k in range(4)]
        if kind == "chan":
            return [(xc(k)[:, 128 * a:128 * a + 128], m.inv[:, k, :]) for k in range(4)]
        c = 128 * a
        first = [(u[:, t, c:c + 128], m.dft[:, b, t, :]) for t in range(NT)]
        second = [(u[:, t, (512 if b == 0 else 256) + c:(512 if b == 0 else 256) + c + 128], m.dft[:, 1 - b, t, :]) for t in range(NT)]
        return first + second

    def tensor(pe, S):
        def rows(i):
            e, n = STEPS[i]
            if i >= 2:
                pe.wait_ge(S["dbu"], i - 1)
                pe.wait_ge(S["c_sb"], i - 1)
            nc.tensor.matmul(m.ps[i % 2][:, :], m.sel[0:96, n, :], pc[0:96, e, :], start=True, stop=True).then_inc(S["b_row"], 1)
            nc.tensor.matmul(m.ps[2 + i % 2][:, :], m.sel[0:96, NS + n, :], pc[0:96, e, :], start=True, stop=True).then_inc(S["c_row"], 1)
        rows(0)
        for i in range(len(STEPS)):
            if i + 1 < len(STEPS):
                rows(i + 1)
            for unit, part in plan[i]:
                kind = units[unit][0]
                if part == 0:
                    need = {"dft": 0, "conv": 4, "chan": 8, "time": 12}[kind]
                    if kind == "time":
                        pe.wait_ge(S["u_main"], NT)
                    if max(need, unit - 3) > 0:
                        pe.wait_ge(S["unit_out"], max(need, unit - 3))
                ps = products(unit)
                for j in range(4 * part, 4 * part + 4):
                    last = nc.tensor.matmul(bank(unit)[:, :], ps[j][0], ps[j][1], start=(j == 0), stop=(j == len(ps) - 1))
                if 4 * part + 4 == len(ps):
                    last.then_inc(S["unit"], 1)

    def scalar(a, S):
        def leave(i):
            kind, p, b = units[i]
            a.wait_ge(S["unit"], i + 1)
            if kind == "dft":
                nc.scalar.activation(yp[:, 2 * b + p, 4:4 + L], bank(i)[:, :], ACT.Copy, scale=(1.0, -1.0)[b]).then_inc(S["unit_out"], 1)
            elif kind == "conv":
                if i >= 6:
                    a.wait_ge(S["unit_out"], i - 1)
                nc.scalar.activation(m.s(C_TH[i % 2]), bank(i)[:, :], ACT.Tanh, bias=m.small[:, 104 + p:105 + p], scale=0.5).then_inc(S["tanh"], 1)
            elif kind == "chan":
                nc.scalar.activation(u[:, p, 0:512], bank(i)[:, :], ACT.Copy).then_inc(S["u_main"], 1)
                nc.scalar.activation(u[:, p, 512:768], bank(i)[:, 256:512], ACT.Copy, scale=-1.0).then_inc(S["unit_out"], 1)
            else:
                nc.scalar.activation(sq(i - 12), bank(i)[:, :], ACT.Square).then_inc(S["unit_out"], 1)

        for i, (e, n) in enumerate(STEPS):
            if i >= 2:
                a.wait_ge(S["h"], 2 * (i - 1))
            for k in range(2):
                c = SM["A"] + 32 * e + 16 * k + n
                nc.scalar.activation(m.s(C_DA + 2 * (i % 2) + k), m.s(C_DEL + 2 * e + k), ACT.Exp, scale=m.small[:, c:c + 1]).then_inc(S["da"], 1)
            a.wait_ge(S["c_row"], i + 1)
            if i >= 2:
                a.wait_ge(S["hc"], i - 1)
            nc.scalar.activation(m.s(C_CS + i % 2), m.ps[2 + i % 2][:, :], ACT.Copy).then_inc(S["c_sb"], 1)
            if i:
                for unit in ends[i - 1]:
                    leave(unit)

    def vector(v, S):
        link = linker(v, S["chain"])
        nc.vector.memset(yp[:, :, 0:4], 0.0)
        nc.vector.memset(yp[:, :, 4 + L:8 + L], 0.0)
        link(nc.vector.tensor_scalar(m.small[:, 104:108], m.W("fftb"), 0.5, None, ALU.mult))
        for i, (e, n) in enumerate(STEPS):
            v.wait_ge(S["b_row"], i + 1)
            if i:
                v.wait_ge(S["h"], 2 * i)
            nc.vector.tensor_tensor(two(C_DBU), two(C_DU + 2 * e), m.ps[i % 2][:, :].unsqueeze(1).to_broadcast([128, 2, L]), ALU.mult).then_inc(S["dbu"], 1)
            v.wait_ge(S["dbu"], i + 1)
            if i >= 2:
                v.wait_ge(S["hc"], i - 1)
            for k in range(2):
                v.wait_ge(S["da"], 2 * i + k + 1)
                s = slice(None) if e == 0 else slice(None, None, -1)
                nc.vector.tensor_tensor_scan(m.s(C_HS[i % 2] + k)[:, s], m.s(C_DA + 2 * (i % 2) + k)[:, s], m.s(C_DBU + k)[:, s], 0.0, ALU.mult, ALU.add).then_inc(S["h"], 1)
            if i:
                v.wait_ge(S["hc"], i)
                if i > 1:
                    v.wait_ge(S["acc"], i - 1)
                nc.vector.tensor_tensor(two(C_ACC), two(C_ACC), two(C_HC), ALU.add).then_inc(S["acc"], 1)
                for unit in ends[i - 1]:
                    if units[unit][0] == "conv":
                        o = unit - 4
                        v.wait_ge(S["tanh"], o + 1)
                        link(nc.vector.tensor_scalar(m.s(C_TH[unit % 2]), m.s(C_TH[unit % 2]), 0.5, 0.5, ALU.mult, ALU.add))
                        nc.vector.scalar_tensor_tensor(xc(o), bank(unit)[:, :], m.W("fftb")[:, o:o + 1], m.s(C_TH[unit % 2]), ALU.add, ALU.mult).then_inc(S["unit_out"], 1)
        last = len(STEPS)
        v.wait_ge(S["hc"], last)
        v.wait_ge(S["acc"], last - 1)
        nc.vector.tensor_tensor(two(C_ACC), two(C_ACC), two(C_HC), ALU.add)

    def gpsimd(g, S):
        for i, (e, n) in enumerate(STEPS):
            g.wait_ge(S["h"], 2 * i + 2)
            g.wait_ge(S["c_sb"], i + 1)
            if i:
                g.wait_ge(S["acc"], i)
            nc.gpsimd.tensor_tensor(two(C_HC), two(C_HS[i % 2]), m.s(C_CS + i % 2).unsqueeze(1).to_broadcast([128, 2, L]), ALU.mult).then_inc(S["hc"], 1)

    run_block(nc, "scan", {"tensor": tensor, "vector": vector, "scalar": scalar, "gpsimd": gpsimd})


def l1_output(nc, m):
    sq = lambda i: m.s(C_XC[i])
    sm = m.small

    def vector(v, S):
        link = linker(v, S["chain"])
        for k in range(2):
            nc.vector.tensor_tensor(sq(2 * k), sq(2 * k), sq(2 * k + 1), ALU.add).then_inc(S["power"], 1)
        for k in range(2):
            link(nc.vector.tensor_tensor(m.s(C_ACC + k), m.s(C_ACC + k), m.s(C_ZS + k), ALU.mult))
        link(nc.vector.tensor_scalar(sm[:, 102:104], sm[:, 100:102], -1.0, None, ALU.mult))
        link(nc.vector.tensor_tensor(sm[:, 100:102], sm[:, 100:102], sm[:, 102:104], ALU.max))
        for k in range(2):
            v.wait_ge(S["mag"], k + 1)
            link(nc.vector.bn_stats(m.s(0)[:, 0:6], sq(2 * k)))
            link(nc.vector.bn_aggr(m.s(0)[:, 8 + 2 * k:10 + 2 * k], m.s(0)[:, 0:6]))
            z, mean, var = sm[:, 100 + k:101 + k], m.s(0)[:, 8 + 2 * k:9 + 2 * k], m.s(0)[:, 9 + 2 * k:10 + 2 * k]
            link(nc.vector.tensor_tensor(var, var, z, ALU.mult))
            link(nc.vector.tensor_tensor(var, var, z, ALU.mult))
            nc.vector.tensor_scalar(m.s(0)[:, 16 + k:17 + k], var, 1e-5, None, ALU.add).then_inc(S["var"], 1)
        for k in range(2):
            v.wait_ge(S["std"], k + 1)
            z, mean = sm[:, 100 + k:101 + k], m.s(0)[:, 8 + 2 * k:9 + 2 * k]
            r = m.s(0)[:, 20 + k:21 + k]
            link(nc.vector.reciprocal(r, m.s(0)[:, 18 + k:19 + k]))
            link(nc.vector.tensor_tensor(r, r, z, ALU.mult))
            link(nc.vector.tensor_scalar(sq(2 * k), sq(2 * k), mean, r, ALU.subtract, ALU.mult))
            nc.vector.tensor_tensor(m.s(C_ACC + k), m.s(C_ACC + k), sq(2 * k), ALU.add).then_inc(S["y"], 1)
        v.wait_ge(S["proj"], 1)
        nc.vector.tensor_tensor(m.x[:, :], m.x[:, :], m.ps[0][:, :], ALU.add)

    def scalar(a, S):
        for k in range(2):
            a.wait_ge(S["power"], k + 1)
            nc.scalar.activation(sq(2 * k), sq(2 * k), ACT.Sqrt).then_inc(S["mag"], 1)
        for k in range(2):
            a.wait_ge(S["var"], k + 1)
            nc.scalar.activation(m.s(0)[:, 18 + k:19 + k], m.s(0)[:, 16 + k:17 + k], ACT.Sqrt).then_inc(S["std"], 1)

    def tensor(pe, S):
        for k in range(2):
            pe.wait_ge(S["y"], k + 1)
            last = nc.tensor.matmul(m.ps[0][:, :], m.W("outp")[:, 128 * k:128 * k + 128], m.s(C_ACC + k), start=(k == 0), stop=(k == 1))
        last.then_inc(S["proj"], 1)

    run_block(nc, "mout", {"tensor": tensor, "vector": vector, "scalar": scalar})


MASK, WGT, RF, HID, HM = 3, 11, 13, 15, 20
INT, VEL, HALT, DIF = 28, 29, 30, 31
SG, SA, SPT, ACCX, ACCV, TA = 32, 35, 16, 0, 1, 2


def l1_route(nc, m):
    tok = m.work[:, 38, :]
    lg, mx, eq, m2, pk = tok[:, 0:32], tok[:, 32:36], tok[:, 40:72], tok[:, 36:40], tok[:, 128:256]
    e8 = lambda ap: ap.rearrange("p (t k) -> p t k", k=8)
    b8 = lambda ap: ap.unsqueeze(2).to_broadcast([128, 4, 8])
    rb = m.work[:, RF + 1, :].bitcast(BF16)[:, 0:L]
    pk3 = pk.rearrange("p (t k) -> p t k", k=32)
    dec = m.T("dec").unsqueeze(1).to_broadcast([128, 4, 8])

    def tensor(pe, S):
        ln_tensor(nc, pe, S, m)
        pe.wait_ge(S["h_ready"], 1)
        nc.tensor.matmul(m.ps[2][:, :], m.W("m1")[:, 0:128], m.h, start=True, stop=True).then_inc(S["hid"], 1)
        pe.wait_ge(S["gelu"], 1)
        for t in range(NT):
            last = nc.tensor.matmul(m.ps[3][:, 8 * t:8 * t + 8], m.s(HID)[:, 128 * t:128 * t + 128], m.W("rw2"), start=True, stop=True)
        last.then_inc(S["logits"], 1)
        pe.wait_ge(S["packed"], 1)
        for t in range(NT):
            last = nc.tensor.transpose(m.ps[4][0:32, 128 * t:128 * t + 128], pk[:, 32 * t:32 * t + 32], m.T("ident"))
        last.then_inc(S["routes"], 1)
        pe.wait_ge(S["routes_sb"], 2)
        for r in range(2):
            nc.tensor.matmul(m.ps[5 + r][:, :], m.T("wsel")[0:32, 128 * r:128 * r + 128], m.s(RF)[0:32, :], start=True, stop=True).then_inc(S["w_bc"], 1)
        for i in range(8):
            if i >= 4:
                pe.wait_ge(S["mask_sb"], i - 3)
            nc.tensor.matmul(m.ps[i % 4][:, :], m.sel[0:32, 32 + i, :], rb[0:32, :], start=True, stop=True).then_inc(S["mask"], 1)

    def scalar(a, S):
        ln_scalar(nc, a, S, m)
        a.wait_ge(S["hid"], 1)
        nc.scalar.activation(m.s(HID), m.ps[2][:, :], ACT.Gelu, bias=m.W("m1b")).then_inc(S["gelu"], 1)
        a.wait_ge(S["shifted"], 1)
        nc.scalar.activation(lg, lg, ACT.Exp).then_inc(S["exp"], 1)
        a.wait_ge(S["routes"], 1)
        nc.scalar.activation(m.s(RF)[0:32, :], m.ps[4][0:32, :], ACT.Copy).then_inc(S["routes_sb"], 1)
        nc.scalar.activation(rb[0:32, :], m.ps[4][0:32, :], ACT.Copy).then_inc(S["routes_sb"], 1)
        for i in range(8):
            a.wait_ge(S["mask"], i + 1)
            nc.scalar.activation(m.s(MASK + i), m.ps[i % 4][:, :], ACT.Copy).then_inc(S["mask_sb"], 1)

    def vector(v, S):
        ln_vector(nc, v, S, m)
        link = linker(v, S["chain"])
        link(nc.vector.memset(pk, 0.0))
        v.wait_ge(S["logits"], 1)
        link(nc.vector.tensor_tensor(e8(lg), e8(m.ps[3][:, 0:32]), m.W("rb2").unsqueeze(1).to_broadcast([128, 4, 8]), ALU.add))
        link(nc.vector.tensor_reduce(mx, e8(lg), AXX, ALU.max))
        nc.vector.tensor_tensor(e8(lg), e8(lg), b8(mx), ALU.subtract).then_inc(S["shifted"], 1)
        v.wait_ge(S["exp"], 1)
        top = (mx, m2)
        for r in range(2):
            link(nc.vector.tensor_reduce(top[r], e8(lg), AXX, ALU.max))
            link(nc.vector.tensor_tensor(e8(eq), e8(lg), b8(top[r]), ALU.is_equal))
            link(nc.vector.tensor_tensor(e8(eq), e8(eq), dec, ALU.mult))
            link(nc.vector.tensor_reduce(tok[:, 76:80], e8(eq), AXX, ALU.max))
            link(nc.vector.tensor_tensor(pk3[:, :, 8 * r:8 * r + 8], e8(eq), b8(tok[:, 76:80]), ALU.is_equal))
            if r == 0:
                link(nc.vector.scalar_tensor_tensor(e8(lg), pk3[:, :, 0:8], -2.0, e8(lg), ALU.mult, ALU.add))
        s = tok[:, 80:84]
        link(nc.vector.tensor_tensor(s, mx, m2, ALU.add))
        link(nc.vector.reciprocal(s, s))
        link(nc.vector.tensor_tensor(pk3[:, :, 16], mx, s, ALU.mult))
        nc.vector.tensor_tensor(pk3[:, :, 17], m2, s, ALU.mult).then_inc(S["packed"], 1)
        for r in range(2):
            v.wait_ge(S["w_bc"], r + 1)
            nc.vector.tensor_scalar(m.s(WGT + r), m.ps[5 + r][:, :], m.small[:, 22:23], None, ALU.mult)
        nc.vector.tensor_copy(m.s(INT), m.h)

    run_block(nc, "route", {"tensor": tensor, "vector": vector, "scalar": scalar})


def l1_iterate(nc, m, it):
    K1 = 1 if it == 0 else 2
    src = (m.s(INT), m.s(VEL))
    sig = ([("a", s) for s in range(3)] if it else []) + [("g", s) for s in range(3)]
    outs = sig + [("b", s) for s in range(3)]
    col = {"a": 0, "b": 1, "g": 2}
    bank = lambda i: m.ps[5 + i % 3]
    place = {**{("a", s): m.s(SA + s) for s in range(3)}, **{("g", s): m.s(SG + s) for s in range(3)}, **{("b", s): m.s(SPT + s) for s in range(3)}}
    nsig = len(sig)

    def tensor(pe, S):
        for i in range(5):
            for k in range(K1):
                w = m.W("m1")[:, 128 * k:128 * k + 128] if i == 0 else m.W("e1")[:, 512 * k + 128 * (i - 1):512 * k + 128 * i]
                last = nc.tensor.matmul(m.ps[i][:, :], w, src[k], start=(k == 0), stop=(k == K1 - 1))
            last.then_inc(S["hid"], 1)
        pe.wait_ge(S["gelu"], 5)
        nc.tensor.matmul(m.ps[0][:, :], m.W("hw2"), m.s(HID), start=True, stop=True).then_inc(S["halt_lin"], 1)
        for i, (what, s) in enumerate(outs):
            if i >= 3:
                pe.wait_ge(S["ctrl_sig"], min(i - 2, nsig))
                if i - 2 > nsig:
                    pe.wait_ge(S["sp"], i - 2 - nsig)
            c = 128 * col[what]
            if s == 0:
                last = nc.tensor.matmul(bank(i)[:, :], m.W("s2")[:, c:c + 128], m.s(HID), start=True, stop=True)
            else:
                for t in range(4):
                    pe.wait_ge(S["masked"], 4 * (s - 1) + t + 1)
                    nc.tensor.matmul(bank(i)[:, :], m.W("e2")[:, 384 * t + c:384 * t + c + 128], m.s(HM + 4 * (s - 1) + t), start=(t == 0), stop=False)
                last = nc.tensor.matmul(bank(i)[:, :], m.W("e2b")[0:32, 384 * (s - 1) + c:384 * (s - 1) + c + 128], m.s(RF)[0:32, :], start=False, stop=True)
            last.then_inc(S["ctrl"], 1)

    def scalar(a, S):
        for i in range(5):
            a.wait_ge(S["hid"], i + 1)
            nc.scalar.activation(m.s(HID + i), m.ps[i][:, :], ACT.Gelu, bias=m.W("m1b") if i == 0 else m.W("e1b")[:, i - 1:i]).then_inc(S["gelu"], 1)
        a.wait_ge(S["halt_lin"], 1)
        nc.scalar.activation(m.s(HALT), m.ps[0][:, :], ACT.Sigmoid, bias=m.W("hb2")).then_inc(S["halt"], 1)
        for i, (what, s) in enumerate(sig):
            a.wait_ge(S["ctrl"], i + 1)
            if s == 0:
                nc.scalar.activation(place[what, s], bank(i)[:, :], ACT.Sigmoid, bias=m.W("s2b")[:, col[what]:col[what] + 1]).then_inc(S["ctrl_sig"], 1)
            else:
                nc.scalar.activation(place[what, s], bank(i)[:, :], ACT.Sigmoid).then_inc(S["ctrl_sig"], 1)
        for s in range(3):
            a.wait_ge(S["sp_in"], s + 1)
            nc.scalar.activation(m.s(SPT + s), m.s(SPT + s), ACT.Exp).then_inc(S["sp_exp"], 1)
            a.wait_ge(S["sp_exp"], s + 1)
            nc.scalar.activation(m.s(SPT + s), m.s(SPT + s), ACT.Ln, bias=m.small[:, 122:123]).then_inc(S["sp_ln"], 1)

    def vector(v, S):
        link = linker(v, S["chain"])
        nc.vector.tensor_scalar(m.s(DIF), m.s(INT), m.W("mu"), None, ALU.subtract).then_inc(S["dif"], 1)
        v.wait_ge(S["gelu"], 5)
        for i in range(8):
            nc.vector.tensor_tensor(m.s(HM + i), m.s(HID + 1 + i % 4), m.s(MASK + i), ALU.mult).then_inc(S["masked"], 1)
        v.wait_ge(S["dif"], 1)
        bias = lambda s: m.W("s2b")[:, 1:2] if s == 0 else m.small[:, 125:126]
        for s in range(3):
            i = nsig + s
            v.wait_ge(S["ctrl"], i + 1)
            nc.vector.tensor_scalar(m.s(SPT + s), bank(i)[:, :], bias(s), SP_CAP, ALU.add, ALU.min).then_inc(S["sp_in"], 1)
        for s in range(3):
            i = nsig + s
            v.wait_ge(S["sp_ln"], s + 1)
            nc.vector.scalar_tensor_tensor(m.s(SPT + s), bank(i)[:, :], bias(s), m.s(SPT + s), ALU.add, ALU.max).then_inc(S["sp"], 1)
            v.wait_ge(S["sp"], s + 1)
            link(nc.vector.scalar_tensor_tensor(m.s(TA), m.s(SPT + s), -1.0, m.s(DIF), ALU.mult, ALU.mult))
            if it:
                v.wait_ge(S["ctrl_sig"], nsig)
                link(nc.vector.tensor_tensor(m.s(SA + s), m.s(SA + s), m.s(VEL), ALU.mult))
                link(nc.vector.tensor_tensor(m.s(TA), m.s(TA), m.s(SA + s), ALU.add))
            if s == 0:
                link(nc.vector.tensor_scalar(m.s(ACCV), m.s(TA), m.small[:, 21:22], None, ALU.mult))
                v.wait_ge(S["ctrl_sig"], nsig)
                link(nc.vector.tensor_tensor(m.s(ACCX), m.s(ACCV), m.s(SG), ALU.mult))
            else:
                link(nc.vector.tensor_tensor(m.s(TA), m.s(TA), m.s(WGT + s - 1), ALU.mult))
                nc.vector.tensor_tensor(m.s(ACCV), m.s(ACCV), m.s(TA), ALU.add)
                link(nc.vector.tensor_tensor(m.s(SG + s), m.s(SG + s), m.s(TA), ALU.mult))
                link(nc.vector.tensor_tensor(m.s(ACCX), m.s(ACCX), m.s(SG + s), ALU.add))
        v.wait_ge(S["halt"], 1)
        link(nc.vector.scalar_tensor_tensor(m.s(TA), m.s(ACCX), 0.1, m.s(HALT), ALU.mult, ALU.mult))
        nc.vector.tensor_tensor(m.s(INT), m.s(INT), m.s(TA), ALU.add)
        if it == 0:
            nc.vector.tensor_tensor(m.s(VEL), m.s(ACCV), m.s(HALT), ALU.mult)

    run_block(nc, f"step{it}", {"tensor": tensor, "vector": vector, "scalar": scalar})


def l1_refine(nc, m, out_dram, b):
    H0, RES, OUT = 15, 17, 18

    def tensor(pe, S):
        for k in range(2):
            nc.tensor.matmul(m.ps[k][:, :], m.W("r1")[:, 128 * k:128 * k + 128], m.s(INT), start=True, stop=True).then_inc(S["hid"], 1)
        for k in range(2):
            pe.wait_ge(S["gelu"], k + 1)
            last = nc.tensor.matmul(m.ps[2][:, :], m.W("r2")[:, 128 * k:128 * k + 128], m.s(H0 + k), start=(k == 0), stop=(k == 1))
        last.then_inc(S["refined"], 1)

    def scalar(a, S):
        for k in range(2):
            a.wait_ge(S["hid"], k + 1)
            nc.scalar.activation(m.s(H0 + k), m.ps[k][:, :], ACT.Gelu, bias=m.W("r1b")[:, k:k + 1]).then_inc(S["gelu"], 1)

    def vector(v, S):
        nc.vector.tensor_tensor(m.s(RES), m.x[:, :], m.h, ALU.add).then_inc(S["res"], 1)
        v.wait_ge(S["refined"], 1)
        nc.vector.tensor_scalar(m.s(OUT), m.ps[2][:, :], m.W("r2b"), m.W("iw"), ALU.add, ALU.mult).then_inc(S["scaled"], 1)
        v.wait_ge(S["scaled"], 1)
        v.wait_ge(S["res"], 1)
        nc.vector.tensor_tensor(m.x[:, :], m.s(OUT), m.s(RES), ALU.add).then_inc(S["done"], 1)

    def sync(sp, S):
        sp.wait_ge(S["done"], 1)
        sp.dma_start(out_dram[bass.ds(b, 1), :, :].rearrange("o c t -> (o c) t"), m.x[:, :]).then_inc(S["stored"], 16)
        sp.wait_ge(S["stored"], 16)

    run_block(nc, "refine", {"tensor": tensor, "vector": vector, "scalar": scalar, "sync": sync})


def build(nc, d, out):
    with ExitStack() as ctx:
        m = Mem(nc, ctx)
        setup(nc, m, d)
        with nc.Fori(0, B) as b:
            l0_inputs(nc, m, d["x"], b)
            l0_delta(nc, m)
            l0_gate(nc, m)
            l0_ffn(nc, m)
            l1_inputs(nc, m)
            l1_core(nc, m)
            l1_output(nc, m)
            l1_route(nc, m)
            l1_iterate(nc, m, 0)
            l1_iterate(nc, m, 1)
            l1_refine(nc, m, out, b)


def lay_out(inputs, np):
    g = {k: np.asarray(v) for k, v in inputs.items()}
    A = lambda n: g["L0_attn_" + n]
    F = lambda n: g["L0_ffn_" + n]
    C = lambda n: g["L1_attn_" + n]
    E = lambda n: g["L1_ffn_" + n]
    z = lambda *s: np.zeros(s, np.float32)
    rows = lambda a: np.tile(np.reshape(a, (1, -1)), (128, 1))
    cols = lambda a: np.reshape(a, (-1, 128)).T
    w = {}
    w["Wb"] = np.repeat(A("Wb"), 32, axis=1)
    w["fir_s"] = A("fir_short_w").reshape(128, FIR_S)
    w["fir_l"] = A("fir_long_w").reshape(128, FIR_L)
    w["W1x"] = A("mlp_w1")[:128]
    t = z(128, 4, 128)
    for h in range(4):
        for s in range(4):
            for k in range(4):
                t[32 * k + 4 * s + h, h] = A("mlp_w1")[128 + 4 * s + k]
    w["W1s"] = t
    w["b1"], w["W2"], w["b2"] = A("mlp_b1"), A("mlp_w2"), rows(A("mlp_b2"))
    w["temp"], w["res"], w["rms"] = rows(A("logit_temp")), rows(A("conv_res_logit")), np.tile(A("rms_w"), 4)
    w["Wo"] = A("Wo")
    w["Wvf"], w["mur"], w["muk"] = F("W_v").T, F("mu_r"), F("mu_k")
    w["inp"] = C("in_proj_w").T
    both = lambda a, b: np.stack([C(a), C(b)])
    w["mconv"] = both("conv1d_w", "conv1db_w").reshape(2, 2, 128, 4).transpose(2, 0, 1, 3)
    w["mconvb"] = cols(both("conv1d_bias", "conv1db_bias"))
    xp, dp = both("x_proj_w", "x_projb_w"), both("dt_proj_w", "dt_projb_w")
    t, u = z(128, 2, 2, 128), z(128, 2, 2, 128)
    for e in range(2):
        for k in range(2):
            t[:, e, k, 0:32] = xp[e, 64:96, 128 * k:128 * k + 128].T
            t[:, e, k, 64:128] = xp[e, 0:64, 128 * k:128 * k + 128].T
            u[64:128, e, k] = dp[e, 128 * k:128 * k + 128].T
    w["xproj"], w["dtproj"] = t, u
    w["dtb"] = cols(both("dt_proj_b", "dt_projb_b"))
    w["Alog"] = both("A_log", "A_b_log").reshape(2, 2, 128, 16).transpose(2, 0, 1, 3)
    w["Dp"] = cols(both("D", "D_b"))
    w["outp"] = C("out_proj_w").T.reshape(2, 128, 128).transpose(1, 0, 2)
    w["fftb"] = cols(C("fft_conv_b"))
    w["iw"], w["mu"] = E("integration_weight"), E("mu")
    t, u = z(128, 2, 128), z(128)
    t[:, 0, 0:64], t[:, 1, 0:64] = E("shared_w1")[:128], E("shared_w1")[128:]
    t[:, 0, 64:96], t[:, 0, 96:128] = E("halt_w1"), E("router_w1")
    u[0:64], u[64:96], u[96:128] = E("shared_b1"), E("halt_b1"), E("router_b1")
    w["m1"], w["m1b"] = t, u
    t = z(128, 8)
    t[96:128] = E("router_w2")
    w["rw2"], w["rb2"] = t, rows(E("router_b2"))
    t = z(128, 128)
    t[64:96] = np.tile(E("halt_w2"), (1, 128))
    w["hw2"], w["hb2"] = t, rows(E("halt_b2"))
    w["e1"] = E("expert_w1").reshape(8, 2, 128, 64).transpose(2, 1, 0, 3)
    w["e1b"] = E("expert_b1").reshape(4, 128).T
    w["e2"] = E("expert_w2").reshape(4, 128, 384).transpose(1, 0, 2)
    t = z(128, 2, 384)
    t[0:8, 0], t[8:16, 1] = E("expert_b2"), E("expert_b2")
    w["e2b"] = t
    t = z(128, 384)
    t[0:64] = E("shared_w2")
    w["s2"], w["s2b"], w["sw"] = t, cols(E("shared_b2")), rows(E("shared_weight"))
    w["r1"], w["r1b"] = E("refine_w1"), cols(E("refine_b1"))
    w["r2"], w["r2b"] = E("refine_w2").reshape(2, 128, 128).transpose(1, 0, 2), E("refine_b2")
    for name, c in WEIGHTS:
        assert w[name].size == 128 * c, (name, w[name].shape)
    arrays = {"w": np.concatenate([w[name].reshape(128, -1) for name, _ in WEIGHTS], 1)}
    arrays["prep"] = np.concatenate([A("Wq"), A("Wk"), A("Wv"), F("W_r").T, F("W_k").T], 1)
    arrays["taps"] = np.concatenate([rows(A("conv_w_" + n).T) for n in "qkv"], 1)
    arrays["fw"] = C("fft_conv_w").transpose(2, 1, 0).reshape(TAPS, 4, 128, 512).transpose(2, 0, 1, 3).reshape(128, -1)
    arrays["x"] = A("hidden_states").transpose(0, 2, 1)
    arrays["tab"] = np.concatenate(list(shape_tables().values()), 1)
    arrays["sel"] = selector_tables()
    arrays["time"], arrays["fwd"], arrays["inv"] = dft_tables()
    return {k: np.ascontiguousarray(v) for k, v in arrays.items()}


def kernel(**inputs):
    import numpy as _np
    import concourse.bacc as _bacc
    from concourse import mybir as _mybir
    from concourse.bass_utils import run_bass_kernel_spmd as _run

    nc = _bacc.Bacc("TRN2", target_bir_lowering=False, num_devices=1, dynamic_dma_scratch_size=1024)
    arrays, d = {}, {}
    for name, a in lay_out(inputs, _np).items():
        arrays[f"in_{name}_dram"] = a
        d[name] = nc.dram_tensor(f"in_{name}_dram", a.shape, _mybir.dt.from_np(a.dtype), kind="ExternalInput").ap()
    out = nc.dram_tensor("out_0_dram", (B, D, L), F32, kind="ExternalOutput").ap()
    build(nc, d, out)
    r = _run(nc, [arrays], core_ids=[0])
    return r.results[0]["out_0_dram"].transpose(0, 2, 1)
```

```python
import concourse.bass as bass
from concourse import mybir
from contextlib import ExitStack
import numpy as np

F32 = mybir.dt.float32
BF16 = mybir.dt.bfloat16
ALU = mybir.AluOpType
ACT = mybir.ActivationFunctionType
AXX = mybir.AxisListType.X

B, L, D = 8, 512, 128
H, DK, CH = 4, 32, 32
NCH = L // CH
FIR_S, FIR_L = 5, 64
NS = 16
NT = L // 128
TAPS = 5
NE, HE = 8, 64
PAD = 4
DWORK = 39
SP_CAP = 40.0


def shape_tables():
    p = np.arange(128)
    blk = (p[:, None] // 32 == p[None, :] // 32).astype(np.float32)
    i, j = p[:, None] % 32, np.arange(32)[None, :]
    t = {"ident": np.eye(128), "ones_mean": np.full((128, 128), 1 / 128), "head_ones": blk, "head_mean": blk / 32,
         "neg_blk": -blk, "ident_st": (i == j)}
    for s in (1, 2, 4, 8):
        off = ((i // (2 * s) == j // (2 * s)) & (i // s % 2 == 1) & (j // s % 2 == 0)).astype(np.float32)
        t["neg_level1" if s == 1 else f"level{s}"] = -off if s == 1 else off
    t["row_low"], t["row_high"] = (p % 32 < 16), (p % 32 >= 16)
    t["causal_bd"] = (blk.reshape(128, 4, 32) * (i <= j)[:, None, :]).reshape(128, 128)
    sel = np.zeros((128, 4, 16))
    for s in range(4):
        for h in range(4):
            sel[32 * h:32 * h + 32, s, 4 * s + h] = 1 / 32
    t["stat_sel"] = sel.reshape(128, 64)
    prob = np.zeros((128, 4, 128))
    for h in range(4):
        for k in range(4):
            prob[4 * h + k, k, 32 * h:32 * h + 32] = 1
    t["prob_sel"] = prob.reshape(128, 512)
    t["floor"] = np.tile(np.array([0.08, 0.08, 0, 0]), (128, 4))
    t["dec"] = np.tile(np.arange(8, 0, -1.0), (128, 1))
    wsel = np.zeros((128, 2, 128))
    wsel[16, 0], wsel[17, 1] = 1, 1
    t["wsel"] = wsel.reshape(128, 256)
    return {k: np.asarray(v, np.float32).reshape(128, -1) for k, v in t.items()}


def selector_tables():
    s = np.zeros((128, 32, 128), np.float32)
    for n in range(32):
        s[[n, 32 + n, 64 + n], n] = 1
    m = np.zeros((128, 2, 4, 128), np.float32)
    for r in range(2):
        for t in range(4):
            for e in range(2):
                m[8 * r + 2 * t + e, r, t, 64 * e:64 * e + 64] = 1
    return np.concatenate([s.reshape(128, -1), m.reshape(128, -1)], 1)


def dft_tables():
    k = np.arange(L)
    a = 2 * np.pi * ((k[:, None] * k[None]) % L) / L
    time = np.stack([np.cos(a), np.sin(a)]).reshape(2, NT, 128, L).transpose(2, 0, 1, 3)
    k = np.arange(256)
    a = 2 * np.pi * ((k[:, None] * k[None]) % 256) / 256
    c, s = np.cos(a), np.sin(a)
    fwd = np.block([[c, s], [-s, c]])
    inv = np.block([[c, s], [-s, c]]) / (256 * L)
    lay = lambda m: m.reshape(4, 128, 512).transpose(1, 0, 2)
    return (np.ascontiguousarray(time.reshape(128, -1), np.float32),
            np.ascontiguousarray(lay(fwd).reshape(128, -1), np.float32),
            np.ascontiguousarray(lay(inv).reshape(128, -1), np.float32))


WEIGHTS = [
    ("Wb", 128), ("fir_s", 5), ("fir_l", 64),
    ("W1x", 128), ("W1s", 512), ("b1", 1), ("W2", 4), ("b2", 4), ("temp", 1), ("res", 4), ("rms", 1), ("Wo", 128),
    ("Wvf", 128), ("mur", 1), ("muk", 1),
    ("inp", 512), ("mconv", 16), ("mconvb", 4), ("xproj", 512), ("dtproj", 512), ("dtb", 4), ("Alog", 64), ("Dp", 4),
    ("outp", 256), ("fftb", 4),
    ("iw", 1), ("mu", 1), ("m1", 256), ("m1b", 1), ("rw2", 8), ("rb2", 8), ("hw2", 128), ("hb2", 1),
    ("e1", 1024), ("e1b", 4), ("e2", 1536), ("e2b", 768), ("s2", 384), ("s2b", 3), ("sw", 1),
    ("r1", 256), ("r1b", 2), ("r2", 256), ("r2b", 1),
]
WAT, _n = {}, 0
for _name, _c in WEIGHTS:
    WAT[_name] = (_n, _c)
    _n += _c
WCOLS = _n
TAT, _n = {}, 0
for _name, _v in shape_tables().items():
    TAT[_name] = (_n, _v.shape[1])
    _n += _v.shape[1]
TCOLS = _n


class Sems(dict):

    def __init__(self, nc, stack, stage):
        self.nc, self.stack, self.stage = nc, stack, stage

    def __missing__(self, name):
        self[name] = self.stack.enter_context(self.nc.semaphore(f"{self.stage}_{name}"))
        return self[name]


def linker(eng, sem):
    n = [0]

    def link(ins):
        n[0] += 1
        ins.then_inc(sem, 1)
        eng.wait_ge(sem, n[0])
    return link


class Mem:

    def __init__(self, nc, ctx):
        sb = lambda n, s, d=F32: ctx.enter_context(nc.sbuf_tensor(n, s, d))
        self.w = sb("weights", [128, WCOLS])
        self.t = sb("tables", [128, TCOLS])
        self.sel = sb("selectors", [128, 40, 128], BF16)
        self.inv = sb("dft_chan_inv", [128, 4, 512])
        self.qkvw = sb("qkv_tap_w", [128, 3, 4, 128])
        self.mixw = sb("token_mix_w", [128, 4, 128])
        self.small = sb("small", [128, 128])
        self.x = sb("x", [128, L])
        self.hp = sb("h_padded", [128, PAD + L])
        self.xd = sb("x_experts", [128, L])
        self.hd = sb("h_experts", [128, L])
        self.work = sb("work", [128, 70, L])
        self.dft = self.work[:, DWORK:DWORK + 8, :].rearrange("p (a t) n -> p a t n", a=2)
        self.fw = self.work[:, DWORK + 8:DWORK + 28, :].rearrange("p (t k) n -> p t k n", t=TAPS)
        self.ps = [ctx.enter_context(nc.psum_tensor(f"ps{i}", [128, 512], F32)) for i in range(8)]

    def W(self, name):
        a, n = WAT[name]
        return self.w[:, a:a + n]

    def T(self, name):
        a, n = TAT[name]
        return self.t[:, a:a + n]

    def s(self, i):
        return self.work[:, i, :]

    @property
    def h(self):
        return self.hp[:, PAD:PAD + L]


SM = {"temp": 0, "res": 1, "pconst": 5, "sw": 21, "omsw": 22, "A": 23, "one_mu_r": 87, "one_mu_k": 88, "tmp": 89}


ENGINES = ("sync", "tensor", "vector", "scalar", "gpsimd")


def emit(eng, parts):
    due = [(next(p, None), i, p) for i, p in enumerate(parts)]
    due = [x for x in due if x[0] is not None]
    while due:
        _, i, p = due.pop(due.index(min(due, key=lambda x: x[:2])))
        t = next(p, None)
        if t is not None:
            due.append((t, i, p))


def run_block(nc, *streams):
    with ExitStack() as st:
        sems = [Sems(nc, st, name) for name, _ in streams]

        def parts(engine, eng):
            return [progs[engine](eng, S) for (_, progs), S in zip(streams, sems) if engine in progs]

        with nc.Block() as block:
            for engine, open_ in (("sync", block.sync), ("tensor", block.tensor), ("vector", block.vector),
                                  ("scalar", block.scalar), ("gpsimd", block.gpsimd)):
                if any(engine in progs for _, progs in streams):
                    open_(lambda eng, engine=engine: emit(eng, parts(engine, eng)))
        nums = [x.num for S in sems for x in S.values()]
        nc.gpsimd.sem_clear(range(min(nums), max(nums) + 1))
        nc.all_engine_barrier()


def ln_tensor(nc, pe, S, m, x, scr, banks, loaded=0):
    if loaded:
        pe.wait_ge(S["x_loaded"], loaded)
    nc.tensor.matmul(m.ps[banks[0]][:, :], m.T("ones_mean"), x, start=True, stop=True).then_inc(S["ln_mean"], 1)
    pe.wait_ge(S["ln_squared"], 1)
    nc.tensor.matmul(m.ps[banks[1]][:, :], m.T("ones_mean"), m.s(scr[1]), start=True, stop=True).then_inc(S["ln_var"], 1)


def ln_vector(nc, v, S, m, x, h, scr, banks):
    v.wait_ge(S["ln_mean"], 1)
    nc.vector.tensor_tensor(m.s(scr[0]), x, m.ps[banks[0]][:, :], ALU.subtract).then_inc(S["ln_centred"], 1)
    v.wait_ge(S["ln_centred"], 1)
    v.wait_ge(S["ln_rstd"], 1)
    nc.vector.tensor_tensor(h, m.s(scr[0]), m.s(scr[2]), ALU.mult).then_inc(S["h_ready"], 1)


def ln_scalar(nc, a, S, m, scr, banks):
    a.wait_ge(S["ln_centred"], 1)
    nc.scalar.activation(m.s(scr[1]), m.s(scr[0]), ACT.Square).then_inc(S["ln_squared"], 1)
    a.wait_ge(S["ln_var"], 1)
    nc.scalar.activation(m.s(scr[2]), m.ps[banks[1]][:, :], ACT.Ln, bias=m.small[:, 120:121]).then_inc(S["ln_log"], 1)
    a.wait_ge(S["ln_log"], 1)
    nc.scalar.activation(m.s(scr[2]), m.s(scr[2]), ACT.Exp, scale=-0.5).then_inc(S["ln_rstd"], 1)


def setup(nc, m, d):
    raw = m.work[:, 0:20, :].rearrange("p (t k) n -> p t k n", t=TAPS)
    folded = m.fw
    fwd = m.work[:, 20:24, :]
    taps = m.work[:, 24:27, :]
    sel32 = m.work[:, 27:37, :]
    prep = m.work[:, 37:39, :].rearrange("p a n -> p (a n)")
    sm = m.small

    def sync(sp, S):
        yield 0
        sp.dma_start(m.w[:, :], d["w"]).then_inc(S["weights"], 16)
        sp.dma_start(m.t[:, :], d["tab"]).then_inc(S["weights"], 16)
        sp.dma_start(taps, d["taps"].rearrange("p (a n) -> p a n", a=3)).then_inc(S["weights"], 16)
        sp.dma_start(prep[:, 0:640], d["prep"]).then_inc(S["weights"], 16)
        sp.dma_start(sel32, d["sel"].rearrange("p (a n) -> p a n", a=10)).then_inc(S["selectors"], 16)
        sp.dma_start(fwd, d["fwd"].rearrange("p (a n) -> p a n", a=4)).then_inc(S["freq"], 16)
        sp.dma_start(raw, d["fw"].rearrange("p (t k n) -> p t k n", t=TAPS, k=4)).then_inc(S["freq"], 16)
        sp.dma_start(m.inv[:, :, :], d["inv"].rearrange("p (a n) -> p a n", a=4)).then_inc(S["dft"], 16)
        sp.wait_ge(S["dft"], 16)
        for t in range(TAPS):
            sp.wait_ge(S["folded_copied"], 4 * t + 4)
            sp.dma_start(d["folded"][:, 2048 * t:2048 * t + 2048].rearrange("p (k n) -> p k n", k=4), folded[:, t, :, :]).then_inc(S["stored"], 16)
        sp.wait_ge(S["stored"], 16 * TAPS)

    def tensor(pe, S):
        yield 0
        pe.wait_ge(S["freq"], 32)
        n = 0
        for t in range(TAPS):
            for yc in range(4):
                if n >= 4:
                    pe.wait_ge(S["folded_copied"], n - 3)
                for j in range(4):
                    last = nc.tensor.matmul(m.ps[n % 4][:, :], fwd[:, j, 128 * yc:128 * yc + 128], raw[:, t, j, :],
                                            start=(j == 0), stop=(j == 3))
                last.then_inc(S["folded"], 1)
                n += 1

    def vector(v, S):
        yield 0
        link = linker(v, S["chain"])
        link(nc.vector.memset(m.hp[:, 0:PAD], 0.0))
        link(nc.vector.memset(sm[:, 119:128], 0.0))
        link(nc.vector.memset(sm[:, 120:121], 1e-5))
        link(nc.vector.memset(sm[:, 121:122], 1e-12))
        link(nc.vector.memset(sm[:, 122:123], 1.0))
        v.wait_ge(S["weights"], 64)
        for p in range(3):
            for j in range(4):
                nc.vector.tensor_tensor(m.qkvw[:, p, j, :], prep[:, 128 * p:128 * p + 128], taps[:, p, 128 * j:128 * j + 128], ALU.mult)
        for i, (w, mu, one_mu) in enumerate(((prep[:, 384:512], "mur", "one_mu_r"), (prep[:, 512:640], "muk", "one_mu_k"))):
            c = SM[one_mu]
            nc.vector.tensor_scalar(m.mixw[:, 2 * i, :], w, m.W(mu)[:, 0:1], None, ALU.mult)
            link(nc.vector.tensor_scalar(sm[:, c:c + 1], m.W(mu)[:, 0:1], -1.0, 1.0, ALU.mult, ALU.add))
            nc.vector.tensor_scalar(m.mixw[:, 2 * i + 1, :], w, sm[:, c:c + 1], None, ALU.mult)
        link(nc.vector.tensor_scalar(sm[:, 89:90], m.W("temp"), SP_CAP, None, ALU.min))
        nc.vector.tensor_scalar(sm[:, 90:91], m.W("temp"), 1.0, None, ALU.mult).then_inc(S["sp_in"], 1)
        v.wait_ge(S["exps"], 6)
        link(nc.vector.tensor_tensor(sm[:, 92:93], m.W("temp"), sm[:, 91:92], ALU.max))
        link(nc.vector.tensor_scalar(sm[:, 92:93], sm[:, 92:93], 1e-6, None, ALU.add))
        link(nc.vector.reciprocal(sm[:, 0:1], sm[:, 92:93]))
        link(nc.vector.tensor_scalar(sm[:, 93:98], sm[:, 93:98], 1.0, None, ALU.add))
        link(nc.vector.reciprocal(sm[:, 93:98], sm[:, 93:98]))
        link(nc.vector.tensor_copy(sm[:, 1:5], sm[:, 93:97]))
        link(nc.vector.tensor_copy(sm[:, 21:22], sm[:, 97:98]))
        link(nc.vector.tensor_scalar(sm[:, 22:23], sm[:, 21:22], -1.0, 1.0, ALU.mult, ALU.add))
        link(nc.vector.tensor_copy(sm[:, 5:21], m.T("floor")))
        pc = sm[:, 5:21].rearrange("p (h k) -> p h k", k=4)[:, :, 0]
        link(nc.vector.tensor_tensor(pc, pc, sm[:, 1:5], ALU.add))
        link(nc.vector.tensor_scalar(sm[:, 23:87], sm[:, 23:87], -1.0, None, ALU.mult))
        v.wait_ge(S["selectors"], 16)
        nc.vector.tensor_copy(m.sel[:, :, :].rearrange("p a n -> p (a n)"), sel32.rearrange("p a n -> p (a n)"))
        for n in range(20):
            v.wait_ge(S["folded"], n + 1)
            nc.vector.tensor_copy(folded[:, n // 4, n % 4, :], m.ps[n % 4][:, :]).then_inc(S["folded_copied"], 1)

    def scalar(a, S):
        yield 0
        a.wait_ge(S["sp_in"], 1)
        nc.scalar.activation(sm[:, 90:91], sm[:, 89:90], ACT.Exp).then_inc(S["exps"], 1)
        nc.scalar.activation(sm[:, 93:97], m.W("res"), ACT.Exp, scale=-1.0).then_inc(S["exps"], 1)
        nc.scalar.activation(sm[:, 97:98], m.W("sw"), ACT.Exp, scale=-1.0).then_inc(S["exps"], 1)
        nc.scalar.activation(sm[:, 23:87], m.W("Alog"), ACT.Exp).then_inc(S["exps"], 1)
        a.wait_ge(S["exps"], 4)
        nc.scalar.activation(sm[:, 91:92], sm[:, 90:91], ACT.Ln, bias=sm[:, 122:123]).then_inc(S["exps"], 2)

    return "setup", {"sync": sync, "tensor": tensor, "vector": vector, "scalar": scalar}


QN, KN, KB, VS, VB, BETA = 3, 4, 5, 6, 8, 9
RQ, RK, KBT, VT, KT = 10, 13, 11, 12, 13
KBD, GBD, KTBD, ATTBD = 15, 19, 23, 27
NATBD, XTBD = 31, 35
PTBD, ATT_ST = 15, 19
XST, ZST, XTST, ST_ALL, WST = 0, 1, 2, 4, 10
AU = 10
XR_ST, WU_ST = 0, 9
SHORT, DELTA, FL = 8, 5, 14


def bd(m, slot):
    return m.work[:, slot:slot + 4, :].rearrange("p a n -> p (a n)").rearrange("p (c h t) -> p c h t", c=NCH, h=H)


def spread(ap2d):
    return ap2d.rearrange("p (c t) -> p c t", t=32).unsqueeze(2).to_broadcast([128, NCH, H, 32])


def over_chunks(mask):
    return mask.rearrange("p (h t) -> p h t", h=H).unsqueeze(1).to_broadcast([128, NCH, H, 32])


def st_over_chunks(mask):
    return mask.unsqueeze(1).to_broadcast([128, NCH, 32])


def l0_inputs(nc, m, x_dram, b):
    vs = m.work[:, VS:VS + 2, :].rearrange("p a n -> p (a n)")[:, 64:64 + L]

    def sync(sp, S):
        yield 0
        sp.dma_start(m.x[:, :], x_dram[bass.ds(b, 1), :, :].rearrange("o c t -> (o c) t")).then_inc(S["x_loaded"], 16)

    def tensor(pe, S):
        yield 0
        ln_tensor(nc, pe, S, m, m.x[:, :], (0, 1, 2), (0, 1), loaded=16)
        pe.wait_ge(S["h_ready"], 1)
        for p in range(3):
            for j in range(4):
                last = nc.tensor.matmul(m.ps[2 + p][:, :], m.qkvw[:, p, j, :], m.hp[:, PAD - 3 + j:PAD - 3 + j + L],
                                        start=(j == 0), stop=(j == 3))
            last.then_inc(S["qkv"], 1)
        nc.tensor.matmul(m.ps[0][:, :], m.W("Wb"), m.h, start=True, stop=True).then_inc(S["qkv"], 1)
        yield 18
        for i, slot in enumerate((0, 1)):
            pe.wait_ge(S["squares"], i + 1)
            nc.tensor.matmul(m.ps[1 + i][:, :], m.T("head_ones"), m.s(slot), start=True, stop=True).then_inc(S["norms"], 1)

    def scalar(a, S):
        yield 0
        ln_scalar(nc, a, S, m, (0, 1, 2), (0, 1))
        yield 12
        for p, out in enumerate((m.s(QN), m.s(KN), vs)):
            a.wait_ge(S["qkv"], p + 1)
            nc.scalar.activation(out, m.ps[2 + p][:, :], ACT.Silu).then_inc(S["silu"], 1)
        a.wait_ge(S["qkv"], 4)
        nc.scalar.activation(m.s(BETA), m.ps[0][:, :], ACT.Tanh, scale=0.5).then_inc(S["tanh"], 1)
        a.wait_ge(S["silu"], 2)
        a.wait_ge(S["h_ready"], 1)
        nc.scalar.activation(m.s(0), m.s(QN), ACT.Square).then_inc(S["squares"], 1)
        nc.scalar.activation(m.s(1), m.s(KN), ACT.Square).then_inc(S["squares"], 1)
        yield 18
        for i, slot in enumerate((RQ, RK)):
            a.wait_ge(S["norms"], i + 1)
            nc.scalar.activation(m.s(slot), m.ps[1 + i][:, :], ACT.Ln, bias=m.small[:, 121:122]).then_inc(S["logs"], 1)
        for i, slot in enumerate((RQ, RK)):
            a.wait_ge(S["logs"], i + 1)
            nc.scalar.activation(m.s(slot), m.s(slot), ACT.Exp, scale=-0.5).then_inc(S["rnorm"], 1)

    def vector(v, S):
        yield 0
        ln_vector(nc, v, S, m, m.x[:, :], m.h, (0, 1, 2), (0, 1))
        link = linker(v, S["chain"])
        nc.vector.memset(m.work[:, VS, 0:64], 0.0)
        yield 12
        v.wait_ge(S["tanh"], 1)
        link(nc.vector.tensor_scalar(m.s(BETA), m.s(BETA), 0.5, 0.5, ALU.mult, ALU.add))
        v.wait_ge(S["silu"], 3)
        link(nc.vector.tensor_tensor(m.s(VB), vs, m.s(BETA), ALU.mult))
        nc.vector.transpose(m.s(VT), m.s(VB))
        yield 18
        v.wait_ge(S["rnorm"], 1)
        v.wait_ge(S["squares"], 2)
        nc.vector.tensor_tensor(m.s(QN), m.s(QN), m.s(RQ), ALU.mult).then_inc(S["qn"], 1)
        v.wait_ge(S["rnorm"], 2)
        link(nc.vector.tensor_tensor(m.s(KN), m.s(KN), m.s(RK), ALU.mult))
        link(nc.vector.tensor_tensor(m.s(KB), m.s(KN), m.s(BETA), ALU.mult))
        nc.vector.transpose(m.s(KT), m.s(KN))
        nc.vector.transpose(m.s(KBT), m.s(KB))
        nc.vector.tensor_tensor(bd(m, KBD), spread(m.s(KN)), over_chunks(m.T("head_ones")), ALU.mult)

    return "qkv", {"sync": sync, "tensor": tensor, "vector": vector, "scalar": scalar}


def l0_delta(nc, m):
    vp = m.work[:, VS:VS + 2, :].rearrange("p a n -> p (a n)")
    cols = lambda n: slice(32 * n, 32 * n + 32)
    GRP = NCH // 2
    gcol = lambda g: slice(256 * g, 256 * g + 256)
    chunks = lambda g: range(GRP * g, GRP * g + GRP)
    GRAM_PS, Z_PS, Y_PS = (0, 1), (2, 3), (4, 0)
    XR_PS, AXR_PS, WU_PS, KWU_PS, AWU_PS = (1, 0), (2, 3), (4, 0), (1, 2), (3, 4)
    CHAIN_PS, GS_PS = 0, 3
    LEVELS = (2, 4, 8)
    T_LEVEL, T_XR, T_AXR, T_WU, T_KWU = [12 + 14 * i for i in range(3)], 54, 62, 70, 78
    T_CHAIN = [92 + 2.5 * n for n in range(NCH)]
    T_O = 132
    flat = lambda slot, n: bd(m, slot)[:, n, :, :].rearrange("p h t -> p (h t)")
    ch = lambda ap: ap.rearrange("p (c t) -> p c t", t=32)
    gmask = lambda name: m.T(name).unsqueeze(1).to_broadcast([128, GRP, 32])
    state = lambda n: m.s(ST_ALL)[:, cols(n)]
    halves = lambda bank: m.ps[bank][:, :].rearrange("p (a t) -> p a t", a=2)
    both = lambda bank, n: halves(bank)[:, :, cols(n % GRP)]
    QK = m.work[:, QN:KB + 1:KB - QN, :]
    R = m.work[:, KBT:KBT + 2, :]
    XR = m.work[:, XR_ST:XR_ST + 2, :]
    WU = m.work[:, WU_ST:WU_ST + 2, :]
    low, high = m.T("row_low")[:, 0:1], m.T("row_high")[:, 0:1]

    def expand(src, dst, g, h0, h1, mask):
        out = bd(m, dst)[:, GRP * g:GRP * g + GRP, h0:h1, :]
        return out, ch(src).unsqueeze(2).to_broadcast([128, GRP, h1 - h0, 32]), \
            m.T(mask).rearrange("p (h t) -> p h t", h=H)[:, h0:h1, :].unsqueeze(1).to_broadcast([128, GRP, h1 - h0, 32])

    def tensor(pe, S):
        yield 0

        def stacked(bank, slot, rhs, g):
            for n in chunks(g):
                last = nc.tensor.matmul(m.ps[bank][:, cols(n)], flat(slot, n), rhs[:, cols(n)], start=True, stop=True)
            return last

        def paired(bank, slot, rhs, g):
            for n in chunks(g):
                last = nc.tensor.matmul(both(bank, n), flat(slot, n), rhs[:, :, cols(n)], start=True, stop=True)
            return last

        for g in range(2):
            paired(GRAM_PS[g], KBD, QK, g).then_inc(S["gram"], 1)
        for i in range(len(LEVELS)):
            yield T_LEVEL[i]
            for g in range(2):
                pe.wait_ge(S["xt_dve"], 2 * i + g + 1)
                pe.wait_ge(S["xt_act"], 2 * i + g + 1)
                stacked(Z_PS[g], NATBD, m.s(XST), g).then_inc(S["z"], 1)
            yield T_LEVEL[i] + 7
            for g in range(2):
                pe.wait_ge(S["z_plus"], 2 * i + g + 1)
                if i == 0 and g == 1:
                    pe.wait_ge(S["att_sb"], 1)
                stacked(Y_PS[g], XTBD, m.s(ZST), g).then_inc(S["y"], 1)
        yield T_XR
        pe.wait_ge(S["att_sb"], 2)
        for g in range(2):
            pe.wait_ge(S["xt_dve"], 2 * len(LEVELS) + g + 1)
            pe.wait_ge(S["xt_act"], 2 * len(LEVELS) + g + 1)
            paired(XR_PS[g], XTBD, R, g).then_inc(S["xr"], 1)
        yield T_AXR
        for g in range(2):
            pe.wait_ge(S["xr_sb"], g + 1)
            paired(AXR_PS[g], NATBD, XR, g).then_inc(S["axr"], 1)
        yield T_WU
        for g in range(2):
            pe.wait_ge(S["rest"], g + 1)
            paired(WU_PS[g], XTBD, R, g).then_inc(S["wu"], 1)
        yield T_KWU
        pe.wait_ge(S["kt_bd"], 1)
        pe.wait_ge(S["attn_bd"], 1)
        for g in range(2):
            pe.wait_ge(S["wu_sb"], g + 1)
            paired(KWU_PS[g], KTBD, WU, g).then_inc(S["kwu"], 1)
        for g in range(2):
            paired(AWU_PS[g], ATTBD, WU, g).then_inc(S["awu"], 1)
        pe.wait_ge(S["ku_sb"], 1)
        pe.wait_ge(S["pt_dve"], 2)
        pe.wait_ge(S["pt_act"], 2)
        for n in range(1, NCH):
            yield T_CHAIN[n]
            if n > 1:
                pe.wait_ge(S["state"], n - 1)
            if n < NCH - 1:
                nc.tensor.matmul(m.ps[CHAIN_PS][:, cols(n)], flat(PTBD, n), state(n), start=True, stop=True).then_inc(S["chain"], 1)
            if n == 1:
                pe.wait_ge(S["au_sb"], 1)
            if n in (1, GRP):
                pe.wait_ge(S["g_bd"], n // GRP + 1)
            last = nc.tensor.matmul(m.ps[GS_PS][:, cols(n)], flat(GBD, n), state(n), start=True, stop=True)
        last.then_inc(S["o"], 1)

    def vector(v, S):
        yield 0
        link = linker(v, S["link"])
        taps = [(m.s(SHORT), vp[:, 64 - (FIR_S - 1) + k:64 - (FIR_S - 1) + k + L], m.W("fir_s")[:, k:k + 1], k == 0) for k in range(FIR_S)] + \
            [(m.s(FL), vp[:, 64 - (FIR_L - 1) + k:64 - (FIR_L - 1) + k + L], m.W("fir_l")[:, k:k + 1], k == 0) for k in range(FIR_L)]
        done = [0]

        def fir_tap(k):
            for acc, src, w, first in taps[done[0]:done[0] + k]:
                if first:
                    nc.vector.tensor_scalar(acc, src, w, None, ALU.mult).then_inc(S["fir_acc"], 1)
                else:
                    v.wait_ge(S["fir_acc"], done[0])
                    nc.vector.scalar_tensor_tensor(acc, src, w, acc, ALU.mult, ALU.add).then_inc(S["fir_acc"], 1)
                done[0] += 1

        fir_tap(6)
        for g in range(2):
            gc = gcol(g)
            v.wait_ge(S["gram"], g + 1)
            kk = halves(GRAM_PS[g])[:, 1, :]
            nc.vector.tensor_tensor(*expand(kk, NATBD, g, 0, H, "neg_blk"), ALU.mult)
            link(nc.vector.transpose(m.s(ZST)[:, gc], kk))
            link(nc.vector.tensor_tensor(ch(m.s(ZST)[:, gc]), ch(m.s(ZST)[:, gc]), gmask("neg_level1"), ALU.mult))
            link(nc.vector.tensor_tensor(ch(m.s(XST)[:, gc]), ch(m.s(ZST)[:, gc]), gmask("ident_st"), ALU.add))
            nc.vector.transpose(m.s(XTST)[:, gc], m.s(XST)[:, gc]).then_inc(S["xt"], 1)
            v.wait_ge(S["xt"], g + 1)
            nc.vector.tensor_tensor(*expand(m.s(XTST)[:, gc], XTBD, g, 0, 2, "head_ones"), ALU.mult).then_inc(S["xt_dve"], 1)
        for i, s in enumerate(LEVELS):
            yield T_LEVEL[i]
            fir_tap(4)
            for g in range(2):
                gc = gcol(g)
                v.wait_ge(S["z"], 2 * i + g + 1)
                link(nc.vector.tensor_tensor(ch(m.s(WST)[:, gc]), ch(m.ps[Z_PS[g]][:, gc]), gmask(f"level{s}"), ALU.mult))
                nc.vector.tensor_tensor(ch(m.s(ZST)[:, gc]), ch(m.s(WST)[:, gc]), gmask("ident_st"), ALU.add).then_inc(S["z_plus"], 1)
            yield T_LEVEL[i] + 7
            fir_tap(3)
            for g in range(2):
                gc = gcol(g)
                v.wait_ge(S["y"], 2 * i + g + 1)
                v.wait_ge(S["xt_act"], 2 * i + g + 1)
                nc.vector.transpose(m.s(XTST)[:, gc], m.ps[Y_PS[g]][:, gc]).then_inc(S["xt"], 1)
                if s < LEVELS[-1]:
                    nc.vector.tensor_copy(m.s(XST)[:, gc], m.ps[Y_PS[g]][:, gc])
                v.wait_ge(S["xt"], 2 * i + g + 3)
                nc.vector.tensor_tensor(*expand(m.s(XTST)[:, gc], XTBD, g, 0, 2, "head_ones"), ALU.mult).then_inc(S["xt_dve"], 1)
        yield T_XR
        fir_tap(7)
        yield T_AXR
        fir_tap(5)
        for g in range(2):
            v.wait_ge(S["axr"], g + 1)
            nc.vector.scalar_tensor_tensor(R[:, :, gcol(g)], halves(AXR_PS[g]), high, R[:, :, gcol(g)], ALU.mult, ALU.add).then_inc(S["rest"], 1)
        yield T_WU
        fir_tap(7)
        yield T_KWU
        fir_tap(5)
        for g in range(2):
            gc = gcol(g)
            v.wait_ge(S["kwu"], g + 1)
            link(nc.vector.transpose(m.s(XST)[:, gc], halves(KWU_PS[g])[:, 0, :]))
            nc.vector.scalar_tensor_tensor(ch(m.s(XTST)[:, gc]), ch(m.s(XST)[:, gc]), -1.0, gmask("ident_st"), ALU.mult, ALU.add).then_inc(S["pt"], 1)
            v.wait_ge(S["pt"], g + 1)
            nc.vector.tensor_tensor(*expand(m.s(XTST)[:, gc], PTBD, g, 0, 2, "head_ones"), ALU.mult).then_inc(S["pt_dve"], 1)
        for g in range(2):
            gc = gcol(g)
            v.wait_ge(S["awu"], g + 1)
            link(nc.vector.transpose(m.s(XST)[:, gc], halves(AWU_PS[g])[:, 0, :]))
            nc.vector.tensor_tensor(m.s(ZST)[:, gc], m.s(QN)[:, gc], m.s(XST)[:, gc], ALU.subtract).then_inc(S["g_st"], 1)
        for n in range(1, NCH - 1):
            yield T_CHAIN[n]
            if n in (1, GRP - 1):
                v.wait_ge(S["ku_sb"], n // (GRP - 1) + 1)
            v.wait_ge(S["chain"], n)
            nc.vector.tensor_tensor(state(n + 1), state(n + 1), m.ps[CHAIN_PS][:, cols(n)], ALU.add).then_inc(S["state"], 1)
            fir_tap(1)
        yield T_O
        fir_tap(len(taps))
        v.wait_ge(S["o"], 1)
        v.wait_ge(S["au_sb"], 2)
        link(nc.vector.tensor_tensor(m.s(AU)[:, 32:L], m.s(AU)[:, 32:L], m.ps[GS_PS][:, 32:L], ALU.add))
        nc.vector.transpose(m.s(DELTA), m.s(AU))

    def scalar(a, S):
        yield 0
        def expand_act(src, dst, g, sem):
            for h in (2, 3):
                last = nc.scalar.activation(bd(m, dst)[:, GRP * g:GRP * g + GRP, h, :], ch(src), ACT.Copy,
                                            scale=m.T("head_ones")[:, 32 * h:32 * h + 1])
            last.then_inc(sem, 1)

        for i in range(len(LEVELS) + 1):
            if i:
                yield T_LEVEL[i - 1] + 7
            for g in range(2):
                a.wait_ge(S["xt"], 2 * i + g + 1)
                if i:
                    a.wait_ge(S["y"], 2 * (i - 1) + g + 1)
                expand_act(m.s(XTST)[:, gcol(g)], XTBD, g, S["xt_act"])
                if i == 0:
                    nc.scalar.activation(m.s(ATT_ST)[:, gcol(g)], halves(GRAM_PS[g])[:, 0, :], ACT.Copy).then_inc(S["att_sb"], 1)
        yield T_AXR
        for g in range(2):
            a.wait_ge(S["xr"], g + 1)
            nc.scalar.activation(XR[:, :, gcol(g)], halves(XR_PS[g]), ACT.Copy, scale=low).then_inc(S["xr_sb"], 1)
        yield T_WU
        for g in range(2):
            a.wait_ge(S["wu"], g + 1)
            nc.scalar.activation(WU[:, :, gcol(g)], halves(WU_PS[g]), ACT.Copy).then_inc(S["wu_sb"], 1)
        yield T_KWU
        for g in range(2):
            a.wait_ge(S["pt"], g + 1)
            expand_act(m.s(XTST)[:, gcol(g)], PTBD, g, S["pt_act"])
            n0, n1 = GRP * g, min(GRP * g + GRP, NCH - 1)
            nc.scalar.activation(m.s(ST_ALL)[:, 32 * n0 + 32:32 * n1 + 32], halves(KWU_PS[g])[:, 1, 0:32 * (n1 - n0)], ACT.Copy).then_inc(S["ku_sb"], 1)
        for g in range(2):
            a.wait_ge(S["g_st"], g + 1)
            nc.scalar.activation(m.s(AU)[:, gcol(g)], halves(AWU_PS[g])[:, 1, :], ACT.Copy).then_inc(S["au_sb"], 1)

    def gpsimd(g_, S):
        yield 0
        nc.gpsimd.tensor_tensor(bd(m, KTBD), spread(m.s(KT)), over_chunks(m.T("head_ones")), ALU.mult).then_inc(S["kt_bd"], 1)
        g_.wait_ge(S["att_sb"], 2)
        nc.gpsimd.tensor_tensor(bd(m, ATTBD), spread(m.s(ATT_ST)), over_chunks(m.T("causal_bd")), ALU.mult).then_inc(S["attn_bd"], 1)
        yield T_KWU
        g_.wait_ge(S["attn_bd"], 1)
        for g in range(2):
            g_.wait_ge(S["g_st"], g + 1)
            nc.gpsimd.tensor_tensor(*expand(m.s(ZST)[:, gcol(g)], GBD, g, 0, H, "head_ones"), ALU.mult).then_inc(S["g_bd"], 1)

    return "delta", {"tensor": tensor, "vector": vector, "scalar": scalar, "gpsimd": gpsimd}


def l0_gate(nc, m):
    vs = m.work[:, VS:VS + 2, :].rearrange("p a n -> p (a n)")[:, 64:64 + L]
    streams = (m.s(SHORT), m.s(FL), m.s(DELTA), vs)
    ABS, SQ, ST, M2, HG = 15, 19, 23, 24, 25
    PRT, O, T1, T2 = 29, 30, 31, 32
    PB = (2, 3, 4, 0)
    tok = m.work[:, 33, :]
    lg, mx, pr = tok[:, 0:64], tok[:, 64:80], tok[:, 80:144]
    rs = tok[:, 144:160]
    j4 = lambda ap: ap.rearrange("p (g k) -> p g k", k=4)
    b16 = lambda ap: ap.unsqueeze(2).to_broadcast([128, 16, 4])

    def tensor(pe, S):
        yield 0
        sel = m.T("stat_sel")
        for s in range(4):
            nc.tensor.matmul(m.ps[0][0:16, :], sel[:, 16 * s:16 * s + 16], streams[s], start=(s == 0), stop=(s == 3))
        for s in range(4):
            pe.wait_ge(S["abs_sq"], 2 * s + 1)
            nc.tensor.matmul(m.ps[1][0:16, :], sel[:, 16 * s:16 * s + 16], m.s(ABS + s), start=(s == 0), stop=(s == 3))
            pe.wait_ge(S["abs_sq"], 2 * s + 2)
            last = nc.tensor.matmul(m.ps[2][0:16, :], sel[:, 16 * s:16 * s + 16], m.s(SQ + s), start=(s == 0), stop=(s == 3))
        last.then_inc(S["sums"], 1)
        yield 19
        pe.wait_ge(S["stats"], 4)
        for h in range(4):
            bank = m.ps[3 + h % 2]
            if h >= 2:
                pe.wait_ge(S["gelu"], h - 1)
            nc.tensor.matmul(bank[:, :], m.W("W1x"), m.h, start=True, stop=False)
            nc.tensor.matmul(bank[:, :], m.W("W1s")[:, 128 * h:128 * h + 128], m.s(ST), start=False, stop=True).then_inc(S["hid"], 1)
        for h in range(4):
            pe.wait_ge(S["gelu"], h + 1)
            for t in range(NT):
                c = 16 * t + 4 * h
                last = nc.tensor.matmul(m.ps[0][:, c:c + 4], m.s(HG + h)[:, 128 * t:128 * t + 128], m.W("W2"), start=True, stop=True)
        last.then_inc(S["logits"], 1)
        yield 30
        pe.wait_ge(S["probs"], 1)
        for t in range(NT):
            last = nc.tensor.transpose(m.ps[1][0:16, 128 * t:128 * t + 128], pr[:, 16 * t:16 * t + 16], m.T("ident"))
        last.then_inc(S["probs_t"], 1)
        pe.wait_ge(S["probs_sb"], 1)
        for k in range(4):
            nc.tensor.matmul(m.ps[PB[k]][:, :], m.T("prob_sel")[0:16, 128 * k:128 * k + 128], m.s(PRT)[0:16, :], start=True, stop=True).then_inc(S["prob_bc"], 1)
        pe.wait_ge(S["o_sq"], 1)
        nc.tensor.matmul(m.ps[1][:, :], m.T("head_mean"), m.s(T1), start=True, stop=True).then_inc(S["o_ms"], 1)
        pe.wait_ge(S["o_norm"], 1)
        nc.tensor.matmul(m.ps[2][:, :], m.W("Wo"), m.s(T2), start=True, stop=True).then_inc(S["proj"], 1)

    def scalar(a, S):
        yield 0
        for s in range(4):
            nc.scalar.activation(m.s(ABS + s), streams[s], ACT.Abs).then_inc(S["abs_sq"], 1)
            nc.scalar.activation(m.s(SQ + s), streams[s], ACT.Square).then_inc(S["abs_sq"], 1)
        a.wait_ge(S["sums"], 1)
        a.wait_ge(S["st_zero"], 1)
        nc.scalar.activation(m.s(M2)[0:16, :], m.ps[0][0:16, :], ACT.Square).then_inc(S["mean_sq"], 1)
        nc.scalar.activation(m.s(ST)[0:16, :], m.ps[0][0:16, :], ACT.Copy).then_inc(S["stats"], 1)
        nc.scalar.activation(m.s(ST)[64:80, :], m.ps[1][0:16, :], ACT.Copy).then_inc(S["stats"], 1)
        nc.scalar.activation(m.s(ST)[96:112, :], m.ps[2][0:16, :], ACT.Sqrt, scale=32.0).then_inc(S["stats"], 1)
        yield 19
        for h in range(4):
            a.wait_ge(S["hid"], h + 1)
            nc.scalar.activation(m.s(HG + h), m.ps[3 + h % 2][:, :], ACT.Gelu, bias=m.W("b1")).then_inc(S["gelu"], 1)
        yield 30
        a.wait_ge(S["shifted"], 1)
        nc.scalar.activation(pr, lg, ACT.Exp).then_inc(S["exp"], 1)
        a.wait_ge(S["probs_t"], 1)
        nc.scalar.activation(m.s(PRT)[0:16, :], m.ps[1][0:16, :], ACT.Copy).then_inc(S["probs_sb"], 1)
        a.wait_ge(S["o"], 1)
        nc.scalar.activation(m.s(T1), m.s(O), ACT.Square).then_inc(S["o_sq"], 1)
        a.wait_ge(S["o_ms"], 1)
        nc.scalar.activation(m.s(T2), m.ps[1][:, :], ACT.Ln, bias=m.small[:, 120:121]).then_inc(S["o_ln"], 1)
        a.wait_ge(S["o_ln"], 1)
        nc.scalar.activation(m.s(T2), m.s(T2), ACT.Exp, scale=-0.5).then_inc(S["o_rstd"], 1)

    def vector(v, S):
        yield 0
        link = linker(v, S["chain"])
        nc.vector.memset(m.s(ST), 0.0).then_inc(S["st_zero"], 1)
        v.wait_ge(S["st_zero"], 1)
        v.wait_ge(S["mean_sq"], 1)
        v.wait_ge(S["stats"], 3)
        nc.vector.tensor_tensor(m.s(ST)[32:48, :], m.ps[2][0:16, :], m.s(M2)[0:16, :], ALU.subtract).then_inc(S["stats"], 1)
        yield 30
        v.wait_ge(S["logits"], 1)
        link(nc.vector.tensor_tensor(j4(lg), j4(m.ps[0][:, 0:64]), m.W("b2").unsqueeze(1).to_broadcast([128, 16, 4]), ALU.add))
        link(nc.vector.tensor_scalar(lg, lg, m.small[:, 0:1], None, ALU.mult))
        link(nc.vector.tensor_reduce(mx, j4(lg), AXX, ALU.max))
        nc.vector.tensor_tensor(j4(lg), j4(lg), b16(mx), ALU.subtract).then_inc(S["shifted"], 1)
        v.wait_ge(S["exp"], 1)
        link(nc.vector.tensor_reduce(rs, j4(pr), AXX, ALU.add))
        link(nc.vector.reciprocal(rs, rs))
        link(nc.vector.tensor_tensor(j4(pr), j4(pr), b16(rs), ALU.mult))
        pc = m.small[:, 5:21].unsqueeze(1).to_broadcast([128, 4, 16])
        t16 = lambda ap: ap.rearrange("p (t k) -> p t k", t=4)
        nc.vector.scalar_tensor_tensor(t16(pr), t16(pr), 1.0 - 2.0 * 0.08, pc, ALU.mult, ALU.add).then_inc(S["probs"], 1)
        v.wait_ge(S["prob_bc"], 1)
        link(nc.vector.tensor_tensor(m.s(O), streams[0], m.ps[PB[0]][:, :], ALU.mult))
        for k in range(1, 4):
            v.wait_ge(S["prob_bc"], k + 1)
            link(nc.vector.tensor_tensor(m.s(T2), streams[k], m.ps[PB[k]][:, :], ALU.mult))
            add = nc.vector.tensor_tensor(m.s(O), m.s(O), m.s(T2), ALU.add)
            if k < 3:
                link(add)
        add.then_inc(S["o"], 1)
        v.wait_ge(S["o"], 1)
        v.wait_ge(S["o_rstd"], 1)
        nc.vector.scalar_tensor_tensor(m.s(T2), m.s(O), m.W("rms"), m.s(T2), ALU.mult, ALU.mult).then_inc(S["o_norm"], 1)
        v.wait_ge(S["proj"], 1)
        nc.vector.tensor_tensor(m.x[:, :], m.x[:, :], m.ps[2][:, :], ALU.add)

    return "gate", {"tensor": tensor, "vector": vector, "scalar": scalar}


def l0_ffn(nc, m):
    R, K, K2 = 3, 4, 5

    def tensor(pe, S):
        yield 0
        ln_tensor(nc, pe, S, m, m.x[:, :], (0, 1, 2), (0, 1))
        pe.wait_ge(S["h_ready"], 1)
        for i in range(2):
            nc.tensor.matmul(m.ps[2 + i][:, :], m.mixw[:, 2 * i, :], m.h, start=True, stop=False)
            nc.tensor.matmul(m.ps[2 + i][:, :], m.mixw[:, 2 * i + 1, :], m.hp[:, PAD - 1:PAD - 1 + L], start=False, stop=True).then_inc(S["rk"], 1)
        pe.wait_ge(S["k_act"], 1)
        nc.tensor.matmul(m.ps[4][:, :], m.W("Wvf"), m.s(K2), start=True, stop=True).then_inc(S["kv"], 1)

    def scalar(a, S):
        yield 0
        ln_scalar(nc, a, S, m, (0, 1, 2), (0, 1))
        a.wait_ge(S["rk"], 1)
        nc.scalar.activation(m.s(R), m.ps[2][:, :], ACT.Sigmoid).then_inc(S["r"], 1)
        a.wait_ge(S["rk"], 2)
        nc.scalar.activation(m.s(K), m.ps[3][:, :], ACT.Relu).then_inc(S["relu"], 1)

    def vector(v, S):
        yield 0
        ln_vector(nc, v, S, m, m.x[:, :], m.h, (0, 1, 2), (0, 1))
        v.wait_ge(S["relu"], 1)
        nc.vector.tensor_tensor(m.s(K2), m.s(K), m.s(K), ALU.mult).then_inc(S["k_act"], 1)
        v.wait_ge(S["kv"], 1)
        v.wait_ge(S["r"], 1)
        nc.vector.tensor_tensor(m.s(R), m.s(R), m.ps[4][:, :], ALU.mult).then_inc(S["rv"], 1)
        v.wait_ge(S["rv"], 1)
        nc.vector.tensor_tensor(m.x[:, :], m.x[:, :], m.s(R), ALU.add)

    return "ffn", {"tensor": tensor, "vector": vector, "scalar": scalar}


C_PC = 3
C_X1, C_ZS, C_DEL, C_DU = 4, 8, 10, 14
C_XT, C_XP, C_T = 18, 20, 23
C_ACC = 33
C_DA, C_DBU, C_HS, C_HC, C_CS = 4, 30, (0, 28), 35, 37
C_XC = (18, 19, 20, 21)
C_YP, C_U = 22, 22
C_TH = (2, 32)


def l1_inputs(nc, m):
    xp = m.work[:, C_XP:C_XP + 3, :].rearrange("p a n -> p (a n)")[:, 0:2 * (L + 8)].rearrange("p (k n) -> p k n", k=2)
    xt = m.work[:, C_XT:C_XT + 2, :].rearrange("p a n -> p (a n)")
    pc = m.work[:, C_PC, :].bitcast(BF16).rearrange("p (e n) -> p e n", e=2)
    i4 = [(e, k) for e in range(2) for k in range(2)]

    def tensor(pe, S):
        yield 0
        ln_tensor(nc, pe, S, m, m.x[:, :], (0, 1, 2), (0, 1))
        pe.wait_ge(S["h_ready"], 1)
        for k in range(4):
            nc.tensor.matmul(m.ps[2 + k][:, :], m.W("inp")[:, 128 * k:128 * k + 128], m.h, start=True, stop=True).then_inc(S["xz"], 1)
        for t in range(NT):
            last = nc.tensor.matmul(m.ps[6 + t // 2][:, 256 * (t % 2):256 * (t % 2) + 256], m.h[:, 128 * t:128 * t + 128],
                                    m.W("inp")[:, 0:256], start=True, stop=True)
        last.then_inc(S["xt"], 1)
        for e in range(2):
            for k in range(2):
                pe.wait_ge(S["x1"], 2 * e + k + 1)
                last = nc.tensor.matmul(m.ps[e][:, :], m.W("xproj")[:, 256 * e + 128 * k:256 * e + 128 * k + 128], m.s(C_X1 + 2 * e + k),
                                        start=(k == 0), stop=(k == 1))
            last.then_inc(S["xdbl"], 1)
        for i, (e, k) in enumerate(i4):
            pe.wait_ge(S["xd"], e + 1)
            if i == 0:
                pe.wait_ge(S["xz_used"], 4)
            nc.tensor.matmul(m.ps[2 + i][:, :], m.W("dtproj")[:, 256 * e + 128 * k:256 * e + 128 * k + 128], m.s(C_T + 8 + e),
                             start=True, stop=True).then_inc(S["dt"], 1)

    def scalar(a, S):
        yield 0
        ln_scalar(nc, a, S, m, (0, 1, 2), (0, 1))
        for k in range(2):
            a.wait_ge(S["xz"], k + 1)
            nc.scalar.activation(xp[:, k, 4:4 + L], m.ps[2 + k][:, :], ACT.Copy).then_inc(S["xz_used"], 1)
        for k in range(2):
            a.wait_ge(S["xz"], k + 3)
            nc.scalar.activation(m.s(C_ZS + k), m.ps[4 + k][:, :], ACT.Silu).then_inc(S["xz_used"], 1)
        a.wait_ge(S["xt"], 1)
        for t in range(2):
            nc.scalar.activation(xt[:, 512 * t:512 * t + 512], m.ps[6 + t][:, :], ACT.Copy).then_inc(S["xt_sb"], 1)
        for i in range(4):
            a.wait_ge(S["conv"], i + 1)
            nc.scalar.activation(m.s(C_X1 + i), m.s(C_T + i), ACT.Silu).then_inc(S["x1"], 1)
        for e in range(2):
            a.wait_ge(S["xdbl"], e + 1)
            nc.scalar.activation(m.s(C_T + 8 + e), m.ps[e][:, :], ACT.Copy).then_inc(S["xd"], 1)
        for i in range(4):
            a.wait_ge(S["sp_in"], i + 1)
            nc.scalar.activation(m.s(C_T + i), m.s(C_T + i), ACT.Exp).then_inc(S["sp_exp"], 1)
        for i in range(4):
            a.wait_ge(S["sp_exp"], i + 1)
            nc.scalar.activation(m.s(C_T + i), m.s(C_T + i), ACT.Ln, bias=m.small[:, 122:123]).then_inc(S["sp_ln"], 1)

    def vector(v, S):
        yield 0
        link = linker(v, S["chain"])
        nc.vector.memset(xp[:, :, 0:4], 0.0)
        link(nc.vector.memset(xp[:, :, 4 + L:8 + L], 0.0))
        ln_vector(nc, v, S, m, m.x[:, :], m.h, (0, 1, 2), (0, 1))
        v.wait_ge(S["xz_used"], 2)
        for i, (e, k) in enumerate(i4):
            w = m.W("mconv")[:, 4 * i:4 * i + 4]
            src = lambda j: xp[:, k, 1 + j:1 + j + L] if e == 0 else xp[:, k, 7 - j:7 - j + L]
            link(nc.vector.tensor_scalar(m.s(C_T + i), src(0), w[:, 0:1], m.W("mconvb")[:, i:i + 1], ALU.mult, ALU.add))
            for j in range(1, 4):
                last = nc.vector.scalar_tensor_tensor(m.s(C_T + i), src(j), w[:, j:j + 1], m.s(C_T + i), ALU.mult, ALU.add)
                if j < 3:
                    link(last)
            last.then_inc(S["conv"], 1)
        v.wait_ge(S["xz_used"], 4)
        for k in range(2):
            link(nc.vector.tensor_reduce(m.small[:, 100 + k:101 + k], m.s(C_ZS + k), AXX, ALU.max))
        r1, md = m.s(C_T + 5)[0:32, :], m.s(C_T + 6).bitcast(BF16)[0:32, 0:L]
        for e in range(2):
            v.wait_ge(S["xd"], e + 1)
            full = m.s(C_T + 8 + e)[0:32, :]
            link(nc.vector.tensor_copy(pc[0:32, e, :], full))
            link(nc.vector.tensor_tensor(r1, full, pc[0:32, e, :], ALU.subtract))
            link(nc.vector.tensor_copy(md, r1))
            link(nc.vector.tensor_tensor(r1, r1, md, ALU.subtract))
            nc.vector.tensor_copy(pc[32:64, e, :], md)
            link(nc.vector.tensor_copy(pc[64:96, e, :], r1))
        for i in range(4):
            v.wait_ge(S["dt"], i + 1)
            v.wait_ge(S["x1"], 4)
            nc.vector.tensor_scalar(m.s(C_T + i), m.ps[2 + i][:, :], m.W("dtb")[:, i:i + 1], SP_CAP, ALU.add, ALU.min).then_inc(S["sp_in"], 1)
        for i in range(4):
            v.wait_ge(S["sp_ln"], i + 1)
            link(nc.vector.scalar_tensor_tensor(m.s(C_DEL + i), m.ps[2 + i][:, :], m.W("dtb")[:, i:i + 1], m.s(C_T + i), ALU.add, ALU.max))
            nc.vector.tensor_tensor(m.s(C_DU + i), m.s(C_DEL + i), m.s(C_X1 + i), ALU.mult)
        for k in range(2):
            link(nc.vector.tensor_scalar(m.s(C_ACC + k), m.s(C_X1 + k), m.W("Dp")[:, k:k + 1], None, ALU.mult))
            nc.vector.scalar_tensor_tensor(m.s(C_ACC + k), m.s(C_X1 + 2 + k), m.W("Dp")[:, 2 + k:3 + k], m.s(C_ACC + k), ALU.mult, ALU.add)

    return "proj", {"tensor": tensor, "vector": vector, "scalar": scalar}


def l1_core(nc, m, d):
    xt = m.work[:, C_XT:C_XT + 2, :].rearrange("p a n -> p (a n)").rearrange("p (t c) -> p t c", t=NT)
    yp = m.work[:, C_YP:C_YP + 5, :].rearrange("p a n -> p (a n)")[:, 0:4 * 520].rearrange("p (k n) -> p k n", k=4)
    pc = m.work[:, C_PC, :].bitcast(BF16).rearrange("p (e n) -> p e n", e=2)
    u = m.work[:, C_U:C_U + 6, :].rearrange("p a n -> p (a n)").rearrange("p (t n) -> p t n", t=NT)
    xc = lambda o: m.s(C_XC[o])
    sq = xc
    two = lambda slot: m.work[:, slot:slot + 2, :]
    STEPS = [(e, n) for e in range(2) for n in range(NS)]

    units = ([("dft", c, r) for r in range(2) for c in range(2)] + [("conv", o, 0) for o in range(4)]
             + [("chan", t, 0) for t in range(4)] + [("time", c, r) for c in range(2) for r in range(2)])
    slices = [(i, k) for i, u_ in enumerate(units) for k in range({"dft": 1, "conv": 5, "chan": 1, "time": 2}[u_[0]])]
    plan = [slices[i * len(slices) // (len(STEPS) - 1):(i + 1) * len(slices) // (len(STEPS) - 1)] for i in range(len(STEPS) - 1)] + [[]]
    ends = [[i for i, k in p if k == {"dft": 1, "conv": 5, "chan": 1, "time": 2}[units[i][0]] - 1] for p in plan]
    bank = lambda i: m.ps[4 + i % 4]

    def products(i):
        kind, a, b = units[i]
        if kind == "dft":
            return [(xt[:, t, 128 * a:128 * a + 128], m.dft[:, b, t, :]) for t in range(NT)]
        if kind == "conv":
            return [(m.fw[:, t, k, 128 * a:128 * a + 128], yp[:, k, 2 + t:2 + t + L]) for t in range(TAPS) for k in range(4)]
        if kind == "chan":
            return [(xc(k)[:, 128 * a:128 * a + 128], m.inv[:, k, :]) for k in range(4)]
        c = 128 * a
        first = [(u[:, t, c:c + 128], m.dft[:, b, t, :]) for t in range(NT)]
        second = [(u[:, t, (512 if b == 0 else 256) + c:(512 if b == 0 else 256) + c + 128], m.dft[:, 1 - b, t, :]) for t in range(NT)]
        return first + second

    def sync(sp, S):
        yield 0
        sp.dma_start(m.dft, d["time"].rearrange("p (a t n) -> p a t n", a=2, t=NT)).then_inc(S["dft"], 16)
        for t in range(TAPS):
            sp.dma_start(m.fw[:, t, :, :], d["folded"][:, 2048 * t:2048 * t + 2048].rearrange("p (k n) -> p k n", k=4)).then_inc(S["fw"], 16)

    def tensor(pe, S):
        yield 0
        def rows(i):
            e, n = STEPS[i]
            if i >= 2:
                pe.wait_ge(S["dbu"], i - 1)
                pe.wait_ge(S["c_sb"], i - 1)
            nc.tensor.matmul(m.ps[i % 2][:, :], m.sel[0:96, n, :], pc[0:96, e, :], start=True, stop=True).then_inc(S["b_row"], 1)
            nc.tensor.matmul(m.ps[2 + i % 2][:, :], m.sel[0:96, NS + n, :], pc[0:96, e, :], start=True, stop=True).then_inc(S["c_row"], 1)
        rows(0)
        for i in range(len(STEPS)):
            if i + 1 < len(STEPS):
                rows(i + 1)
            for unit, part in plan[i]:
                kind = units[unit][0]
                if part == 0:
                    need = {"dft": 0, "conv": 4, "chan": 8, "time": 12}[kind]
                    if unit == 0:
                        pe.wait_ge(S["dft"], 16)
                    if kind == "time":
                        pe.wait_ge(S["u_main"], NT)
                    if max(need, unit - 3) > 0:
                        pe.wait_ge(S["unit_out"], max(need, unit - 3))
                if unit == 4:
                    pe.wait_ge(S["fw"], 16 * TAPS)
                ps = products(unit)
                for j in range(4 * part, 4 * part + 4):
                    last = nc.tensor.matmul(bank(unit)[:, :], ps[j][0], ps[j][1], start=(j == 0), stop=(j == len(ps) - 1))
                if 4 * part + 4 == len(ps):
                    last.then_inc(S["unit"], 1)

    def scalar(a, S):
        yield 0
        def leave(i):
            kind, p, b = units[i]
            a.wait_ge(S["unit"], i + 1)
            if kind == "dft":
                nc.scalar.activation(yp[:, 2 * b + p, 4:4 + L], bank(i)[:, :], ACT.Copy, scale=(1.0, -1.0)[b]).then_inc(S["unit_out"], 1)
            elif kind == "conv":
                if i >= 6:
                    a.wait_ge(S["unit_out"], i - 1)
                nc.scalar.activation(m.s(C_TH[i % 2]), bank(i)[:, :], ACT.Tanh, bias=m.small[:, 104 + p:105 + p], scale=0.5).then_inc(S["tanh"], 1)
            elif kind == "chan":
                nc.scalar.activation(u[:, p, 0:512], bank(i)[:, :], ACT.Copy).then_inc(S["u_main"], 1)
                nc.scalar.activation(u[:, p, 512:768], bank(i)[:, 256:512], ACT.Copy, scale=-1.0).then_inc(S["unit_out"], 1)
            else:
                nc.scalar.activation(sq(i - 12), bank(i)[:, :], ACT.Square).then_inc(S["unit_out"], 1)

        for i, (e, n) in enumerate(STEPS):
            if i >= 2:
                a.wait_ge(S["h"], 2 * (i - 1))
            for k in range(2):
                c = SM["A"] + 32 * e + 16 * k + n
                nc.scalar.activation(m.s(C_DA + 2 * (i % 2) + k), m.s(C_DEL + 2 * e + k), ACT.Exp, scale=m.small[:, c:c + 1]).then_inc(S["da"], 1)
            a.wait_ge(S["c_row"], i + 1)
            if i >= 2:
                a.wait_ge(S["hc"], i - 1)
            nc.scalar.activation(m.s(C_CS + i % 2), m.ps[2 + i % 2][:, :], ACT.Copy).then_inc(S["c_sb"], 1)
            if i:
                for unit in ends[i - 1]:
                    leave(unit)

    def vector(v, S):
        yield 0
        link = linker(v, S["chain"])
        nc.vector.memset(yp[:, :, 0:4], 0.0)
        nc.vector.memset(yp[:, :, 4 + L:8 + L], 0.0)
        link(nc.vector.tensor_scalar(m.small[:, 104:108], m.W("fftb"), 0.5, None, ALU.mult))
        for i, (e, n) in enumerate(STEPS):
            v.wait_ge(S["b_row"], i + 1)
            if i:
                v.wait_ge(S["h"], 2 * i)
            nc.vector.tensor_tensor(two(C_DBU), two(C_DU + 2 * e), m.ps[i % 2][:, :].unsqueeze(1).to_broadcast([128, 2, L]), ALU.mult).then_inc(S["dbu"], 1)
            v.wait_ge(S["dbu"], i + 1)
            if i >= 2:
                v.wait_ge(S["hc"], i - 1)
            for k in range(2):
                v.wait_ge(S["da"], 2 * i + k + 1)
                s = slice(None) if e == 0 else slice(None, None, -1)
                nc.vector.tensor_tensor_scan(m.s(C_HS[i % 2] + k)[:, s], m.s(C_DA + 2 * (i % 2) + k)[:, s], m.s(C_DBU + k)[:, s], 0.0, ALU.mult, ALU.add).then_inc(S["h"], 1)
            if i:
                v.wait_ge(S["hc"], i)
                if i > 1:
                    v.wait_ge(S["acc"], i - 1)
                nc.vector.tensor_tensor(two(C_ACC), two(C_ACC), two(C_HC), ALU.add).then_inc(S["acc"], 1)
                for unit in ends[i - 1]:
                    if units[unit][0] == "conv":
                        o = unit - 4
                        v.wait_ge(S["tanh"], o + 1)
                        link(nc.vector.tensor_scalar(m.s(C_TH[unit % 2]), m.s(C_TH[unit % 2]), 0.5, 0.5, ALU.mult, ALU.add))
                        nc.vector.scalar_tensor_tensor(xc(o), bank(unit)[:, :], m.W("fftb")[:, o:o + 1], m.s(C_TH[unit % 2]), ALU.add, ALU.mult).then_inc(S["unit_out"], 1)
        last = len(STEPS)
        v.wait_ge(S["hc"], last)
        v.wait_ge(S["acc"], last - 1)
        nc.vector.tensor_tensor(two(C_ACC), two(C_ACC), two(C_HC), ALU.add)

    def gpsimd(g, S):
        yield 0
        for i, (e, n) in enumerate(STEPS):
            g.wait_ge(S["h"], 2 * i + 2)
            g.wait_ge(S["c_sb"], i + 1)
            if i:
                g.wait_ge(S["acc"], i)
            nc.gpsimd.tensor_tensor(two(C_HC), two(C_HS[i % 2]), m.s(C_CS + i % 2).unsqueeze(1).to_broadcast([128, 2, L]), ALU.mult).then_inc(S["hc"], 1)

    return "scan", {"sync": sync, "tensor": tensor, "vector": vector, "scalar": scalar, "gpsimd": gpsimd}


def l1_output(nc, m):
    sq = lambda i: m.s(C_XC[i])
    sm = m.small

    def vector(v, S):
        yield 0
        link = linker(v, S["chain"])
        for k in range(2):
            nc.vector.tensor_tensor(sq(2 * k), sq(2 * k), sq(2 * k + 1), ALU.add).then_inc(S["power"], 1)
        for k in range(2):
            link(nc.vector.tensor_tensor(m.s(C_ACC + k), m.s(C_ACC + k), m.s(C_ZS + k), ALU.mult))
        link(nc.vector.tensor_scalar(sm[:, 102:104], sm[:, 100:102], -1.0, None, ALU.mult))
        link(nc.vector.tensor_tensor(sm[:, 100:102], sm[:, 100:102], sm[:, 102:104], ALU.max))
        for k in range(2):
            v.wait_ge(S["mag"], k + 1)
            link(nc.vector.bn_stats(m.s(0)[:, 0:6], sq(2 * k)))
            link(nc.vector.bn_aggr(m.s(0)[:, 8 + 2 * k:10 + 2 * k], m.s(0)[:, 0:6]))
            z, mean, var = sm[:, 100 + k:101 + k], m.s(0)[:, 8 + 2 * k:9 + 2 * k], m.s(0)[:, 9 + 2 * k:10 + 2 * k]
            link(nc.vector.tensor_tensor(var, var, z, ALU.mult))
            link(nc.vector.tensor_tensor(var, var, z, ALU.mult))
            nc.vector.tensor_scalar(m.s(0)[:, 16 + k:17 + k], var, 1e-5, None, ALU.add).then_inc(S["var"], 1)
        for k in range(2):
            v.wait_ge(S["std"], k + 1)
            z, mean = sm[:, 100 + k:101 + k], m.s(0)[:, 8 + 2 * k:9 + 2 * k]
            r = m.s(0)[:, 20 + k:21 + k]
            link(nc.vector.reciprocal(r, m.s(0)[:, 18 + k:19 + k]))
            link(nc.vector.tensor_tensor(r, r, z, ALU.mult))
            link(nc.vector.tensor_scalar(sq(2 * k), sq(2 * k), mean, r, ALU.subtract, ALU.mult))
            nc.vector.tensor_tensor(m.s(C_ACC + k), m.s(C_ACC + k), sq(2 * k), ALU.add).then_inc(S["y"], 1)
        v.wait_ge(S["proj"], 1)
        nc.vector.tensor_tensor(m.xd[:, :], m.x[:, :], m.ps[0][:, :], ALU.add)

    def scalar(a, S):
        yield 0
        for k in range(2):
            a.wait_ge(S["power"], k + 1)
            nc.scalar.activation(sq(2 * k), sq(2 * k), ACT.Sqrt).then_inc(S["mag"], 1)
        for k in range(2):
            a.wait_ge(S["var"], k + 1)
            nc.scalar.activation(m.s(0)[:, 18 + k:19 + k], m.s(0)[:, 16 + k:17 + k], ACT.Sqrt).then_inc(S["std"], 1)

    def tensor(pe, S):
        yield 0
        for k in range(2):
            pe.wait_ge(S["y"], k + 1)
            last = nc.tensor.matmul(m.ps[0][:, :], m.W("outp")[:, 128 * k:128 * k + 128], m.s(C_ACC + k), start=(k == 0), stop=(k == 1))
        last.then_inc(S["proj"], 1)

    return "mout", {"tensor": tensor, "vector": vector, "scalar": scalar}


MASK, WGT, RF, HID, HM = DWORK, DWORK + 4, DWORK + 6, DWORK + 7, DWORK + 12
INT, VEL, HALT = DWORK + 16, DWORK + 17, DWORK + 18
SG, SA, SPT, ACCX, ACCV, TA = DWORK + 19, DWORK + 22, DWORK + 25, DWORK + 28, DWORK + 29, DWORK + 30
D_BANKS = (5, 6, 7)
D_LN = (ACCX, ACCV, TA)


def mask(m, i):
    return m.work[:, MASK:MASK + 4, :].bitcast(BF16)[:, i // 2, L * (i % 2):L * (i % 2) + L]


def l1_route(nc, m):
    tok = m.work[:, SG, :]
    lg, mx, eq, m2, pk = tok[:, 0:32], tok[:, 32:36], tok[:, 40:72], tok[:, 36:40], tok[:, 128:256]
    e8 = lambda ap: ap.rearrange("p (t k) -> p t k", k=8)
    b8 = lambda ap: ap.unsqueeze(2).to_broadcast([128, 4, 8])
    rb = m.work[:, SA, :].bitcast(BF16)[:, 0:L]
    pk3 = pk.rearrange("p (t k) -> p t k", k=32)
    dec = m.T("dec").unsqueeze(1).to_broadcast([128, 4, 8])
    mask_bank = lambda i: m.ps[(6, 7, 5)[i % 3]]

    def tensor(pe, S):
        yield 0
        ln_tensor(nc, pe, S, m, m.xd[:, :], D_LN, (5, 6))
        pe.wait_ge(S["h_ready"], 1)
        nc.tensor.matmul(m.ps[7][:, :], m.W("m1")[:, 0:128], m.hd[:, :], start=True, stop=True).then_inc(S["hid"], 1)
        yield 10
        pe.wait_ge(S["gelu"], 1)
        for t in range(NT):
            last = nc.tensor.matmul(m.ps[5][:, 8 * t:8 * t + 8], m.s(HID)[:, 128 * t:128 * t + 128], m.W("rw2"), start=True, stop=True)
        last.then_inc(S["logits"], 1)
        yield 15
        pe.wait_ge(S["packed"], 1)
        for t in range(NT):
            last = nc.tensor.transpose(m.ps[6][0:32, 128 * t:128 * t + 128], pk[:, 32 * t:32 * t + 32], m.T("ident"))
        last.then_inc(S["routes"], 1)
        pe.wait_ge(S["routes_sb"], 2)
        for r in range(2):
            nc.tensor.matmul(m.ps[(7, 5)[r]][:, :], m.T("wsel")[0:32, 128 * r:128 * r + 128], m.s(RF)[0:32, :], start=True, stop=True).then_inc(S["w_bc"], 1)
        yield 20
        for i in range(8):
            if i in (1, 2):
                pe.wait_ge(S["w_sb"], i)
            if i >= 3:
                pe.wait_ge(S["mask_sb"], i - 2)
            nc.tensor.matmul(mask_bank(i)[:, :], m.sel[0:32, 32 + i, :], rb[0:32, :], start=True, stop=True).then_inc(S["mask"], 1)

    def scalar(a, S):
        yield 0
        ln_scalar(nc, a, S, m, D_LN, (5, 6))
        yield 10
        a.wait_ge(S["hid"], 1)
        nc.scalar.activation(m.s(HID), m.ps[7][:, :], ACT.Gelu, bias=m.W("m1b")).then_inc(S["gelu"], 1)
        yield 15
        a.wait_ge(S["shifted"], 1)
        nc.scalar.activation(lg, lg, ACT.Exp).then_inc(S["exp"], 1)
        a.wait_ge(S["routes"], 1)
        nc.scalar.activation(m.s(RF)[0:32, :], m.ps[6][0:32, :], ACT.Copy).then_inc(S["routes_sb"], 1)
        nc.scalar.activation(rb[0:32, :], m.ps[6][0:32, :], ACT.Copy).then_inc(S["routes_sb"], 1)
        yield 20
        for i in range(8):
            a.wait_ge(S["mask"], i + 1)
            nc.scalar.activation(mask(m, i), mask_bank(i)[:, :], ACT.Copy).then_inc(S["mask_sb"], 1)

    def vector(v, S):
        yield 0
        ln_vector(nc, v, S, m, m.xd[:, :], m.hd[:, :], D_LN, (5, 6))
        link = linker(v, S["chain"])
        yield 10
        link(nc.vector.memset(pk, 0.0))
        v.wait_ge(S["logits"], 1)
        link(nc.vector.tensor_tensor(e8(lg), e8(m.ps[5][:, 0:32]), m.W("rb2").unsqueeze(1).to_broadcast([128, 4, 8]), ALU.add))
        link(nc.vector.tensor_reduce(mx, e8(lg), AXX, ALU.max))
        nc.vector.tensor_tensor(e8(lg), e8(lg), b8(mx), ALU.subtract).then_inc(S["shifted"], 1)
        yield 15
        v.wait_ge(S["exp"], 1)
        top = (mx, m2)
        for r in range(2):
            link(nc.vector.tensor_reduce(top[r], e8(lg), AXX, ALU.max))
            link(nc.vector.tensor_tensor(e8(eq), e8(lg), b8(top[r]), ALU.is_equal))
            link(nc.vector.tensor_tensor(e8(eq), e8(eq), dec, ALU.mult))
            link(nc.vector.tensor_reduce(tok[:, 76:80], e8(eq), AXX, ALU.max))
            link(nc.vector.tensor_tensor(pk3[:, :, 8 * r:8 * r + 8], e8(eq), b8(tok[:, 76:80]), ALU.is_equal))
            if r == 0:
                link(nc.vector.scalar_tensor_tensor(e8(lg), pk3[:, :, 0:8], -2.0, e8(lg), ALU.mult, ALU.add))
        s = tok[:, 80:84]
        link(nc.vector.tensor_tensor(s, mx, m2, ALU.add))
        link(nc.vector.reciprocal(s, s))
        link(nc.vector.tensor_tensor(pk3[:, :, 16], mx, s, ALU.mult))
        nc.vector.tensor_tensor(pk3[:, :, 17], m2, s, ALU.mult).then_inc(S["packed"], 1)
        yield 20
        for r in range(2):
            v.wait_ge(S["w_bc"], r + 1)
            nc.vector.tensor_scalar(m.s(WGT + r), m.ps[(7, 5)[r]][:, :], m.small[:, 22:23], None, ALU.mult).then_inc(S["w_sb"], 1)
        nc.vector.tensor_copy(m.s(INT), m.hd[:, :])

    return "route", {"tensor": tensor, "vector": vector, "scalar": scalar}


def l1_steps(nc, m):
    src = (m.s(INT), m.s(VEL))
    col = {"a": 0, "b": 1, "g": 2}
    place = {"a": SA, "g": SG, "b": SPT}
    bank = lambda i: m.ps[D_BANKS[i % 3]]
    sigs = [[("g", s) for s in range(3)], [(w, s) for w in "ag" for s in range(3)]]
    outs = [sig + [("b", s) for s in range(3)] for sig in sigs]
    T0, T_MASK = (0, 62), 9
    t_out = lambda it, i: T0[it] + 14 + (6 if it == 0 else 7) * i
    T_MEET, T_END = 61, 140
    before = (0, 6)

    def meet(eng, S):
        eng.drain().then_inc(S["met"], 1)
        eng.wait_ge(S["met"], 3)

    def tensor(pe, S):
        for it in range(2):
            yield T0[it]
            if it:
                meet(pe, S)
            for i in range(5):
                if i >= 3:
                    pe.wait_ge(S["gelu"], 5 * it + i - 2)
                for k in range(1 + it):
                    w = m.W("m1")[:, 128 * k:128 * k + 128] if i == 0 else m.W("e1")[:, 512 * k + 128 * (i - 1):512 * k + 128 * i]
                    last = nc.tensor.matmul(bank(i)[:, :], w, src[k], start=(k == 0), stop=(k == it))
                last.then_inc(S["hid"], 1)
            yield T0[it] + T_MASK
            pe.wait_ge(S["gelu"], 5 * it + 5)
            nc.tensor.matmul(bank(5)[:, :], m.W("hw2"), m.s(HID), start=True, stop=True).then_inc(S["halt_lin"], 1)
            n0, nsig = 3 * it, len(sigs[it])
            for i, (what, s) in enumerate(outs[it]):
                yield t_out(it, i)
                if i == 2:
                    pe.wait_ge(S["halt"], it + 1)
                if i >= 3:
                    pe.wait_ge(S["sig"], n0 + i - 2)
                c = 128 * col[what]
                if s == 0:
                    last = nc.tensor.matmul(bank(i)[:, :], m.W("s2")[:, c:c + 128], m.s(HID), start=True, stop=True)
                else:
                    h = (HM, HID + 1)[s - 1]
                    for t in range(4):
                        pe.wait_ge(S["masked"], 8 * it + 4 * (s - 1) + t + 1)
                        nc.tensor.matmul(bank(i)[:, :], m.W("e2")[:, 384 * t + c:384 * t + c + 128], m.s(h + t), start=(t == 0), stop=False)
                    last = nc.tensor.matmul(bank(i)[:, :], m.W("e2b")[0:32, 384 * (s - 1) + c:384 * (s - 1) + c + 128], m.s(RF)[0:32, :], start=False, stop=True)
                last.then_inc(S["ctrl"], 1)

    def scalar(a, S):
        for it in range(2):
            yield T0[it]
            if it:
                meet(a, S)
            for i in range(5):
                a.wait_ge(S["hid"], 5 * it + i + 1)
                nc.scalar.activation(m.s(HID + i), bank(i)[:, :], ACT.Gelu, bias=m.W("m1b") if i == 0 else m.W("e1b")[:, i - 1:i]).then_inc(S["gelu"], 1)
            yield T0[it] + T_MASK
            a.wait_ge(S["halt_lin"], it + 1)
            nc.scalar.activation(m.s(HALT), bank(5)[:, :], ACT.Sigmoid, bias=m.W("hb2")).then_inc(S["halt"], 1)
            o0 = len(outs[0]) * it
            for i, (what, s) in enumerate(outs[it]):
                yield t_out(it, i)
                if what != "b":
                    a.wait_ge(S["ctrl"], o0 + i + 1)
                    bias = {"bias": m.W("s2b")[:, col[what]:col[what] + 1]} if s == 0 else {}
                    nc.scalar.activation(m.s(place[what] + s), bank(i)[:, :], ACT.Sigmoid, **bias).then_inc(S["sig"], 1)
                else:
                    a.wait_ge(S["sp_in"], 3 * it + s + 1)
                    nc.scalar.activation(m.s(SPT + s), m.s(SPT + s), ACT.Exp).then_inc(S["sp_exp"], 1)
                    a.wait_ge(S["sp_exp"], 3 * it + s + 1)
                    nc.scalar.activation(m.s(SPT + s), m.s(SPT + s), ACT.Ln, bias=m.small[:, 122:123]).then_inc(S["sp_ln"], 1)

    def vector(v, S):
        link = linker(v, S["chain"])
        bias = lambda s: m.W("s2b")[:, 1:2] if s == 0 else m.small[:, 125:126]
        for it in range(2):
            yield T0[it]
            if it:
                meet(v, S)
            yield T0[it] + T_MASK
            for r in range(2):
                for t in range(4):
                    v.wait_ge(S["gelu"], 5 * it + t + 2)
                    if r:
                        v.wait_ge(S["masked"], 8 * it + t + 1)
                    nc.vector.tensor_tensor(m.s((HM, HID + 1)[r] + t), m.s(HID + 1 + t), mask(m, 4 * r + t), ALU.mult).then_inc(S["masked"], 1)
            nsig, o0, sig0 = len(sigs[it]), len(outs[0]) * it, 3 * it
            for s in range(3):
                i = nsig + s
                yield t_out(it, i)
                v.wait_ge(S["ctrl"], o0 + i + 1)
                nc.vector.tensor_scalar(m.s(SPT + s), bank(i)[:, :], bias(s), SP_CAP, ALU.add, ALU.min).then_inc(S["sp_in"], 1)
                yield t_out(it, i) + 5
                v.wait_ge(S["sp_ln"], 3 * it + s + 1)
                link(nc.vector.scalar_tensor_tensor(m.s(SPT + s), bank(i)[:, :], bias(s), m.s(SPT + s), ALU.add, ALU.max))
                link(nc.vector.scalar_tensor_tensor(m.s(TA), m.s(INT), m.W("mu"), m.s(SPT + s), ALU.subtract, ALU.mult))
                w = m.small[:, 21:22] if s == 0 else None
                if it:
                    v.wait_ge(S["sig"], sig0 + nsig)
                    link(nc.vector.tensor_tensor(m.s(SA + s), m.s(SA + s), m.s(VEL), ALU.mult))
                    link(nc.vector.tensor_tensor(m.s(TA), m.s(SA + s), m.s(TA), ALU.subtract))
                else:
                    v.wait_ge(S["sig"], nsig)
                    link(nc.vector.tensor_scalar(m.s(TA), m.s(TA), -1.0, None, ALU.mult))
                if s == 0:
                    link(nc.vector.tensor_scalar(m.s(ACCV), m.s(TA), w, None, ALU.mult))
                    link(nc.vector.tensor_tensor(m.s(ACCX), m.s(ACCV), m.s(SG), ALU.mult))
                else:
                    link(nc.vector.tensor_tensor(m.s(TA), m.s(TA), m.s(WGT + s - 1), ALU.mult))
                    nc.vector.tensor_tensor(m.s(ACCV), m.s(ACCV), m.s(TA), ALU.add)
                    link(nc.vector.tensor_tensor(m.s(SG + s), m.s(SG + s), m.s(TA), ALU.mult))
                    link(nc.vector.tensor_tensor(m.s(ACCX), m.s(ACCX), m.s(SG + s), ALU.add))
            v.wait_ge(S["halt"], it + 1)
            link(nc.vector.scalar_tensor_tensor(m.s(TA), m.s(ACCX), 0.1, m.s(HALT), ALU.mult, ALU.mult))
            link(nc.vector.tensor_tensor(m.s(INT), m.s(INT), m.s(TA), ALU.add))
            if it == 0:
                link(nc.vector.tensor_tensor(m.s(VEL), m.s(ACCV), m.s(HALT), ALU.mult))

    return "steps", {"tensor": tensor, "vector": vector, "scalar": scalar}


def l1_refine(nc, m, out_dram, b):
    H0, RES, OUT = HID, HM, HM + 1

    def tensor(pe, S):
        yield 0
        for k in range(2):
            nc.tensor.matmul(m.ps[5 + k][:, :], m.W("r1")[:, 128 * k:128 * k + 128], m.s(INT), start=True, stop=True).then_inc(S["hid"], 1)
        yield 20
        for k in range(2):
            pe.wait_ge(S["gelu"], k + 1)
            last = nc.tensor.matmul(m.ps[7][:, :], m.W("r2")[:, 128 * k:128 * k + 128], m.s(H0 + k), start=(k == 0), stop=(k == 1))
        last.then_inc(S["refined"], 1)

    def scalar(a, S):
        yield 20
        for k in range(2):
            a.wait_ge(S["hid"], k + 1)
            nc.scalar.activation(m.s(H0 + k), m.ps[5 + k][:, :], ACT.Gelu, bias=m.W("r1b")[:, k:k + 1]).then_inc(S["gelu"], 1)

    def vector(v, S):
        yield 0
        nc.vector.tensor_tensor(m.s(RES), m.xd[:, :], m.hd[:, :], ALU.add).then_inc(S["res"], 1)
        yield 21
        v.wait_ge(S["refined"], 1)
        nc.vector.tensor_scalar(m.s(OUT), m.ps[7][:, :], m.W("r2b"), m.W("iw"), ALU.add, ALU.mult).then_inc(S["scaled"], 1)
        v.wait_ge(S["scaled"], 1)
        v.wait_ge(S["res"], 1)
        nc.vector.tensor_tensor(m.xd[:, :], m.s(OUT), m.s(RES), ALU.add).then_inc(S["done"], 1)

    def sync(sp, S):
        yield 22
        sp.wait_ge(S["done"], 1)
        sp.dma_start(out_dram[bass.ds(b, 1), :, :].rearrange("o c t -> (o c) t"), m.xd[:, :]).then_inc(S["stored"], 16)
        sp.wait_ge(S["stored"], 16)

    return "refine", {"tensor": tensor, "vector": vector, "scalar": scalar, "sync": sync}


def build(nc, d, out):
    with ExitStack() as ctx:
        m = Mem(nc, ctx)

        def scan_stages():
            run_block(nc, l1_inputs(nc, m))
            run_block(nc, l1_core(nc, m, d))
            run_block(nc, l1_output(nc, m))

        run_block(nc, setup(nc, m, d))
        run_block(nc, l0_inputs(nc, m, d["x"], 0))
        run_block(nc, l0_delta(nc, m))
        run_block(nc, l0_gate(nc, m))
        run_block(nc, l0_ffn(nc, m))
        with nc.Fori(0, B - 1) as b:
            scan_stages()
            run_block(nc, l0_inputs(nc, m, d["x"], b + 1), l1_route(nc, m))
            run_block(nc, l0_delta(nc, m), l1_steps(nc, m))
            run_block(nc, l0_gate(nc, m), l1_refine(nc, m, out, b))
            run_block(nc, l0_ffn(nc, m))
        scan_stages()
        run_block(nc, l1_route(nc, m))
        run_block(nc, l1_steps(nc, m))
        run_block(nc, l1_refine(nc, m, out, B - 1))


def lay_out(inputs, np):
    g = {k: np.asarray(v) for k, v in inputs.items()}
    A = lambda n: g["L0_attn_" + n]
    F = lambda n: g["L0_ffn_" + n]
    C = lambda n: g["L1_attn_" + n]
    E = lambda n: g["L1_ffn_" + n]
    z = lambda *s: np.zeros(s, np.float32)
    rows = lambda a: np.tile(np.reshape(a, (1, -1)), (128, 1))
    cols = lambda a: np.reshape(a, (-1, 128)).T
    w = {}
    w["Wb"] = np.repeat(A("Wb"), 32, axis=1)
    w["fir_s"] = A("fir_short_w").reshape(128, FIR_S)
    w["fir_l"] = A("fir_long_w").reshape(128, FIR_L)
    w["W1x"] = A("mlp_w1")[:128]
    t = z(128, 4, 128)
    for h in range(4):
        for s in range(4):
            for k in range(4):
                t[32 * k + 4 * s + h, h] = A("mlp_w1")[128 + 4 * s + k]
    w["W1s"] = t
    w["b1"], w["W2"], w["b2"] = A("mlp_b1"), A("mlp_w2"), rows(A("mlp_b2"))
    w["temp"], w["res"], w["rms"] = rows(A("logit_temp")), rows(A("conv_res_logit")), np.tile(A("rms_w"), 4)
    w["Wo"] = A("Wo")
    w["Wvf"], w["mur"], w["muk"] = F("W_v").T, F("mu_r"), F("mu_k")
    w["inp"] = C("in_proj_w").T
    both = lambda a, b: np.stack([C(a), C(b)])
    w["mconv"] = both("conv1d_w", "conv1db_w").reshape(2, 2, 128, 4).transpose(2, 0, 1, 3)
    w["mconvb"] = cols(both("conv1d_bias", "conv1db_bias"))
    xp, dp = both("x_proj_w", "x_projb_w"), both("dt_proj_w", "dt_projb_w")
    t, u = z(128, 2, 2, 128), z(128, 2, 2, 128)
    for e in range(2):
        for k in range(2):
            t[:, e, k, 0:32] = xp[e, 64:96, 128 * k:128 * k + 128].T
            t[:, e, k, 64:128] = xp[e, 0:64, 128 * k:128 * k + 128].T
            u[64:128, e, k] = dp[e, 128 * k:128 * k + 128].T
    w["xproj"], w["dtproj"] = t, u
    w["dtb"] = cols(both("dt_proj_b", "dt_projb_b"))
    w["Alog"] = both("A_log", "A_b_log").reshape(2, 2, 128, 16).transpose(2, 0, 1, 3)
    w["Dp"] = cols(both("D", "D_b"))
    w["outp"] = C("out_proj_w").T.reshape(2, 128, 128).transpose(1, 0, 2)
    w["fftb"] = cols(C("fft_conv_b"))
    w["iw"], w["mu"] = E("integration_weight"), E("mu")
    t, u = z(128, 2, 128), z(128)
    t[:, 0, 0:64], t[:, 1, 0:64] = E("shared_w1")[:128], E("shared_w1")[128:]
    t[:, 0, 64:96], t[:, 0, 96:128] = E("halt_w1"), E("router_w1")
    u[0:64], u[64:96], u[96:128] = E("shared_b1"), E("halt_b1"), E("router_b1")
    w["m1"], w["m1b"] = t, u
    t = z(128, 8)
    t[96:128] = E("router_w2")
    w["rw2"], w["rb2"] = t, rows(E("router_b2"))
    t = z(128, 128)
    t[64:96] = np.tile(E("halt_w2"), (1, 128))
    w["hw2"], w["hb2"] = t, rows(E("halt_b2"))
    w["e1"] = E("expert_w1").reshape(8, 2, 128, 64).transpose(2, 1, 0, 3)
    w["e1b"] = E("expert_b1").reshape(4, 128).T
    w["e2"] = E("expert_w2").reshape(4, 128, 384).transpose(1, 0, 2)
    t = z(128, 2, 384)
    t[0:8, 0], t[8:16, 1] = E("expert_b2"), E("expert_b2")
    w["e2b"] = t
    t = z(128, 384)
    t[0:64] = E("shared_w2")
    w["s2"], w["s2b"], w["sw"] = t, cols(E("shared_b2")), rows(E("shared_weight"))
    w["r1"], w["r1b"] = E("refine_w1"), cols(E("refine_b1"))
    w["r2"], w["r2b"] = E("refine_w2").reshape(2, 128, 128).transpose(1, 0, 2), E("refine_b2")
    for name, c in WEIGHTS:
        assert w[name].size == 128 * c, (name, w[name].shape)
    arrays = {"w": np.concatenate([w[name].reshape(128, -1) for name, _ in WEIGHTS], 1)}
    arrays["prep"] = np.concatenate([A("Wq"), A("Wk"), A("Wv"), F("W_r").T, F("W_k").T], 1)
    arrays["taps"] = np.concatenate([rows(A("conv_w_" + n).T) for n in "qkv"], 1)
    arrays["fw"] = C("fft_conv_w").transpose(2, 1, 0).reshape(TAPS, 4, 128, 512).transpose(2, 0, 1, 3).reshape(128, -1)
    arrays["x"] = A("hidden_states").transpose(0, 2, 1)
    arrays["tab"] = np.concatenate(list(shape_tables().values()), 1)
    arrays["sel"] = selector_tables()
    arrays["time"], arrays["fwd"], arrays["inv"] = dft_tables()
    return {k: np.ascontiguousarray(v) for k, v in arrays.items()}


def kernel(**inputs):
    import numpy as _np
    import concourse.bacc as _bacc
    from concourse import mybir as _mybir
    from concourse.bass_utils import run_bass_kernel_spmd as _run

    nc = _bacc.Bacc("TRN2", target_bir_lowering=False, num_devices=1, dynamic_dma_scratch_size=1024)
    arrays, d = {}, {}
    for name, a in lay_out(inputs, _np).items():
        arrays[f"in_{name}_dram"] = a
        d[name] = nc.dram_tensor(f"in_{name}_dram", a.shape, _mybir.dt.from_np(a.dtype), kind="ExternalInput").ap()
    d["folded"] = nc.dram_tensor("folded_dram", (128, TAPS * 2048), F32, kind="Internal").ap()
    out = nc.dram_tensor("out_0_dram", (B, D, L), F32, kind="ExternalOutput").ap()
    build(nc, d, out)
    r = _run(nc, [arrays], core_ids=[0])
    return r.results[0]["out_0_dram"].transpose(0, 2, 1)
```

```python
import concourse.bass as bass
from concourse import mybir
from contextlib import ExitStack
import numpy as np

F32 = mybir.dt.float32
BF16 = mybir.dt.bfloat16
ALU = mybir.AluOpType
ACT = mybir.ActivationFunctionType
AXX = mybir.AxisListType.X

B, L, D = 8, 512, 128
H, DK, CH = 4, 32, 32
NCH = L // CH
FIR_S, FIR_L = 5, 64
NS = 16
NT = L // 128
TAPS = 5
NF = L // 2 + 3
NC = NF + 4
NE, HE = 8, 64
PAD = 4
DWORK = 39
SP_CAP = 40.0


def shape_tables():
    p = np.arange(128)
    blk = (p[:, None] // 32 == p[None, :] // 32).astype(np.float32)
    i, j = p[:, None] % 32, np.arange(32)[None, :]
    t = {"ident": np.eye(128), "ones_mean": np.full((128, 128), 1 / 128), "head_ones": blk, "head_mean": blk / 32,
         "neg_blk": -blk, "ident_st": (i == j)}
    for s in (1, 2, 4, 8):
        off = ((i // (2 * s) == j // (2 * s)) & (i // s % 2 == 1) & (j // s % 2 == 0)).astype(np.float32)
        t["neg_level1" if s == 1 else f"level{s}"] = -off if s == 1 else off
    t["row_low"], t["row_high"] = (p % 32 < 16), (p % 32 >= 16)
    t["causal_bd"] = (blk.reshape(128, 4, 32) * (i <= j)[:, None, :]).reshape(128, 128)
    sel = np.zeros((128, 4, 16))
    for s in range(4):
        for h in range(4):
            sel[32 * h:32 * h + 32, s, 4 * s + h] = 1 / 32
    t["stat_sel"] = sel.reshape(128, 64)
    prob = np.zeros((128, 4, 128))
    for h in range(4):
        for k in range(4):
            prob[4 * h + k, k, 32 * h:32 * h + 32] = 1
    t["prob_sel"] = prob.reshape(128, 512)
    t["floor"] = np.tile(np.array([0.08, 0.08, 0, 0]), (128, 4))
    t["dec"] = np.tile(np.arange(8, 0, -1.0), (128, 1))
    wsel = np.zeros((128, 2, 128))
    wsel[16, 0], wsel[17, 1] = 1, 1
    t["wsel"] = wsel.reshape(128, 256)
    return {k: np.asarray(v, np.float32).reshape(128, -1) for k, v in t.items()}


def selector_tables():
    s = np.zeros((128, 32, 128), np.float32)
    for n in range(32):
        s[[n, 32 + n, 64 + n], n] = 1
    m = np.zeros((128, 2, 4, 128), np.float32)
    for r in range(2):
        for t in range(4):
            for e in range(2):
                m[8 * r + 2 * t + e, r, t, 64 * e:64 * e + 64] = 1
    return np.concatenate([s.reshape(128, -1), m.reshape(128, -1)], 1)


def dft_tables():
    k = np.arange(L)
    a = 2 * np.pi * ((k[:, None] * k[None]) % L) / L
    time = np.stack([np.cos(a), np.sin(a)])[:, :, :NF].reshape(2, NT, 128, NF).transpose(2, 0, 1, 3)
    k = np.arange(256)
    a = 2 * np.pi * ((k[:, None] * k[None]) % 256) / 256
    c, s = np.cos(a), np.sin(a)
    fwd = np.block([[c, s], [-s, c]])
    inv = np.block([[c, s], [-s, c]]) / (256 * L)
    lay = lambda m: m.reshape(4, 128, 512).transpose(1, 0, 2)
    return (np.ascontiguousarray(time.reshape(128, -1), np.float32),
            np.ascontiguousarray(lay(fwd).reshape(128, -1), np.float32),
            np.ascontiguousarray(lay(inv).reshape(128, -1), np.float32))


WEIGHTS = [
    ("Wb", 128), ("fir_s", 5), ("fir_l", 64),
    ("W1x", 128), ("W1s", 512), ("b1", 1), ("W2", 4), ("b2", 4), ("temp", 1), ("res", 4), ("rms", 1), ("Wo", 128),
    ("Wvf", 128), ("mur", 1), ("muk", 1),
    ("inp", 512), ("mconv", 16), ("mconvb", 4), ("xproj", 512), ("dtproj", 512), ("dtb", 4), ("Alog", 64), ("Dp", 4),
    ("outp", 256), ("fftb", 4),
    ("iw", 1), ("mu", 1), ("m1", 256), ("m1b", 1), ("rw2", 8), ("rb2", 8), ("hw2", 128), ("hb2", 1),
    ("e1", 1024), ("e1b", 4), ("e2", 1536), ("e2b", 768), ("s2", 384), ("s2b", 3), ("sw", 1),
    ("r1", 256), ("r1b", 2), ("r2", 256), ("r2b", 1),
]
WAT, _n = {}, 0
for _name, _c in WEIGHTS:
    WAT[_name] = (_n, _c)
    _n += _c
WCOLS = _n
TAT, _n = {}, 0
for _name, _v in shape_tables().items():
    TAT[_name] = (_n, _v.shape[1])
    _n += _v.shape[1]
TCOLS = _n


class Sems(dict):

    def __init__(self, nc, stack, stage):
        self.nc, self.stack, self.stage = nc, stack, stage

    def __missing__(self, name):
        self[name] = self.stack.enter_context(self.nc.semaphore(f"{self.stage}_{name}"))
        return self[name]


def linker(eng, sem):
    n = [0]

    def link(ins):
        n[0] += 1
        ins.then_inc(sem, 1)
        eng.wait_ge(sem, n[0])
    return link


class Mem:

    def __init__(self, nc, ctx):
        sb = lambda n, s, d=F32: ctx.enter_context(nc.sbuf_tensor(n, s, d))
        self.w = sb("weights", [128, WCOLS])
        self.t = sb("tables", [128, TCOLS])
        self.sel = sb("selectors", [128, 40, 128], BF16)
        self.inv = sb("dft_chan_inv", [128, 4, 512])
        self.qkvw = sb("qkv_tap_w", [128, 3, 4, 128])
        self.mixw = sb("token_mix_w", [128, 4, 128])
        self.small = sb("small", [128, 128])
        self.x = sb("x", [128, L])
        self.hp = sb("h_padded", [128, PAD + L])
        self.xd = sb("x_experts", [128, L])
        self.hd = sb("h_experts", [128, L])
        self.work = sb("work", [128, 73, L])
        self.dft = self.work[:, DWORK:DWORK + 5, :].rearrange("p a n -> p (a n)")[:, 0:2 * NT * NF].rearrange("p (a t n) -> p a t n", a=2, t=NT)
        self.fw = self.work[:, DWORK + 5:DWORK + 25, :].rearrange("p (t k) n -> p t k n", t=TAPS)
        self.combos = self.work[:, DWORK + 25:DWORK + 34, :].rearrange("p a n -> p (a n)")[:, 0:16 * NC].rearrange("p (q k n) -> p q k n", q=4, k=4)
        self.ps = [ctx.enter_context(nc.psum_tensor(f"ps{i}", [128, 512], F32)) for i in range(8)]

    def W(self, name):
        a, n = WAT[name]
        return self.w[:, a:a + n]

    def T(self, name):
        a, n = TAT[name]
        return self.t[:, a:a + n]

    def s(self, i):
        return self.work[:, i, :]

    @property
    def h(self):
        return self.hp[:, PAD:PAD + L]


SM = {"temp": 0, "res": 1, "pconst": 5, "sw": 21, "omsw": 22, "A": 23, "one_mu_r": 87, "one_mu_k": 88}


COMPUTE = ("tensor", "vector", "scalar", "gpsimd")


def emit(eng, parts):
    due = [(next(p, None), i, p) for i, p in enumerate(parts)]
    due = [x for x in due if x[0] is not None]
    while due:
        _, i, p = due.pop(due.index(min(due, key=lambda x: x[:2])))
        t = next(p, None)
        if t is not None:
            due.append((t, i, p))


class Stream:

    def __init__(self, *stages, pace=1.0):
        self.stages, self.pace = stages, pace
        self.engines = [e for e in COMPUTE if any(e in progs for _, (_, progs) in stages)]

    def program(self, engine, eng, sems, met):
        for i, (start, (_, progs)) in enumerate(self.stages):
            if i and engine in self.engines:
                yield start
                eng.drain().then_inc(met, 1)
                eng.wait_ge(met, i * len(self.engines))
            if engine in progs:
                for t in progs[engine](eng, sems[i]):
                    yield start + self.pace * t


def run_block(nc, *streams):
    streams = [x if isinstance(x, Stream) else Stream((0, x)) for x in streams]
    with ExitStack() as st:
        sems = [[Sems(nc, st, name) for _, (name, _) in x.stages] for x in streams]
        mets = [st.enter_context(nc.semaphore(f"stage_met_{i}")) for i in range(len(streams))]

        with nc.Block() as block:
            for engine, open_ in (("sync", block.sync), ("tensor", block.tensor), ("vector", block.vector),
                                  ("scalar", block.scalar), ("gpsimd", block.gpsimd)):
                if any(engine in progs for x in streams for _, (_, progs) in x.stages):
                    open_(lambda eng, engine=engine: emit(eng, [x.program(engine, eng, sems[i], mets[i]) for i, x in enumerate(streams)]))
        nums = [x.num for group in sems for S in group for x in S.values()] + [x.num for x in mets]
        nc.gpsimd.sem_clear(range(min(nums), max(nums) + 1))
        nc.all_engine_barrier()


def ln_tensor(nc, pe, S, m, x, scr, banks, loaded=0):
    yield 0
    if loaded:
        pe.wait_ge(S["x_loaded"], loaded)
    nc.tensor.matmul(m.ps[banks[0]][:, :], m.T("ones_mean"), x, start=True, stop=True).then_inc(S["ln_mean"], 1)
    yield 3
    pe.wait_ge(S["ln_squared"], 1)
    nc.tensor.matmul(m.ps[banks[1]][:, :], m.T("ones_mean"), m.s(scr[1]), start=True, stop=True).then_inc(S["ln_var"], 1)
    yield 8


def ln_vector(nc, v, S, m, x, h, scr, banks):
    yield 1
    v.wait_ge(S["ln_mean"], 1)
    nc.vector.tensor_tensor(m.s(scr[0]), x, m.ps[banks[0]][:, :], ALU.subtract).then_inc(S["ln_centred"], 1)
    yield 7
    v.wait_ge(S["ln_centred"], 1)
    v.wait_ge(S["ln_rstd"], 1)
    nc.vector.tensor_tensor(h, m.s(scr[0]), m.s(scr[2]), ALU.mult).then_inc(S["h_ready"], 1)


def ln_scalar(nc, a, S, m, scr, banks):
    yield 2
    a.wait_ge(S["ln_centred"], 1)
    nc.scalar.activation(m.s(scr[1]), m.s(scr[0]), ACT.Square).then_inc(S["ln_squared"], 1)
    yield 4
    a.wait_ge(S["ln_var"], 1)
    nc.scalar.activation(m.s(scr[2]), m.ps[banks[1]][:, :], ACT.Ln, bias=m.small[:, 120:121]).then_inc(S["ln_log"], 1)
    yield 5
    a.wait_ge(S["ln_log"], 1)
    nc.scalar.activation(m.s(scr[2]), m.s(scr[2]), ACT.Exp, scale=-0.5).then_inc(S["ln_rstd"], 1)


def setup(nc, m, d):
    taps = m.work[:, 24:27, :]
    sel32 = m.work[:, 27:37, :]
    prep = m.work[:, 37:39, :].rearrange("p a n -> p (a n)")
    sm = m.small

    def sync(sp, S):
        yield 0
        sp.dma_start(m.w[:, :], d["w"]).then_inc(S["weights"], 16)
        sp.dma_start(m.t[:, :], d["tab"]).then_inc(S["weights"], 16)
        sp.dma_start(taps, d["taps"].rearrange("p (a n) -> p a n", a=3)).then_inc(S["weights"], 16)
        sp.dma_start(prep[:, 0:640], d["prep"]).then_inc(S["weights"], 16)
        sp.dma_start(sel32, d["sel"].rearrange("p (a n) -> p a n", a=10)).then_inc(S["selectors"], 16)
        sp.dma_start(m.inv[:, :, :], d["inv"].rearrange("p (a n) -> p a n", a=4)).then_inc(S["inverse_dft"], 16)
        sp.wait_ge(S["inverse_dft"], 16)

    def vector(v, S):
        yield 0
        link = linker(v, S["chain"])
        link(nc.vector.memset(m.hp[:, 0:PAD], 0.0))
        link(nc.vector.memset(sm[:, 119:128], 0.0))
        link(nc.vector.memset(sm[:, 120:121], 1e-5))
        link(nc.vector.memset(sm[:, 121:122], 1e-12))
        link(nc.vector.memset(sm[:, 122:123], 1.0))
        v.wait_ge(S["weights"], 64)
        for p in range(3):
            for j in range(4):
                nc.vector.tensor_tensor(m.qkvw[:, p, j, :], prep[:, 128 * p:128 * p + 128], taps[:, p, 128 * j:128 * j + 128], ALU.mult)
        for i, (w, mu, one_mu) in enumerate(((prep[:, 384:512], "mur", "one_mu_r"), (prep[:, 512:640], "muk", "one_mu_k"))):
            c = SM[one_mu]
            nc.vector.tensor_scalar(m.mixw[:, 2 * i, :], w, m.W(mu)[:, 0:1], None, ALU.mult)
            link(nc.vector.tensor_scalar(sm[:, c:c + 1], m.W(mu)[:, 0:1], -1.0, 1.0, ALU.mult, ALU.add))
            nc.vector.tensor_scalar(m.mixw[:, 2 * i + 1, :], w, sm[:, c:c + 1], None, ALU.mult)
        link(nc.vector.tensor_scalar(sm[:, 89:90], m.W("temp"), SP_CAP, None, ALU.min))
        nc.vector.tensor_scalar(sm[:, 90:91], m.W("temp"), 1.0, None, ALU.mult).then_inc(S["sp_in"], 1)
        v.wait_ge(S["exps"], 6)
        link(nc.vector.tensor_tensor(sm[:, 92:93], m.W("temp"), sm[:, 91:92], ALU.max))
        link(nc.vector.tensor_scalar(sm[:, 92:93], sm[:, 92:93], 1e-6, None, ALU.add))
        link(nc.vector.reciprocal(sm[:, 0:1], sm[:, 92:93]))
        link(nc.vector.tensor_scalar(sm[:, 93:98], sm[:, 93:98], 1.0, None, ALU.add))
        link(nc.vector.reciprocal(sm[:, 93:98], sm[:, 93:98]))
        link(nc.vector.tensor_copy(sm[:, 1:5], sm[:, 93:97]))
        link(nc.vector.tensor_copy(sm[:, 21:22], sm[:, 97:98]))
        link(nc.vector.tensor_scalar(sm[:, 22:23], sm[:, 21:22], -1.0, 1.0, ALU.mult, ALU.add))
        link(nc.vector.tensor_copy(sm[:, 5:21], m.T("floor")))
        pc = sm[:, 5:21].rearrange("p (h k) -> p h k", k=4)[:, :, 0]
        link(nc.vector.tensor_tensor(pc, pc, sm[:, 1:5], ALU.add))
        link(nc.vector.tensor_scalar(sm[:, 23:87], sm[:, 23:87], -1.0, None, ALU.mult))
        v.wait_ge(S["selectors"], 16)
        nc.vector.tensor_copy(m.sel[:, :, :].rearrange("p a n -> p (a n)"), sel32.rearrange("p a n -> p (a n)"))

    def scalar(a, S):
        yield 0
        a.wait_ge(S["sp_in"], 1)
        nc.scalar.activation(sm[:, 90:91], sm[:, 89:90], ACT.Exp).then_inc(S["exps"], 1)
        nc.scalar.activation(sm[:, 93:97], m.W("res"), ACT.Exp, scale=-1.0).then_inc(S["exps"], 1)
        nc.scalar.activation(sm[:, 97:98], m.W("sw"), ACT.Exp, scale=-1.0).then_inc(S["exps"], 1)
        nc.scalar.activation(sm[:, 23:87], m.W("Alog"), ACT.Exp).then_inc(S["exps"], 1)
        a.wait_ge(S["exps"], 4)
        nc.scalar.activation(sm[:, 91:92], sm[:, 90:91], ACT.Ln, bias=sm[:, 122:123]).then_inc(S["exps"], 2)

    return "setup", {"sync": sync, "vector": vector, "scalar": scalar}


QN, KN, KB, VS, VB, BETA = 3, 4, 5, 6, 8, 9
RQ, RK, KBT, VT, KT = 10, 13, 11, 12, 13
KBD, GBD, KTBD, ATTBD = 15, 19, 23, 27
NATBD, XTBD = 31, 35
PTBD, ATT_ST = 15, 19
XST, ZST, XTST, ST_ALL, WST = 0, 1, 2, 4, 10
AU = 10
XR_ST, WU_ST = 0, 9
SHORT, DELTA, FL = 8, 5, 14


def bd(m, slot):
    return m.work[:, slot:slot + 4, :].rearrange("p a n -> p (a n)").rearrange("p (c h t) -> p c h t", c=NCH, h=H)


def spread(ap2d):
    return ap2d.rearrange("p (c t) -> p c t", t=32).unsqueeze(2).to_broadcast([128, NCH, H, 32])


def over_chunks(mask):
    return mask.rearrange("p (h t) -> p h t", h=H).unsqueeze(1).to_broadcast([128, NCH, H, 32])


def st_over_chunks(mask):
    return mask.unsqueeze(1).to_broadcast([128, NCH, 32])


def l0_inputs(nc, m, x_dram, b):
    vs = m.work[:, VS:VS + 2, :].rearrange("p a n -> p (a n)")[:, 64:64 + L]

    def sync(sp, S):
        yield 0
        sp.dma_start(m.x[:, :], x_dram[bass.ds(b, 1), :, :].rearrange("o c t -> (o c) t")).then_inc(S["x_loaded"], 16)

    def tensor(pe, S):
        yield 0
        yield from ln_tensor(nc, pe, S, m, m.x[:, :], (0, 1, 2), (0, 1), loaded=16)
        pe.wait_ge(S["h_ready"], 1)
        for p in range(3):
            for j in range(4):
                last = nc.tensor.matmul(m.ps[2 + p][:, :], m.qkvw[:, p, j, :], m.hp[:, PAD - 3 + j:PAD - 3 + j + L],
                                        start=(j == 0), stop=(j == 3))
            last.then_inc(S["qkv"], 1)
            yield 12 + 3 * p
        nc.tensor.matmul(m.ps[0][:, :], m.W("Wb"), m.h, start=True, stop=True).then_inc(S["qkv"], 1)
        yield 22
        for i, slot in enumerate((0, 1)):
            pe.wait_ge(S["squares"], i + 1)
            nc.tensor.matmul(m.ps[1 + i][:, :], m.T("head_ones"), m.s(slot), start=True, stop=True).then_inc(S["norms"], 1)

    def scalar(a, S):
        yield 0
        yield from ln_scalar(nc, a, S, m, (0, 1, 2), (0, 1))
        for p, out in enumerate((m.s(QN), m.s(KN), vs)):
            yield 12 + 3 * p
            a.wait_ge(S["qkv"], p + 1)
            nc.scalar.activation(out, m.ps[2 + p][:, :], ACT.Silu).then_inc(S["silu"], 1)
        a.wait_ge(S["qkv"], 4)
        nc.scalar.activation(m.s(BETA), m.ps[0][:, :], ACT.Tanh, scale=0.5).then_inc(S["tanh"], 1)
        a.wait_ge(S["silu"], 2)
        a.wait_ge(S["h_ready"], 1)
        nc.scalar.activation(m.s(0), m.s(QN), ACT.Square).then_inc(S["squares"], 1)
        nc.scalar.activation(m.s(1), m.s(KN), ACT.Square).then_inc(S["squares"], 1)
        yield 23
        for i, slot in enumerate((RQ, RK)):
            a.wait_ge(S["norms"], i + 1)
            nc.scalar.activation(m.s(slot), m.ps[1 + i][:, :], ACT.Ln, bias=m.small[:, 121:122]).then_inc(S["logs"], 1)
        for i, slot in enumerate((RQ, RK)):
            a.wait_ge(S["logs"], i + 1)
            nc.scalar.activation(m.s(slot), m.s(slot), ACT.Exp, scale=-0.5).then_inc(S["rnorm"], 1)

    def vector(v, S):
        yield 0
        yield from ln_vector(nc, v, S, m, m.x[:, :], m.h, (0, 1, 2), (0, 1))
        link = linker(v, S["chain"])
        nc.vector.memset(m.work[:, VS, 0:64], 0.0)
        yield 20
        v.wait_ge(S["tanh"], 1)
        link(nc.vector.tensor_scalar(m.s(BETA), m.s(BETA), 0.5, 0.5, ALU.mult, ALU.add))
        v.wait_ge(S["silu"], 3)
        link(nc.vector.tensor_tensor(m.s(VB), vs, m.s(BETA), ALU.mult))
        nc.vector.transpose(m.s(VT), m.s(VB))
        yield 28
        v.wait_ge(S["rnorm"], 1)
        v.wait_ge(S["squares"], 2)
        nc.vector.tensor_tensor(m.s(QN), m.s(QN), m.s(RQ), ALU.mult).then_inc(S["qn"], 1)
        v.wait_ge(S["rnorm"], 2)
        link(nc.vector.tensor_tensor(m.s(KN), m.s(KN), m.s(RK), ALU.mult))
        link(nc.vector.tensor_tensor(m.s(KB), m.s(KN), m.s(BETA), ALU.mult))
        nc.vector.transpose(m.s(KT), m.s(KN))
        nc.vector.transpose(m.s(KBT), m.s(KB))
        nc.vector.tensor_tensor(bd(m, KBD), spread(m.s(KN)), over_chunks(m.T("head_ones")), ALU.mult)

    return "qkv", {"sync": sync, "tensor": tensor, "vector": vector, "scalar": scalar}


def l0_delta(nc, m):
    vp = m.work[:, VS:VS + 2, :].rearrange("p a n -> p (a n)")
    cols = lambda n: slice(32 * n, 32 * n + 32)
    GRP = NCH // 2
    gcol = lambda g: slice(256 * g, 256 * g + 256)
    chunks = lambda g: range(GRP * g, GRP * g + GRP)
    GRAM_PS, Z_PS, Y_PS = (0, 1), (2, 3), (4, 0)
    XR_PS, AXR_PS, WU_PS, KWU_PS, AWU_PS = (1, 0), (2, 3), (4, 0), (1, 2), (3, 4)
    CHAIN_PS, GS_PS = 0, 3
    LEVELS = (2, 4, 8)
    T_LEVEL, T_XR, T_AXR, T_WU, T_KWU = [8 + 14 * i for i in range(3)], 50, 57, 64, 71
    T_CHAIN = [85 + 0.75 * n for n in range(NCH)]
    T_O = 97
    flat = lambda slot, n: bd(m, slot)[:, n, :, :].rearrange("p h t -> p (h t)")
    ch = lambda ap: ap.rearrange("p (c t) -> p c t", t=32)
    gmask = lambda name: m.T(name).unsqueeze(1).to_broadcast([128, GRP, 32])
    state = lambda n: m.s(ST_ALL)[:, cols(n)]
    halves = lambda bank: m.ps[bank][:, :].rearrange("p (a t) -> p a t", a=2)
    both = lambda bank, n: halves(bank)[:, :, cols(n % GRP)]
    QK = m.work[:, QN:KB + 1:KB - QN, :]
    R = m.work[:, KBT:KBT + 2, :]
    XR = m.work[:, XR_ST:XR_ST + 2, :]
    WU = m.work[:, WU_ST:WU_ST + 2, :]
    low, high = m.T("row_low")[:, 0:1], m.T("row_high")[:, 0:1]

    def expand(src, dst, g, h0, h1, mask):
        out = bd(m, dst)[:, GRP * g:GRP * g + GRP, h0:h1, :]
        return out, ch(src).unsqueeze(2).to_broadcast([128, GRP, h1 - h0, 32]), \
            m.T(mask).rearrange("p (h t) -> p h t", h=H)[:, h0:h1, :].unsqueeze(1).to_broadcast([128, GRP, h1 - h0, 32])

    def tensor(pe, S):
        yield 0

        def stacked(bank, slot, rhs, g):
            for n in chunks(g):
                last = nc.tensor.matmul(m.ps[bank][:, cols(n)], flat(slot, n), rhs[:, cols(n)], start=True, stop=True)
            return last

        def paired(bank, slot, rhs, g):
            for n in chunks(g):
                last = nc.tensor.matmul(both(bank, n), flat(slot, n), rhs[:, :, cols(n)], start=True, stop=True)
            return last

        for g in range(2):
            paired(GRAM_PS[g], KBD, QK, g).then_inc(S["gram"], 1)
        for i in range(len(LEVELS)):
            yield T_LEVEL[i]
            for g in range(2):
                pe.wait_ge(S["xt_dve"], 2 * i + g + 1)
                pe.wait_ge(S["xt_act"], 2 * i + g + 1)
                stacked(Z_PS[g], NATBD, m.s(XST), g).then_inc(S["z"], 1)
            yield T_LEVEL[i] + 7
            for g in range(2):
                pe.wait_ge(S["z_plus"], 2 * i + g + 1)
                if i == 0 and g == 1:
                    pe.wait_ge(S["att_sb"], 1)
                stacked(Y_PS[g], XTBD, m.s(ZST), g).then_inc(S["y"], 1)
        yield T_XR
        pe.wait_ge(S["att_sb"], 2)
        for g in range(2):
            pe.wait_ge(S["xt_dve"], 2 * len(LEVELS) + g + 1)
            pe.wait_ge(S["xt_act"], 2 * len(LEVELS) + g + 1)
            paired(XR_PS[g], XTBD, R, g).then_inc(S["xr"], 1)
        yield T_AXR
        for g in range(2):
            pe.wait_ge(S["xr_sb"], g + 1)
            paired(AXR_PS[g], NATBD, XR, g).then_inc(S["axr"], 1)
        yield T_WU
        for g in range(2):
            pe.wait_ge(S["rest"], g + 1)
            paired(WU_PS[g], XTBD, R, g).then_inc(S["wu"], 1)
        yield T_KWU
        pe.wait_ge(S["kt_bd"], 1)
        pe.wait_ge(S["attn_bd"], 1)
        for g in range(2):
            pe.wait_ge(S["wu_sb"], g + 1)
            paired(KWU_PS[g], KTBD, WU, g).then_inc(S["kwu"], 1)
        for g in range(2):
            paired(AWU_PS[g], ATTBD, WU, g).then_inc(S["awu"], 1)
        pe.wait_ge(S["ku_sb"], 1)
        pe.wait_ge(S["pt_dve"], 2)
        pe.wait_ge(S["pt_act"], 2)
        for n in range(1, NCH):
            yield T_CHAIN[n]
            if n > 1:
                pe.wait_ge(S["state"], n - 1)
            if n < NCH - 1:
                nc.tensor.matmul(m.ps[CHAIN_PS][:, cols(n)], flat(PTBD, n), state(n), start=True, stop=True).then_inc(S["chain"], 1)
            if n == 1:
                pe.wait_ge(S["au_sb"], 1)
            if n in (1, GRP):
                pe.wait_ge(S["g_bd"], n // GRP + 1)
            last = nc.tensor.matmul(m.ps[GS_PS][:, cols(n)], flat(GBD, n), state(n), start=True, stop=True)
        last.then_inc(S["o"], 1)

    def vector(v, S):
        yield 0
        link = linker(v, S["link"])
        taps = [(m.s(SHORT), vp[:, 64 - (FIR_S - 1) + k:64 - (FIR_S - 1) + k + L], m.W("fir_s")[:, k:k + 1], k == 0) for k in range(FIR_S)] + \
            [(m.s(FL), vp[:, 64 - (FIR_L - 1) + k:64 - (FIR_L - 1) + k + L], m.W("fir_l")[:, k:k + 1], k == 0) for k in range(FIR_L)]
        done = [0]

        def fir_tap(k):
            for acc, src, w, first in taps[done[0]:done[0] + k]:
                if first:
                    nc.vector.tensor_scalar(acc, src, w, None, ALU.mult).then_inc(S["fir_acc"], 1)
                else:
                    v.wait_ge(S["fir_acc"], done[0])
                    nc.vector.scalar_tensor_tensor(acc, src, w, acc, ALU.mult, ALU.add).then_inc(S["fir_acc"], 1)
                done[0] += 1

        fir_tap(6)
        for g in range(2):
            gc = gcol(g)
            v.wait_ge(S["gram"], g + 1)
            kk = halves(GRAM_PS[g])[:, 1, :]
            nc.vector.tensor_tensor(*expand(kk, NATBD, g, 0, H, "neg_blk"), ALU.mult)
            link(nc.vector.transpose(m.s(ZST)[:, gc], kk))
            link(nc.vector.tensor_tensor(ch(m.s(ZST)[:, gc]), ch(m.s(ZST)[:, gc]), gmask("neg_level1"), ALU.mult))
            link(nc.vector.tensor_tensor(ch(m.s(XST)[:, gc]), ch(m.s(ZST)[:, gc]), gmask("ident_st"), ALU.add))
            nc.vector.transpose(m.s(XTST)[:, gc], m.s(XST)[:, gc]).then_inc(S["xt"], 1)
            v.wait_ge(S["xt"], g + 1)
            nc.vector.tensor_tensor(*expand(m.s(XTST)[:, gc], XTBD, g, 0, 2, "head_ones"), ALU.mult).then_inc(S["xt_dve"], 1)
        for i, s in enumerate(LEVELS):
            yield T_LEVEL[i]
            fir_tap(4)
            for g in range(2):
                gc = gcol(g)
                v.wait_ge(S["z"], 2 * i + g + 1)
                link(nc.vector.tensor_tensor(ch(m.s(WST)[:, gc]), ch(m.ps[Z_PS[g]][:, gc]), gmask(f"level{s}"), ALU.mult))
                nc.vector.tensor_tensor(ch(m.s(ZST)[:, gc]), ch(m.s(WST)[:, gc]), gmask("ident_st"), ALU.add).then_inc(S["z_plus"], 1)
            yield T_LEVEL[i] + 7
            fir_tap(3)
            for g in range(2):
                gc = gcol(g)
                v.wait_ge(S["y"], 2 * i + g + 1)
                v.wait_ge(S["xt_act"], 2 * i + g + 1)
                nc.vector.transpose(m.s(XTST)[:, gc], m.ps[Y_PS[g]][:, gc]).then_inc(S["xt"], 1)
                if s < LEVELS[-1]:
                    nc.vector.tensor_copy(m.s(XST)[:, gc], m.ps[Y_PS[g]][:, gc])
                v.wait_ge(S["xt"], 2 * i + g + 3)
                nc.vector.tensor_tensor(*expand(m.s(XTST)[:, gc], XTBD, g, 0, 2, "head_ones"), ALU.mult).then_inc(S["xt_dve"], 1)
        yield T_XR
        fir_tap(7)
        yield T_AXR
        fir_tap(5)
        for g in range(2):
            v.wait_ge(S["axr"], g + 1)
            nc.vector.scalar_tensor_tensor(R[:, :, gcol(g)], halves(AXR_PS[g]), high, R[:, :, gcol(g)], ALU.mult, ALU.add).then_inc(S["rest"], 1)
        yield T_WU
        fir_tap(7)
        yield T_KWU
        fir_tap(5)
        for g in range(2):
            gc = gcol(g)
            v.wait_ge(S["kwu"], g + 1)
            link(nc.vector.transpose(m.s(XST)[:, gc], halves(KWU_PS[g])[:, 0, :]))
            nc.vector.scalar_tensor_tensor(ch(m.s(XTST)[:, gc]), ch(m.s(XST)[:, gc]), -1.0, gmask("ident_st"), ALU.mult, ALU.add).then_inc(S["pt"], 1)
            v.wait_ge(S["pt"], g + 1)
            nc.vector.tensor_tensor(*expand(m.s(XTST)[:, gc], PTBD, g, 0, 2, "head_ones"), ALU.mult).then_inc(S["pt_dve"], 1)
        for g in range(2):
            gc = gcol(g)
            v.wait_ge(S["awu"], g + 1)
            link(nc.vector.transpose(m.s(XST)[:, gc], halves(AWU_PS[g])[:, 0, :]))
            nc.vector.tensor_tensor(m.s(ZST)[:, gc], m.s(QN)[:, gc], m.s(XST)[:, gc], ALU.subtract).then_inc(S["g_st"], 1)
        for n in range(1, NCH - 1):
            yield T_CHAIN[n]
            if n in (1, GRP - 1):
                v.wait_ge(S["ku_sb"], n // (GRP - 1) + 1)
            v.wait_ge(S["chain"], n)
            nc.vector.tensor_tensor(state(n + 1), state(n + 1), m.ps[CHAIN_PS][:, cols(n)], ALU.add).then_inc(S["state"], 1)
            fir_tap(1)
        yield T_O
        fir_tap(len(taps))
        v.wait_ge(S["o"], 1)
        v.wait_ge(S["au_sb"], 2)
        link(nc.vector.tensor_tensor(m.s(AU)[:, 32:L], m.s(AU)[:, 32:L], m.ps[GS_PS][:, 32:L], ALU.add))
        nc.vector.transpose(m.s(DELTA), m.s(AU))

    def scalar(a, S):
        yield 0
        def expand_act(src, dst, g, sem):
            for h in (2, 3):
                last = nc.scalar.activation(bd(m, dst)[:, GRP * g:GRP * g + GRP, h, :], ch(src), ACT.Copy,
                                            scale=m.T("head_ones")[:, 32 * h:32 * h + 1])
            last.then_inc(sem, 1)

        for i in range(len(LEVELS) + 1):
            if i:
                yield T_LEVEL[i - 1] + 7
            for g in range(2):
                a.wait_ge(S["xt"], 2 * i + g + 1)
                if i:
                    a.wait_ge(S["y"], 2 * (i - 1) + g + 1)
                expand_act(m.s(XTST)[:, gcol(g)], XTBD, g, S["xt_act"])
                if i == 0:
                    nc.scalar.activation(m.s(ATT_ST)[:, gcol(g)], halves(GRAM_PS[g])[:, 0, :], ACT.Copy).then_inc(S["att_sb"], 1)
        yield T_AXR
        for g in range(2):
            a.wait_ge(S["xr"], g + 1)
            nc.scalar.activation(XR[:, :, gcol(g)], halves(XR_PS[g]), ACT.Copy, scale=low).then_inc(S["xr_sb"], 1)
        yield T_WU
        for g in range(2):
            a.wait_ge(S["wu"], g + 1)
            nc.scalar.activation(WU[:, :, gcol(g)], halves(WU_PS[g]), ACT.Copy).then_inc(S["wu_sb"], 1)
        yield T_KWU
        for g in range(2):
            a.wait_ge(S["pt"], g + 1)
            expand_act(m.s(XTST)[:, gcol(g)], PTBD, g, S["pt_act"])
            n0, n1 = GRP * g, min(GRP * g + GRP, NCH - 1)
            nc.scalar.activation(m.s(ST_ALL)[:, 32 * n0 + 32:32 * n1 + 32], halves(KWU_PS[g])[:, 1, 0:32 * (n1 - n0)], ACT.Copy).then_inc(S["ku_sb"], 1)
        for g in range(2):
            a.wait_ge(S["g_st"], g + 1)
            nc.scalar.activation(m.s(AU)[:, gcol(g)], halves(AWU_PS[g])[:, 1, :], ACT.Copy).then_inc(S["au_sb"], 1)

    def gpsimd(g_, S):
        yield 0
        nc.gpsimd.tensor_tensor(bd(m, KTBD), spread(m.s(KT)), over_chunks(m.T("head_ones")), ALU.mult).then_inc(S["kt_bd"], 1)
        g_.wait_ge(S["att_sb"], 2)
        nc.gpsimd.tensor_tensor(bd(m, ATTBD), spread(m.s(ATT_ST)), over_chunks(m.T("causal_bd")), ALU.mult).then_inc(S["attn_bd"], 1)
        yield T_KWU
        g_.wait_ge(S["attn_bd"], 1)
        for g in range(2):
            g_.wait_ge(S["g_st"], g + 1)
            nc.gpsimd.tensor_tensor(*expand(m.s(ZST)[:, gcol(g)], GBD, g, 0, H, "head_ones"), ALU.mult).then_inc(S["g_bd"], 1)

    return "delta", {"tensor": tensor, "vector": vector, "scalar": scalar, "gpsimd": gpsimd}


def l0_gate(nc, m):
    vs = m.work[:, VS:VS + 2, :].rearrange("p a n -> p (a n)")[:, 64:64 + L]
    streams = (m.s(SHORT), m.s(FL), m.s(DELTA), vs)
    ABS, SQ, ST, M2, HG = 15, 19, 23, 24, 25
    PRT, O, T1, T2 = 29, 30, 31, 32
    PB = (2, 3, 4, 0)
    tok = m.work[:, 33, :]
    lg, mx, pr = tok[:, 0:64], tok[:, 64:80], tok[:, 80:144]
    rs = tok[:, 144:160]
    j4 = lambda ap: ap.rearrange("p (g k) -> p g k", k=4)
    b16 = lambda ap: ap.unsqueeze(2).to_broadcast([128, 16, 4])

    def tensor(pe, S):
        yield 0
        sel = m.T("stat_sel")
        for s in range(4):
            nc.tensor.matmul(m.ps[0][0:16, :], sel[:, 16 * s:16 * s + 16], streams[s], start=(s == 0), stop=(s == 3))
        for s in range(4):
            pe.wait_ge(S["abs_sq"], 2 * s + 1)
            nc.tensor.matmul(m.ps[1][0:16, :], sel[:, 16 * s:16 * s + 16], m.s(ABS + s), start=(s == 0), stop=(s == 3))
            pe.wait_ge(S["abs_sq"], 2 * s + 2)
            last = nc.tensor.matmul(m.ps[2][0:16, :], sel[:, 16 * s:16 * s + 16], m.s(SQ + s), start=(s == 0), stop=(s == 3))
        last.then_inc(S["sums"], 1)
        for h in range(4):
            yield 16 + 2.2 * h
            if h == 0:
                pe.wait_ge(S["stats"], 4)
            bank = m.ps[3 + h % 2]
            if h >= 2:
                pe.wait_ge(S["gelu"], h - 1)
            nc.tensor.matmul(bank[:, :], m.W("W1x"), m.h, start=True, stop=False)
            nc.tensor.matmul(bank[:, :], m.W("W1s")[:, 128 * h:128 * h + 128], m.s(ST), start=False, stop=True).then_inc(S["hid"], 1)
        for h in range(4):
            yield 26 + 0.7 * h
            pe.wait_ge(S["gelu"], h + 1)
            for t in range(NT):
                c = 16 * t + 4 * h
                last = nc.tensor.matmul(m.ps[0][:, c:c + 4], m.s(HG + h)[:, 128 * t:128 * t + 128], m.W("W2"), start=True, stop=True)
        last.then_inc(S["logits"], 1)
        yield 32
        pe.wait_ge(S["probs"], 1)
        for t in range(NT):
            last = nc.tensor.transpose(m.ps[1][0:16, 128 * t:128 * t + 128], pr[:, 16 * t:16 * t + 16], m.T("ident"))
        last.then_inc(S["probs_t"], 1)
        yield 34
        pe.wait_ge(S["probs_sb"], 1)
        for k in range(4):
            nc.tensor.matmul(m.ps[PB[k]][:, :], m.T("prob_sel")[0:16, 128 * k:128 * k + 128], m.s(PRT)[0:16, :], start=True, stop=True).then_inc(S["prob_bc"], 1)
        yield 42
        pe.wait_ge(S["o_sq"], 1)
        nc.tensor.matmul(m.ps[1][:, :], m.T("head_mean"), m.s(T1), start=True, stop=True).then_inc(S["o_ms"], 1)
        yield 48
        pe.wait_ge(S["o_norm"], 1)
        nc.tensor.matmul(m.ps[2][:, :], m.W("Wo"), m.s(T2), start=True, stop=True).then_inc(S["proj"], 1)

    def scalar(a, S):
        yield 0
        for s in range(4):
            nc.scalar.activation(m.s(ABS + s), streams[s], ACT.Abs).then_inc(S["abs_sq"], 1)
            nc.scalar.activation(m.s(SQ + s), streams[s], ACT.Square).then_inc(S["abs_sq"], 1)
        a.wait_ge(S["sums"], 1)
        a.wait_ge(S["st_zero"], 1)
        nc.scalar.activation(m.s(M2)[0:16, :], m.ps[0][0:16, :], ACT.Square).then_inc(S["mean_sq"], 1)
        nc.scalar.activation(m.s(ST)[0:16, :], m.ps[0][0:16, :], ACT.Copy).then_inc(S["stats"], 1)
        nc.scalar.activation(m.s(ST)[64:80, :], m.ps[1][0:16, :], ACT.Copy).then_inc(S["stats"], 1)
        nc.scalar.activation(m.s(ST)[96:112, :], m.ps[2][0:16, :], ACT.Sqrt, scale=32.0).then_inc(S["stats"], 1)
        for h in range(4):
            yield 18 + 2.2 * h
            a.wait_ge(S["hid"], h + 1)
            nc.scalar.activation(m.s(HG + h), m.ps[3 + h % 2][:, :], ACT.Gelu, bias=m.W("b1")).then_inc(S["gelu"], 1)
        yield 30
        a.wait_ge(S["shifted"], 1)
        nc.scalar.activation(pr, lg, ACT.Exp).then_inc(S["exp"], 1)
        yield 33
        a.wait_ge(S["probs_t"], 1)
        nc.scalar.activation(m.s(PRT)[0:16, :], m.ps[1][0:16, :], ACT.Copy).then_inc(S["probs_sb"], 1)
        yield 41
        a.wait_ge(S["o"], 1)
        nc.scalar.activation(m.s(T1), m.s(O), ACT.Square).then_inc(S["o_sq"], 1)
        yield 43
        a.wait_ge(S["o_ms"], 1)
        nc.scalar.activation(m.s(T2), m.ps[1][:, :], ACT.Ln, bias=m.small[:, 120:121]).then_inc(S["o_ln"], 1)
        a.wait_ge(S["o_ln"], 1)
        nc.scalar.activation(m.s(T2), m.s(T2), ACT.Exp, scale=-0.5).then_inc(S["o_rstd"], 1)

    def vector(v, S):
        yield 0
        link = linker(v, S["chain"])
        nc.vector.memset(m.s(ST), 0.0).then_inc(S["st_zero"], 1)
        v.wait_ge(S["st_zero"], 1)
        v.wait_ge(S["mean_sq"], 1)
        v.wait_ge(S["stats"], 3)
        nc.vector.tensor_tensor(m.s(ST)[32:48, :], m.ps[2][0:16, :], m.s(M2)[0:16, :], ALU.subtract).then_inc(S["stats"], 1)
        yield 29
        v.wait_ge(S["logits"], 1)
        link(nc.vector.tensor_tensor(j4(lg), j4(m.ps[0][:, 0:64]), m.W("b2").unsqueeze(1).to_broadcast([128, 16, 4]), ALU.add))
        link(nc.vector.tensor_scalar(lg, lg, m.small[:, 0:1], None, ALU.mult))
        link(nc.vector.tensor_reduce(mx, j4(lg), AXX, ALU.max))
        nc.vector.tensor_tensor(j4(lg), j4(lg), b16(mx), ALU.subtract).then_inc(S["shifted"], 1)
        yield 31
        v.wait_ge(S["exp"], 1)
        link(nc.vector.tensor_reduce(rs, j4(pr), AXX, ALU.add))
        link(nc.vector.reciprocal(rs, rs))
        link(nc.vector.tensor_tensor(j4(pr), j4(pr), b16(rs), ALU.mult))
        pc = m.small[:, 5:21].unsqueeze(1).to_broadcast([128, 4, 16])
        t16 = lambda ap: ap.rearrange("p (t k) -> p t k", t=4)
        nc.vector.scalar_tensor_tensor(t16(pr), t16(pr), 1.0 - 2.0 * 0.08, pc, ALU.mult, ALU.add).then_inc(S["probs"], 1)
        yield 35
        v.wait_ge(S["prob_bc"], 1)
        link(nc.vector.tensor_tensor(m.s(O), streams[0], m.ps[PB[0]][:, :], ALU.mult))
        for k in range(1, 4):
            yield 35 + 1.5 * k
            v.wait_ge(S["prob_bc"], k + 1)
            link(nc.vector.tensor_tensor(m.s(T2), streams[k], m.ps[PB[k]][:, :], ALU.mult))
            add = nc.vector.tensor_tensor(m.s(O), m.s(O), m.s(T2), ALU.add)
            if k < 3:
                link(add)
        add.then_inc(S["o"], 1)
        yield 47
        v.wait_ge(S["o"], 1)
        v.wait_ge(S["o_rstd"], 1)
        nc.vector.scalar_tensor_tensor(m.s(T2), m.s(O), m.W("rms"), m.s(T2), ALU.mult, ALU.mult).then_inc(S["o_norm"], 1)
        yield 49
        v.wait_ge(S["proj"], 1)
        nc.vector.tensor_tensor(m.x[:, :], m.x[:, :], m.ps[2][:, :], ALU.add)

    return "gate", {"tensor": tensor, "vector": vector, "scalar": scalar}


def l0_ffn(nc, m):
    R, K, K2 = 3, 4, 5

    def tensor(pe, S):
        yield 0
        yield from ln_tensor(nc, pe, S, m, m.x[:, :], (0, 1, 2), (0, 1))
        pe.wait_ge(S["h_ready"], 1)
        for i in range(2):
            nc.tensor.matmul(m.ps[2 + i][:, :], m.mixw[:, 2 * i, :], m.h, start=True, stop=False)
            nc.tensor.matmul(m.ps[2 + i][:, :], m.mixw[:, 2 * i + 1, :], m.hp[:, PAD - 1:PAD - 1 + L], start=False, stop=True).then_inc(S["rk"], 1)
        yield 16
        pe.wait_ge(S["k_act"], 1)
        nc.tensor.matmul(m.ps[4][:, :], m.W("Wvf"), m.s(K2), start=True, stop=True).then_inc(S["kv"], 1)

    def scalar(a, S):
        yield 0
        yield from ln_scalar(nc, a, S, m, (0, 1, 2), (0, 1))
        yield 11
        a.wait_ge(S["rk"], 1)
        nc.scalar.activation(m.s(R), m.ps[2][:, :], ACT.Sigmoid).then_inc(S["r"], 1)
        a.wait_ge(S["rk"], 2)
        nc.scalar.activation(m.s(K), m.ps[3][:, :], ACT.Relu).then_inc(S["relu"], 1)

    def vector(v, S):
        yield 0
        yield from ln_vector(nc, v, S, m, m.x[:, :], m.h, (0, 1, 2), (0, 1))
        yield 15
        v.wait_ge(S["relu"], 1)
        nc.vector.tensor_tensor(m.s(K2), m.s(K), m.s(K), ALU.mult).then_inc(S["k_act"], 1)
        yield 17
        v.wait_ge(S["kv"], 1)
        v.wait_ge(S["r"], 1)
        nc.vector.tensor_tensor(m.s(R), m.s(R), m.ps[4][:, :], ALU.mult).then_inc(S["rv"], 1)
        v.wait_ge(S["rv"], 1)
        nc.vector.tensor_tensor(m.x[:, :], m.x[:, :], m.s(R), ALU.add)

    return "ffn", {"tensor": tensor, "vector": vector, "scalar": scalar}


C_PC = 3
C_X1, C_ZS, C_DEL, C_DU = 4, 8, 10, 14
C_XT, C_XP, C_T = 18, 20, 23
C_ACC = 33
C_DA, C_DBU, C_HS, C_HC, C_CS = 4, 30, (0, 28), (35, 26), 37
C_XC = (18, 19, 20, 21)
C_YQ, C_U = 22, 22
C_TH = (2, 32)


def l1_inputs(nc, m):
    XZ_PS, XT_PS, XDBL_PS, DT_PS = (2, 3, 4, 0), (1, 2), (3, 1), (2, 4, 0, 3)
    xp = m.work[:, C_XP:C_XP + 3, :].rearrange("p a n -> p (a n)")[:, 0:2 * (L + 8)].rearrange("p (k n) -> p k n", k=2)
    xt = m.work[:, C_XT:C_XT + 2, :].rearrange("p a n -> p (a n)")
    pc = m.work[:, C_PC, :].bitcast(BF16).rearrange("p (e n) -> p e n", e=2)
    i4 = [(e, k) for e in range(2) for k in range(2)]

    def tensor(pe, S):
        yield 0
        yield from ln_tensor(nc, pe, S, m, m.x[:, :], (0, 1, 2), (0, 1))
        pe.wait_ge(S["h_ready"], 1)
        for k in range(4):
            nc.tensor.matmul(m.ps[XZ_PS[k]][:, :], m.W("inp")[:, 128 * k:128 * k + 128], m.h, start=True, stop=True).then_inc(S["xz"], 1)
        yield 12
        for t in range(NT):
            if t == 2:
                pe.wait_ge(S["xz_used"], 1)
            last = nc.tensor.matmul(m.ps[XT_PS[t // 2]][:, 256 * (t % 2):256 * (t % 2) + 256], m.h[:, 128 * t:128 * t + 128],
                                    m.W("inp")[:, 0:256], start=True, stop=True)
        last.then_inc(S["xt"], 1)
        for e in range(2):
            yield 20 + 6 * e
            if e == 1:
                pe.wait_ge(S["xt_sb"], 1)
            for k in range(2):
                pe.wait_ge(S["x1"], 2 * e + k + 1)
                last = nc.tensor.matmul(m.ps[XDBL_PS[e]][:, :], m.W("xproj")[:, 256 * e + 128 * k:256 * e + 128 * k + 128], m.s(C_X1 + 2 * e + k),
                                        start=(k == 0), stop=(k == 1))
            last.then_inc(S["xdbl"], 1)
        yield 32
        pe.wait_ge(S["xt_sb"], 2)
        pe.wait_ge(S["xz_used"], 4)
        for i, (e, k) in enumerate(i4):
            pe.wait_ge(S["xd"], e + 1)
            nc.tensor.matmul(m.ps[DT_PS[i]][:, :], m.W("dtproj")[:, 256 * e + 128 * k:256 * e + 128 * k + 128], m.s(C_T + 8 + e),
                             start=True, stop=True).then_inc(S["dt"], 1)

    def scalar(a, S):
        yield 0
        yield from ln_scalar(nc, a, S, m, (0, 1, 2), (0, 1))
        for k in range(2):
            yield 9 + k
            a.wait_ge(S["xz"], k + 1)
            nc.scalar.activation(xp[:, k, 4:4 + L], m.ps[XZ_PS[k]][:, :], ACT.Copy).then_inc(S["xz_used"], 1)
        for k in range(2):
            a.wait_ge(S["xz"], k + 3)
            nc.scalar.activation(m.s(C_ZS + k), m.ps[XZ_PS[2 + k]][:, :], ACT.Silu).then_inc(S["xz_used"], 1)
        yield 14
        a.wait_ge(S["xt"], 1)
        for t in range(2):
            nc.scalar.activation(xt[:, 512 * t:512 * t + 512], m.ps[XT_PS[t]][:, :], ACT.Copy).then_inc(S["xt_sb"], 1)
        for i in range(4):
            yield 16 + 3 * i
            a.wait_ge(S["conv"], i + 1)
            nc.scalar.activation(m.s(C_X1 + i), m.s(C_T + i), ACT.Silu).then_inc(S["x1"], 1)
        for e in range(2):
            yield 29 + e
            a.wait_ge(S["xdbl"], e + 1)
            nc.scalar.activation(m.s(C_T + 8 + e), m.ps[XDBL_PS[e]][:, :], ACT.Copy).then_inc(S["xd"], 1)
        yield 36
        for i in range(4):
            a.wait_ge(S["sp_in"], i + 1)
            nc.scalar.activation(m.s(C_T + i), m.s(C_T + i), ACT.Exp).then_inc(S["sp_exp"], 1)
        for i in range(4):
            a.wait_ge(S["sp_exp"], i + 1)
            nc.scalar.activation(m.s(C_T + i), m.s(C_T + i), ACT.Ln, bias=m.small[:, 122:123]).then_inc(S["sp_ln"], 1)

    def vector(v, S):
        yield 0
        link = linker(v, S["chain"])
        nc.vector.memset(xp[:, :, 0:4], 0.0)
        link(nc.vector.memset(xp[:, :, 4 + L:8 + L], 0.0))
        yield from ln_vector(nc, v, S, m, m.x[:, :], m.h, (0, 1, 2), (0, 1))
        for i, (e, k) in enumerate(i4):
            yield 12 + 3 * i
            v.wait_ge(S["xz_used"], 2)
            w = m.W("mconv")[:, 4 * i:4 * i + 4]
            src = lambda j: xp[:, k, 1 + j:1 + j + L] if e == 0 else xp[:, k, 7 - j:7 - j + L]
            link(nc.vector.tensor_scalar(m.s(C_T + i), src(0), w[:, 0:1], m.W("mconvb")[:, i:i + 1], ALU.mult, ALU.add))
            for j in range(1, 4):
                last = nc.vector.scalar_tensor_tensor(m.s(C_T + i), src(j), w[:, j:j + 1], m.s(C_T + i), ALU.mult, ALU.add)
                if j < 3:
                    link(last)
            last.then_inc(S["conv"], 1)
        v.wait_ge(S["xz_used"], 4)
        for k in range(2):
            link(nc.vector.tensor_reduce(m.small[:, 100 + k:101 + k], m.s(C_ZS + k), AXX, ALU.max))
        r1, md = m.s(C_T + 5)[0:32, :], m.s(C_T + 6).bitcast(BF16)[0:32, 0:L]
        for e in range(2):
            yield 30 + 2 * e
            v.wait_ge(S["xd"], e + 1)
            full = m.s(C_T + 8 + e)[0:32, :]
            link(nc.vector.tensor_copy(pc[0:32, e, :], full))
            link(nc.vector.tensor_tensor(r1, full, pc[0:32, e, :], ALU.subtract))
            link(nc.vector.tensor_copy(md, r1))
            link(nc.vector.tensor_tensor(r1, r1, md, ALU.subtract))
            nc.vector.tensor_copy(pc[32:64, e, :], md)
            link(nc.vector.tensor_copy(pc[64:96, e, :], r1))
        yield 34
        for i in range(4):
            v.wait_ge(S["dt"], i + 1)
            v.wait_ge(S["x1"], 4)
            nc.vector.tensor_scalar(m.s(C_T + i), m.ps[DT_PS[i]][:, :], m.W("dtb")[:, i:i + 1], SP_CAP, ALU.add, ALU.min).then_inc(S["sp_in"], 1)
        for i in range(4):
            yield 39 + i
            v.wait_ge(S["sp_ln"], i + 1)
            link(nc.vector.scalar_tensor_tensor(m.s(C_DEL + i), m.ps[DT_PS[i]][:, :], m.W("dtb")[:, i:i + 1], m.s(C_T + i), ALU.add, ALU.max))
            nc.vector.tensor_tensor(m.s(C_DU + i), m.s(C_DEL + i), m.s(C_X1 + i), ALU.mult)
        for k in range(2):
            link(nc.vector.tensor_scalar(m.s(C_ACC + k), m.s(C_X1 + k), m.W("Dp")[:, k:k + 1], None, ALU.mult))
            nc.vector.scalar_tensor_tensor(m.s(C_ACC + k), m.s(C_X1 + 2 + k), m.W("Dp")[:, 2 + k:3 + k], m.s(C_ACC + k), ALU.mult, ALU.add)

    return "proj", {"tensor": tensor, "vector": vector, "scalar": scalar}


def l1_core(nc, m):
    xt = m.work[:, C_XT:C_XT + 2, :].rearrange("p a n -> p (a n)").rearrange("p (t c) -> p t c", t=NT)
    YW = NC + 4
    yq = m.work[:, C_YQ:C_YQ + 3, :].rearrange("p a n -> p (a n)")[:, 0:4 * YW].rearrange("p (k n) -> p k n", k=4)
    pc = m.work[:, C_PC, :].bitcast(BF16).rearrange("p (e n) -> p e n", e=2)
    u = m.work[:, C_U:C_U + 4, :]
    xc = lambda o: m.s(C_XC[o])
    sq = xc
    two = lambda slot: m.work[:, slot:slot + 2, :]
    hc = lambda i: two(C_HC[i % 2])
    STEPS = [(e, n) for e in range(2) for n in range(NS)]
    HALF = L // 2 + 1
    B_PS, C_PS, SUM_PS = (0, 1), 2, 3

    units = ([("dft", c, r) for r in range(2) for c in range(2)] + [("conv", o, part) for o in range(4) for part in ("odd", "even")]
             + [("chan", t, 0) for t in range(NT)] + [("time", j, part) for j in range(4) for part in ("odd", "even")])
    CONV, CHAN, TIME = 4, 12, 16
    width = {"dft": NF, "conv": NC, "chan": L, "time": HALF}
    bank = lambda i: m.ps[4 + i % 4]

    def products(i):
        kind, a, b = units[i]
        if kind == "dft":
            return [(xt[:, t, 128 * a:128 * a + 128], m.dft[:, b, t, :]) for t in range(NT)]
        if kind == "conv":
            col = slice(128 * a, 128 * a + 128)
            near = lambda q, k: m.combos[:, q - 1, k, :] if q else yq[:, k, 2:2 + NC]
            sums, diffs = (0, 1, 2), (3, 4)
            qs = (diffs, sums) if b == "odd" else (sums, diffs)
            return [(m.fw[:, q, k, col], near(q, k)) for k in range(4) for q in qs[k // 2]]
        if kind == "chan":
            return [(xc(k)[:, 128 * a:128 * a + 128], m.inv[:, k, :]) for k in range(4)]
        c, r = a // 2, a % 2
        odd = b == "odd"
        col = 128 * c + 256 * (r != odd)
        return [(u[:, t, col:col + 128], m.dft[:, int(odd), t, 0:HALF]) for t in range(NT)]

    cut = lambda unit, size: [(unit, j, min(j + size, len(products(unit)))) for j in range(0, len(products(unit)), size)]
    order = [x for i in range(CONV) for x in cut(i, 4)]
    order += [(CONV, 0, 4), (CONV + 1, 0, 6), (CONV, 4, 10), (CONV + 1, 6, 10)]
    order += [x for i in range(CONV + 2, CHAN) for x in cut(i, 5)]
    order += [(CHAN, 0, 2), (CHAN + 1, 0, 2), (CHAN, 2, 3), (CHAN + 1, 2, 3), (CHAN, 3, 4), (CHAN + 1, 3, 4)]
    order += [x for i in range(CHAN + 2, TIME) for x in cut(i, 2)]
    order += [x for i in range(TIME, len(units)) for x in cut(i, 2)]
    closes = lambda x: x[2] == len(products(x[0]))

    def operands(unit, first, end):
        kind = units[unit][0]
        if kind == "conv":
            imag = end > {"odd": 4, "even": 6}[units[unit][2]]
            return [("combos", 1 + imag, 1 + 2 * imag, 2)]
        if kind == "chan":
            return [("xc", end, CONV + 2 * end - 1, 2)]
        if kind == "time":
            return [("unit_out", CHAN + end, CHAN + end - 1, 1)]
        return []

    cost = lambda x: (x[2] - x[1]) * width[units[x[0]][0]]
    total, spent, ended, todo = sum(map(cost, order)), 0, {}, list(order)
    plan = []
    for i in range(len(STEPS)):
        plan.append([])
        share = total * min(1, (i + 1) / (len(STEPS) - 1))
        while todo and spent + cost(todo[0]) / 2 <= share and all(ended[u_] + lag <= i for _, _, u_, lag in operands(*todo[0])):
            x = todo.pop(0)
            plan[-1].append(x)
            spent += cost(x)
            if closes(x):
                ended[x[0]] = i
    assert not todo and not plan[-1], (todo, plan[-1])
    ends = [[x[0] for x in p if closes(x)] for p in plan]

    def tensor(pe, S):
        yield 0
        def b_row(i):
            e, n = STEPS[i]
            if i >= 2:
                pe.wait_ge(S["dbu"], i - 1)
            nc.tensor.matmul(m.ps[B_PS[i % 2]][:, :], m.sel[0:96, n, :], pc[0:96, e, :], start=True, stop=True).then_inc(S["b_row"], 1)

        def c_row(i):
            e, n = STEPS[i]
            if i:
                pe.wait_ge(S["c_sb"], i)
            nc.tensor.matmul(m.ps[C_PS][:, :], m.sel[0:96, NS + n, :], pc[0:96, e, :], start=True, stop=True).then_inc(S["c_row"], 1)

        def add(i):
            pe.wait_ge(S["hc"], i + 1)
            nc.tensor.matmul(m.ps[SUM_PS][:, :], m.T("ident"), hc(i)[:, 0, :], start=(i == 0), stop=(i == len(STEPS) - 1)).then_inc(S["acc_pe"], 1)

        b_row(0)
        c_row(0)
        for i in range(len(STEPS)):
            if i + 1 < len(STEPS):
                b_row(i + 1)
            for unit, first, end in plan[i]:
                if unit >= 4 and first == 0:
                    pe.wait_ge(S["unit_out"], unit - 3)
                for sem, value, _, _ in operands(unit, first, end):
                    pe.wait_ge(S[sem], value)
                ps = products(unit)
                for j in range(first, end):
                    last = nc.tensor.matmul(bank(unit)[:, 0:width[units[unit][0]]], ps[j][0], ps[j][1], start=(j == 0), stop=(j == len(ps) - 1))
                if end == len(ps):
                    last.then_inc(S["unit"], 1)
            if i + 1 < len(STEPS):
                c_row(i + 1)
            if i >= 2:
                add(i - 2)
        for i in range(len(STEPS) - 2, len(STEPS)):
            add(i)

    def scalar(a, S):
        yield 0
        def leave(i):
            kind, p, b = units[i]
            th = C_TH[(i // 2) % 2]
            if kind == "dft":
                a.wait_ge(S["unit"], i + 1)
                nc.scalar.activation(yq[:, 2 * b + p, 2:2 + NF], bank(i)[:, 0:NF], ACT.Copy, scale=(1.0, -1.0)[b]).then_inc(S["unit_out"], 1)
            elif kind == "chan":
                a.wait_ge(S["unit"], i + 1)
                nc.scalar.activation(u[:, p, :], bank(i)[:, :], ACT.Copy).then_inc(S["unit_out"], 1)
            elif b == "odd":
                a.wait_ge(S["unit"], i + 1)
                if kind == "conv" and p >= 2:
                    a.wait_ge(S["xc"], p - 1)
                if kind == "time" and p >= 2:
                    a.wait_ge(S["unit_out"], i - 2)
                nc.scalar.activation(m.s(th)[:, 0:width[kind]], bank(i)[:, 0:width[kind]], ACT.Copy).then_inc(S["odd"], 1)
            else:
                a.wait_ge(S["unit_out"], i + 1)
                if kind == "conv":
                    nc.scalar.activation(m.s(th), xc(p), ACT.Tanh, bias=m.small[:, 104 + p:105 + p], scale=0.5).then_inc(S["tanh"], 1)
                else:
                    nc.scalar.activation(sq(p), sq(p), ACT.Square)

        for i, (e, n) in enumerate(STEPS):
            if i >= 2:
                a.wait_ge(S["h"], 2 * (i - 1))
            for k in range(2):
                c = SM["A"] + 32 * e + 16 * k + n
                nc.scalar.activation(m.s(C_DA + 2 * (i % 2) + k), m.s(C_DEL + 2 * e + k), ACT.Exp, scale=m.small[:, c:c + 1]).then_inc(S["da"], 1)
            a.wait_ge(S["c_row"], i + 1)
            if i >= 2:
                a.wait_ge(S["hc"], i - 1)
            nc.scalar.activation(m.s(C_CS + i % 2), m.ps[C_PS][:, :], ACT.Copy).then_inc(S["c_sb"], 1)
            if i:
                for unit in ends[i - 1]:
                    leave(unit)

    def vector(v, S):
        yield 0
        link = linker(v, S["chain"])
        nc.vector.memset(yq[:, :, 0:2], 0.0)
        nc.vector.memset(yq[:, :, YW - 2:YW], 0.0)
        link(nc.vector.tensor_scalar(m.small[:, 104:108], m.W("fftb"), 0.5, None, ALU.mult))

        def neighbours(r):
            y = yq[:, 2 * r:2 * r + 2, :]
            v.wait_ge(S["unit_out"], 2 * r + 2)
            link(nc.vector.tensor_scalar(y[:, :, 2 + NF:6 + NF], y[:, :, 6:2:-1], (1.0, -1.0)[r], None, ALU.mult))
            for q, (off, op) in enumerate([(o_, op) for op in (ALU.add, ALU.subtract) for o_ in (1, 2)]):
                last = nc.vector.tensor_tensor(m.combos[:, q, 2 * r:2 * r + 2, :], y[:, :, 2 + off:2 + off + NC], y[:, :, 2 - off:2 - off + NC], op)
            last.then_inc(S["combos"], 1)

        def combine(unit):
            kind, p, _ = units[unit]
            odd, even, out = m.s(C_TH[(unit // 2) % 2]), bank(unit), xc(p)
            plus, minus = (ALU.add, ALU.subtract) if kind == "conv" or p % 2 else (ALU.subtract, ALU.add)
            low = 3 if kind == "conv" else 1
            v.wait_ge(S["unit"], unit + 1)
            v.wait_ge(S["odd"], p + 1 + (4 if kind == "time" else 0))
            nc.vector.tensor_tensor(out[:, 0:HALF], even[:, 0:HALF], odd[:, 0:HALF], plus)
            if kind == "conv":
                nc.vector.tensor_tensor(out[:, L - 2:L], even[:, NC - 2:NC], odd[:, NC - 2:NC], plus)
            nc.vector.tensor_tensor(out[:, HALF:L + 1 - low], even[:, HALF - 2:low - 1:-1], odd[:, HALF - 2:low - 1:-1], minus).then_inc(S["unit_out"], 2)

        def finish(o):
            th = m.s(C_TH[o % 2])
            v.wait_ge(S["tanh"], o + 1)
            link(nc.vector.tensor_scalar(th, th, 0.5, 0.5, ALU.mult, ALU.add))
            nc.vector.scalar_tensor_tensor(xc(o), xc(o), m.W("fftb")[:, o:o + 1], th, ALU.add, ALU.mult).then_inc(S["xc"], 1)

        for i, (e, n) in enumerate(STEPS):
            v.wait_ge(S["b_row"], i + 1)
            if i:
                v.wait_ge(S["h"], 2 * i)
            nc.vector.tensor_tensor(two(C_DBU), two(C_DU + 2 * e), m.ps[B_PS[i % 2]][:, :].unsqueeze(1).to_broadcast([128, 2, L]), ALU.mult).then_inc(S["dbu"], 1)
            v.wait_ge(S["dbu"], i + 1)
            if i >= 2:
                v.wait_ge(S["hc"], i - 1)
            for k in range(2):
                v.wait_ge(S["da"], 2 * i + k + 1)
                s = slice(None) if e == 0 else slice(None, None, -1)
                nc.vector.tensor_tensor_scan(m.s(C_HS[i % 2] + k)[:, s], m.s(C_DA + 2 * (i % 2) + k)[:, s], m.s(C_DBU + k)[:, s], 0.0, ALU.mult, ALU.add).then_inc(S["h"], 1)
            if i:
                for unit in ends[i - 1]:
                    kind, p, part = units[unit]
                    if kind == "dft" and p == 1:
                        neighbours(part)
                    if part == "even":
                        combine(unit)
                v.wait_ge(S["hc"], i)
                if i > 1:
                    v.wait_ge(S["acc"], i - 1)
                nc.vector.tensor_tensor(m.s(C_ACC + 1), m.s(C_ACC + 1), hc(i - 1)[:, 1, :], ALU.add).then_inc(S["acc"], 1)
                for unit in ends[i - 1]:
                    if units[unit][0] == "conv" and units[unit][2] == "even":
                        finish(units[unit][1])
        last = len(STEPS)
        v.wait_ge(S["hc"], last)
        v.wait_ge(S["acc"], last - 1)
        nc.vector.tensor_tensor(m.s(C_ACC + 1), m.s(C_ACC + 1), hc(last - 1)[:, 1, :], ALU.add)
        v.wait_ge(S["acc_pe"], last)
        nc.vector.tensor_tensor(m.s(C_ACC), m.s(C_ACC), m.ps[SUM_PS][:, :], ALU.add)

    def gpsimd(g, S):
        yield 0
        for i, (e, n) in enumerate(STEPS):
            g.wait_ge(S["h"], 2 * i + 2)
            g.wait_ge(S["c_sb"], i + 1)
            if i >= 2:
                g.wait_ge(S["acc"], i - 1)
                g.wait_ge(S["acc_pe"], i - 1)
            nc.gpsimd.tensor_tensor(hc(i), two(C_HS[i % 2]), m.s(C_CS + i % 2).unsqueeze(1).to_broadcast([128, 2, L]), ALU.mult).then_inc(S["hc"], 1)

    return "scan", {"tensor": tensor, "vector": vector, "scalar": scalar, "gpsimd": gpsimd}


def l1_output(nc, m):
    sq = lambda i: m.s(C_XC[i])
    sm = m.small

    def vector(v, S):
        yield 0
        link = linker(v, S["chain"])
        for k in range(2):
            nc.vector.tensor_tensor(sq(2 * k), sq(2 * k), sq(2 * k + 1), ALU.add).then_inc(S["power"], 1)
        for k in range(2):
            link(nc.vector.tensor_tensor(m.s(C_ACC + k), m.s(C_ACC + k), m.s(C_ZS + k), ALU.mult))
        link(nc.vector.tensor_scalar(sm[:, 102:104], sm[:, 100:102], -1.0, None, ALU.mult))
        link(nc.vector.tensor_tensor(sm[:, 100:102], sm[:, 100:102], sm[:, 102:104], ALU.max))
        for k in range(2):
            v.wait_ge(S["mag"], k + 1)
            link(nc.vector.bn_stats(m.s(0)[:, 0:6], sq(2 * k)))
            link(nc.vector.bn_aggr(m.s(0)[:, 8 + 2 * k:10 + 2 * k], m.s(0)[:, 0:6]))
            z, mean, var = sm[:, 100 + k:101 + k], m.s(0)[:, 8 + 2 * k:9 + 2 * k], m.s(0)[:, 9 + 2 * k:10 + 2 * k]
            link(nc.vector.tensor_tensor(var, var, z, ALU.mult))
            link(nc.vector.tensor_tensor(var, var, z, ALU.mult))
            nc.vector.tensor_scalar(m.s(0)[:, 16 + k:17 + k], var, 1e-5, None, ALU.add).then_inc(S["var"], 1)
        for k in range(2):
            v.wait_ge(S["std"], k + 1)
            z, mean = sm[:, 100 + k:101 + k], m.s(0)[:, 8 + 2 * k:9 + 2 * k]
            r = m.s(0)[:, 20 + k:21 + k]
            link(nc.vector.reciprocal(r, m.s(0)[:, 18 + k:19 + k]))
            link(nc.vector.tensor_tensor(r, r, z, ALU.mult))
            link(nc.vector.tensor_scalar(sq(2 * k), sq(2 * k), mean, r, ALU.subtract, ALU.mult))
            nc.vector.tensor_tensor(m.s(C_ACC + k), m.s(C_ACC + k), sq(2 * k), ALU.add).then_inc(S["y"], 1)
        v.wait_ge(S["proj"], 1)
        nc.vector.tensor_tensor(m.xd[:, :], m.x[:, :], m.ps[0][:, :], ALU.add)

    def scalar(a, S):
        yield 0
        for k in range(2):
            a.wait_ge(S["power"], k + 1)
            nc.scalar.activation(sq(2 * k), sq(2 * k), ACT.Sqrt).then_inc(S["mag"], 1)
        for k in range(2):
            a.wait_ge(S["var"], k + 1)
            nc.scalar.activation(m.s(0)[:, 18 + k:19 + k], m.s(0)[:, 16 + k:17 + k], ACT.Sqrt).then_inc(S["std"], 1)

    def tensor(pe, S):
        yield 0
        for k in range(2):
            pe.wait_ge(S["y"], k + 1)
            last = nc.tensor.matmul(m.ps[0][:, :], m.W("outp")[:, 128 * k:128 * k + 128], m.s(C_ACC + k), start=(k == 0), stop=(k == 1))
        last.then_inc(S["proj"], 1)

    return "mout", {"tensor": tensor, "vector": vector, "scalar": scalar}


MASK, WGT, RF, HID, HM = DWORK, DWORK + 4, DWORK + 6, DWORK + 7, DWORK + 12
INT, VEL, HALT = DWORK + 16, DWORK + 17, DWORK + 18
SG, SA, SPT, ACCX, ACCV, TA = DWORK + 19, DWORK + 22, DWORK + 25, DWORK + 28, DWORK + 29, DWORK + 30
D_BANKS = (5, 6, 7)
D_LN = (ACCX, ACCV, TA)


def mask(m, i):
    return m.work[:, MASK:MASK + 4, :].bitcast(BF16)[:, i // 2, L * (i % 2):L * (i % 2) + L]


def l1_route(nc, m):
    tok = m.work[:, SG, :]
    lg, mx, eq, m2, pk = tok[:, 0:32], tok[:, 32:36], tok[:, 40:72], tok[:, 36:40], tok[:, 128:256]
    e8 = lambda ap: ap.rearrange("p (t k) -> p t k", k=8)
    b8 = lambda ap: ap.unsqueeze(2).to_broadcast([128, 4, 8])
    rb = m.work[:, SA, :].bitcast(BF16)[:, 0:L]
    pk3 = pk.rearrange("p (t k) -> p t k", k=32)
    dec = m.T("dec").unsqueeze(1).to_broadcast([128, 4, 8])
    mask_bank = lambda i: m.ps[(6, 7, 5)[i % 3]]

    def tensor(pe, S):
        yield 0
        yield from ln_tensor(nc, pe, S, m, m.xd[:, :], D_LN, (5, 6))
        pe.wait_ge(S["h_ready"], 1)
        nc.tensor.matmul(m.ps[7][:, :], m.W("m1")[:, 0:128], m.hd[:, :], start=True, stop=True).then_inc(S["hid"], 1)
        yield 10
        pe.wait_ge(S["gelu"], 1)
        for t in range(NT):
            last = nc.tensor.matmul(m.ps[5][:, 8 * t:8 * t + 8], m.s(HID)[:, 128 * t:128 * t + 128], m.W("rw2"), start=True, stop=True)
        last.then_inc(S["logits"], 1)
        yield 15
        pe.wait_ge(S["packed"], 1)
        for t in range(NT):
            last = nc.tensor.transpose(m.ps[6][0:32, 128 * t:128 * t + 128], pk[:, 32 * t:32 * t + 32], m.T("ident"))
        last.then_inc(S["routes"], 1)
        pe.wait_ge(S["routes_sb"], 2)
        for r in range(2):
            nc.tensor.matmul(m.ps[(7, 5)[r]][:, :], m.T("wsel")[0:32, 128 * r:128 * r + 128], m.s(RF)[0:32, :], start=True, stop=True).then_inc(S["w_bc"], 1)
        yield 20
        for i in range(8):
            if i in (1, 2):
                pe.wait_ge(S["w_sb"], i)
            if i >= 3:
                pe.wait_ge(S["mask_sb"], i - 2)
            nc.tensor.matmul(mask_bank(i)[:, :], m.sel[0:32, 32 + i, :], rb[0:32, :], start=True, stop=True).then_inc(S["mask"], 1)

    def scalar(a, S):
        yield 0
        yield from ln_scalar(nc, a, S, m, D_LN, (5, 6))
        yield 10
        a.wait_ge(S["hid"], 1)
        nc.scalar.activation(m.s(HID), m.ps[7][:, :], ACT.Gelu, bias=m.W("m1b")).then_inc(S["gelu"], 1)
        yield 15
        a.wait_ge(S["shifted"], 1)
        nc.scalar.activation(lg, lg, ACT.Exp).then_inc(S["exp"], 1)
        a.wait_ge(S["routes"], 1)
        nc.scalar.activation(m.s(RF)[0:32, :], m.ps[6][0:32, :], ACT.Copy).then_inc(S["routes_sb"], 1)
        nc.scalar.activation(rb[0:32, :], m.ps[6][0:32, :], ACT.Copy).then_inc(S["routes_sb"], 1)
        yield 20
        for i in range(8):
            a.wait_ge(S["mask"], i + 1)
            nc.scalar.activation(mask(m, i), mask_bank(i)[:, :], ACT.Copy).then_inc(S["mask_sb"], 1)

    def vector(v, S):
        yield 0
        yield from ln_vector(nc, v, S, m, m.xd[:, :], m.hd[:, :], D_LN, (5, 6))
        link = linker(v, S["chain"])
        yield 10
        link(nc.vector.memset(pk, 0.0))
        v.wait_ge(S["logits"], 1)
        link(nc.vector.tensor_tensor(e8(lg), e8(m.ps[5][:, 0:32]), m.W("rb2").unsqueeze(1).to_broadcast([128, 4, 8]), ALU.add))
        link(nc.vector.tensor_reduce(mx, e8(lg), AXX, ALU.max))
        nc.vector.tensor_tensor(e8(lg), e8(lg), b8(mx), ALU.subtract).then_inc(S["shifted"], 1)
        yield 15
        v.wait_ge(S["exp"], 1)
        top = (mx, m2)
        for r in range(2):
            link(nc.vector.tensor_reduce(top[r], e8(lg), AXX, ALU.max))
            link(nc.vector.tensor_tensor(e8(eq), e8(lg), b8(top[r]), ALU.is_equal))
            link(nc.vector.tensor_tensor(e8(eq), e8(eq), dec, ALU.mult))
            link(nc.vector.tensor_reduce(tok[:, 76:80], e8(eq), AXX, ALU.max))
            link(nc.vector.tensor_tensor(pk3[:, :, 8 * r:8 * r + 8], e8(eq), b8(tok[:, 76:80]), ALU.is_equal))
            if r == 0:
                link(nc.vector.scalar_tensor_tensor(e8(lg), pk3[:, :, 0:8], -2.0, e8(lg), ALU.mult, ALU.add))
        s = tok[:, 80:84]
        link(nc.vector.tensor_tensor(s, mx, m2, ALU.add))
        link(nc.vector.reciprocal(s, s))
        link(nc.vector.tensor_tensor(pk3[:, :, 16], mx, s, ALU.mult))
        nc.vector.tensor_tensor(pk3[:, :, 17], m2, s, ALU.mult).then_inc(S["packed"], 1)
        yield 20
        for r in range(2):
            v.wait_ge(S["w_bc"], r + 1)
            nc.vector.tensor_scalar(m.s(WGT + r), m.ps[(7, 5)[r]][:, :], m.small[:, 22:23], None, ALU.mult).then_inc(S["w_sb"], 1)
        nc.vector.tensor_copy(m.s(INT), m.hd[:, :])

    return "route", {"tensor": tensor, "vector": vector, "scalar": scalar}


def l1_steps(nc, m):
    src = (m.s(INT), m.s(VEL))
    col = {"a": 0, "b": 1, "g": 2}
    place = {"a": SA, "g": SG, "b": SPT}
    bank = lambda i: m.ps[D_BANKS[i % 3]]
    sigs = [[("g", s) for s in range(3)], [(w, s) for w in "ag" for s in range(3)]]
    outs = [sig + [("b", s) for s in range(3)] for sig in sigs]
    T0, T_MASK = (0, 47), 9
    t_out = lambda it, i: T0[it] + 11 + 3.2 * i
    t_sp = lambda it: t_out(it, len(outs[it]) - 1) + 1

    def meet(eng, S):
        eng.drain().then_inc(S["met"], 1)
        eng.wait_ge(S["met"], 3)

    def tensor(pe, S):
        for it in range(2):
            yield T0[it]
            if it:
                meet(pe, S)
            for i in range(5):
                if i >= 3:
                    pe.wait_ge(S["gelu"], 5 * it + i - 2)
                for k in range(1 + it):
                    w = m.W("m1")[:, 128 * k:128 * k + 128] if i == 0 else m.W("e1")[:, 512 * k + 128 * (i - 1):512 * k + 128 * i]
                    last = nc.tensor.matmul(bank(i)[:, :], w, src[k], start=(k == 0), stop=(k == it))
                last.then_inc(S["hid"], 1)
            yield T0[it] + T_MASK
            pe.wait_ge(S["gelu"], 5 * it + 5)
            nc.tensor.matmul(bank(5)[:, :], m.W("hw2"), m.s(HID), start=True, stop=True).then_inc(S["halt_lin"], 1)
            n0, nsig = 3 * it, len(sigs[it])
            for i, (what, s) in enumerate(outs[it]):
                yield t_out(it, i)
                if i == 2:
                    pe.wait_ge(S["halt"], it + 1)
                if i >= 3:
                    pe.wait_ge(S["sig"], n0 + i - 2)
                c = 128 * col[what]
                if s == 0:
                    last = nc.tensor.matmul(bank(i)[:, :], m.W("s2")[:, c:c + 128], m.s(HID), start=True, stop=True)
                else:
                    h = (HM, HID + 1)[s - 1]
                    for t in range(4):
                        pe.wait_ge(S["masked"], 8 * it + 4 * (s - 1) + t + 1)
                        nc.tensor.matmul(bank(i)[:, :], m.W("e2")[:, 384 * t + c:384 * t + c + 128], m.s(h + t), start=(t == 0), stop=False)
                    last = nc.tensor.matmul(bank(i)[:, :], m.W("e2b")[0:32, 384 * (s - 1) + c:384 * (s - 1) + c + 128], m.s(RF)[0:32, :], start=False, stop=True)
                last.then_inc(S["ctrl"], 1)

    def scalar(a, S):
        for it in range(2):
            yield T0[it]
            if it:
                meet(a, S)
            for i in range(5):
                a.wait_ge(S["hid"], 5 * it + i + 1)
                nc.scalar.activation(m.s(HID + i), bank(i)[:, :], ACT.Gelu, bias=m.W("m1b") if i == 0 else m.W("e1b")[:, i - 1:i]).then_inc(S["gelu"], 1)
            yield T0[it] + T_MASK
            a.wait_ge(S["halt_lin"], it + 1)
            nc.scalar.activation(m.s(HALT), bank(5)[:, :], ACT.Sigmoid, bias=m.W("hb2")).then_inc(S["halt"], 1)
            o0 = len(outs[0]) * it
            for i, (what, s) in enumerate(outs[it]):
                yield t_out(it, i)
                if what != "b":
                    a.wait_ge(S["ctrl"], o0 + i + 1)
                    bias = {"bias": m.W("s2b")[:, col[what]:col[what] + 1]} if s == 0 else {}
                    nc.scalar.activation(m.s(place[what] + s), bank(i)[:, :], ACT.Sigmoid, **bias).then_inc(S["sig"], 1)
            yield t_sp(it)
            for s in range(3):
                a.wait_ge(S["sp_in"], 3 * it + s + 1)
                nc.scalar.activation(m.s(SPT + s), m.s(SPT + s), ACT.Exp).then_inc(S["sp_exp"], 1)
            for s in range(3):
                a.wait_ge(S["sp_exp"], 3 * it + s + 1)
                nc.scalar.activation(m.s(SPT + s), m.s(SPT + s), ACT.Ln, bias=m.small[:, 122:123]).then_inc(S["sp_ln"], 1)

    def vector(v, S):
        link = linker(v, S["chain"])
        bias = lambda s: m.W("s2b")[:, 1:2] if s == 0 else m.small[:, 125:126]
        for it in range(2):
            yield T0[it]
            if it:
                meet(v, S)
            yield T0[it] + T_MASK
            for r in range(2):
                for t in range(4):
                    v.wait_ge(S["gelu"], 5 * it + t + 2)
                    if r:
                        v.wait_ge(S["masked"], 8 * it + t + 1)
                    nc.vector.tensor_tensor(m.s((HM, HID + 1)[r] + t), m.s(HID + 1 + t), mask(m, 4 * r + t), ALU.mult).then_inc(S["masked"], 1)
            nsig, o0, sig0 = len(sigs[it]), len(outs[0]) * it, 3 * it
            for s in range(3):
                i = nsig + s
                yield t_out(it, i)
                v.wait_ge(S["ctrl"], o0 + i + 1)
                nc.vector.tensor_scalar(m.s(SPT + s), bank(i)[:, :], bias(s), SP_CAP, ALU.add, ALU.min).then_inc(S["sp_in"], 1)
            for s in range(3):
                i = nsig + s
                yield t_sp(it) + 3 + 5 * s
                v.wait_ge(S["sp_ln"], 3 * it + s + 1)
                link(nc.vector.scalar_tensor_tensor(m.s(SPT + s), bank(i)[:, :], bias(s), m.s(SPT + s), ALU.add, ALU.max))
                link(nc.vector.scalar_tensor_tensor(m.s(TA), m.s(INT), m.W("mu"), m.s(SPT + s), ALU.subtract, ALU.mult))
                w = m.small[:, 21:22] if s == 0 else None
                if it:
                    v.wait_ge(S["sig"], sig0 + nsig)
                    link(nc.vector.tensor_tensor(m.s(SA + s), m.s(SA + s), m.s(VEL), ALU.mult))
                    link(nc.vector.tensor_tensor(m.s(TA), m.s(SA + s), m.s(TA), ALU.subtract))
                else:
                    v.wait_ge(S["sig"], nsig)
                    link(nc.vector.tensor_scalar(m.s(TA), m.s(TA), -1.0, None, ALU.mult))
                if s == 0:
                    link(nc.vector.tensor_scalar(m.s(ACCV), m.s(TA), w, None, ALU.mult))
                    link(nc.vector.tensor_tensor(m.s(ACCX), m.s(ACCV), m.s(SG), ALU.mult))
                else:
                    link(nc.vector.tensor_tensor(m.s(TA), m.s(TA), m.s(WGT + s - 1), ALU.mult))
                    nc.vector.tensor_tensor(m.s(ACCV), m.s(ACCV), m.s(TA), ALU.add)
                    link(nc.vector.tensor_tensor(m.s(SG + s), m.s(SG + s), m.s(TA), ALU.mult))
                    link(nc.vector.tensor_tensor(m.s(ACCX), m.s(ACCX), m.s(SG + s), ALU.add))
            v.wait_ge(S["halt"], it + 1)
            link(nc.vector.scalar_tensor_tensor(m.s(TA), m.s(ACCX), 0.1, m.s(HALT), ALU.mult, ALU.mult))
            link(nc.vector.tensor_tensor(m.s(INT), m.s(INT), m.s(TA), ALU.add))
            if it == 0:
                link(nc.vector.tensor_tensor(m.s(VEL), m.s(ACCV), m.s(HALT), ALU.mult))

    return "steps", {"tensor": tensor, "vector": vector, "scalar": scalar}


def load_fourier(sp, sem, m, d):
    sp.dma_start(m.dft, d["time"].rearrange("p (a t n) -> p a t n", a=2, t=NT)).then_inc(sem, 16)
    for t in range(TAPS):
        sp.dma_start(m.fw[:, t, :, :], d["folded"][:, 2048 * t:2048 * t + 2048].rearrange("p (k n) -> p k n", k=4)).then_inc(sem, 16)
    sp.wait_ge(sem, 16 * (1 + TAPS))


def fold_weights(nc, m, d):
    place = m.work[:, DWORK:DWORK + 24, :].rearrange("p (t k) n -> p t k n", t=TAPS + 1)
    fwd = m.work[:, DWORK + 24:DWORK + 28, :]
    UNITS = [(t, y) for t in range(TAPS) for y in range(4)]
    t_unit = lambda n: 20 + 8 * n
    T_SUMS = t_unit(len(UNITS)) + 1
    bank = lambda n: m.ps[5 + n % 3]

    def sync(sp, S):
        yield 0
        sp.dma_start(fwd, d["fwd"].rearrange("p (a n) -> p a n", a=4)).then_inc(S["freq"], 16)
        sp.dma_start(place[:, 1:TAPS + 1], d["fw"].rearrange("p (t k n) -> p t k n", t=TAPS, k=4)).then_inc(S["freq"], 16)
        yield T_SUMS + 1
        sp.wait_ge(S["tap_sums"], 2)
        for q, part in enumerate((2, 5, 1, 3, 4)):
            sp.dma_start(d["folded"][:, 2048 * q:2048 * q + 2048].rearrange("p (k n) -> p k n", k=4), place[:, part]).then_inc(S["stored"], 16)
        sp.wait_ge(S["stored"], 16 * TAPS)
        load_fourier(sp, S["tables"], m, d)

    def tensor(pe, S):
        for n, (t, y) in enumerate(UNITS):
            yield t_unit(n)
            if n == 0:
                pe.wait_ge(S["freq"], 32)
            if n >= 3:
                pe.wait_ge(S["copied"], n - 2)
            for j in range(4):
                last = nc.tensor.matmul(bank(n)[:, :], fwd[:, j, 128 * y:128 * y + 128], place[:, t + 1, j, :], start=(j == 0), stop=(j == 3))
            last.then_inc(S["folded"], 1)

    def vector(v, S):
        for n, (t, y) in enumerate(UNITS):
            yield t_unit(n) + 5
            v.wait_ge(S["folded"], n + 1)
            if t:
                v.wait_ge(S["folded"], 4 * t)
            nc.vector.tensor_copy(place[:, t, y, :], bank(n)[:, :]).then_inc(S["copied"], 1)
        yield T_SUMS
        v.wait_ge(S["copied"], len(UNITS))
        for i, total in enumerate((5, 1)):
            lo, hi = place[:, 1 - i], place[:, 3 + i]
            nc.vector.tensor_scalar(lo, lo, 0.5, None, ALU.mult).then_inc(S["half"], 1)
            v.wait_ge(S["half"], i + 1)
            nc.vector.scalar_tensor_tensor(place[:, total], hi, 0.5, lo, ALU.mult, ALU.add)
            nc.vector.scalar_tensor_tensor(hi, hi, 0.5, lo, ALU.mult, ALU.subtract).then_inc(S["tap_sums"], 1)
            v.wait_ge(S["tap_sums"], i + 1)

    return "fold", {"sync": sync, "tensor": tensor, "vector": vector}


def l1_refine(nc, m, d, out_dram, b, scans_follow):
    H0, RES, OUT = HID, HM, HM + 1

    def tensor(pe, S):
        yield 0
        for k in range(2):
            nc.tensor.matmul(m.ps[5 + k][:, :], m.W("r1")[:, 128 * k:128 * k + 128], m.s(INT), start=True, stop=True).then_inc(S["hid"], 1)
        yield 3
        for k in range(2):
            pe.wait_ge(S["gelu"], k + 1)
            last = nc.tensor.matmul(m.ps[7][:, :], m.W("r2")[:, 128 * k:128 * k + 128], m.s(H0 + k), start=(k == 0), stop=(k == 1))
        last.then_inc(S["refined"], 1)

    def scalar(a, S):
        yield 1
        for k in range(2):
            a.wait_ge(S["hid"], k + 1)
            nc.scalar.activation(m.s(H0 + k), m.ps[5 + k][:, :], ACT.Gelu, bias=m.W("r1b")[:, k:k + 1]).then_inc(S["gelu"], 1)

    def vector(v, S):
        yield 0
        nc.vector.tensor_tensor(m.s(RES), m.xd[:, :], m.hd[:, :], ALU.add).then_inc(S["res"], 1)
        yield 6
        v.wait_ge(S["refined"], 1)
        nc.vector.tensor_scalar(m.s(OUT), m.ps[7][:, :], m.W("r2b"), m.W("iw"), ALU.add, ALU.mult).then_inc(S["scaled"], 1)
        v.wait_ge(S["scaled"], 1)
        v.wait_ge(S["res"], 1)
        nc.vector.tensor_tensor(m.xd[:, :], m.s(OUT), m.s(RES), ALU.add).then_inc(S["done"], 1)

    def sync(sp, S):
        yield 8
        sp.wait_ge(S["done"], 1)
        sp.dma_start(out_dram[bass.ds(b, 1), :, :].rearrange("o c t -> (o c) t"), m.xd[:, :]).then_inc(S["stored"], 16)
        if scans_follow:
            load_fourier(sp, S["tables"], m, d)
        sp.wait_ge(S["stored"], 16)

    return "refine", {"tensor": tensor, "vector": vector, "scalar": scalar, "sync": sync}


def build(nc, d, out):
    AT = (38, 142, 195, 215)
    with ExitStack() as ctx:
        m = Mem(nc, ctx)

        def mixing_stages(b):
            return Stream((0, l0_inputs(nc, m, d["x"], b)), (AT[0], l0_delta(nc, m)), (AT[1], l0_gate(nc, m)),
                          (AT[2], l0_ffn(nc, m)), (AT[3], l1_inputs(nc, m)))

        def scan_stages():
            run_block(nc, l1_core(nc, m))
            run_block(nc, l1_output(nc, m))

        def expert_stages(b, scans_follow, pace=1.0):
            return Stream((0, l1_route(nc, m)), (34 * pace, l1_steps(nc, m)), (137 * pace, l1_refine(nc, m, d, out, b, scans_follow)), pace=pace)

        run_block(nc, setup(nc, m, d))
        run_block(nc, mixing_stages(0), fold_weights(nc, m, d))
        with nc.Fori(0, B - 1) as b:
            scan_stages()
            run_block(nc, mixing_stages(b + 1), expert_stages(b, True, pace=1.65))
        scan_stages()
        run_block(nc, expert_stages(B - 1, False))


def lay_out(inputs, np):
    g = {k: np.asarray(v) for k, v in inputs.items()}
    A = lambda n: g["L0_attn_" + n]
    F = lambda n: g["L0_ffn_" + n]
    C = lambda n: g["L1_attn_" + n]
    E = lambda n: g["L1_ffn_" + n]
    z = lambda *s: np.zeros(s, np.float32)
    rows = lambda a: np.tile(np.reshape(a, (1, -1)), (128, 1))
    cols = lambda a: np.reshape(a, (-1, 128)).T
    w = {}
    w["Wb"] = np.repeat(A("Wb"), 32, axis=1)
    w["fir_s"] = A("fir_short_w").reshape(128, FIR_S)
    w["fir_l"] = A("fir_long_w").reshape(128, FIR_L)
    w["W1x"] = A("mlp_w1")[:128]
    t = z(128, 4, 128)
    for h in range(4):
        for s in range(4):
            for k in range(4):
                t[32 * k + 4 * s + h, h] = A("mlp_w1")[128 + 4 * s + k]
    w["W1s"] = t
    w["b1"], w["W2"], w["b2"] = A("mlp_b1"), A("mlp_w2"), rows(A("mlp_b2"))
    w["temp"], w["res"], w["rms"] = rows(A("logit_temp")), rows(A("conv_res_logit")), np.tile(A("rms_w"), 4)
    w["Wo"] = A("Wo")
    w["Wvf"], w["mur"], w["muk"] = F("W_v").T, F("mu_r"), F("mu_k")
    w["inp"] = C("in_proj_w").T
    both = lambda a, b: np.stack([C(a), C(b)])
    w["mconv"] = both("conv1d_w", "conv1db_w").reshape(2, 2, 128, 4).transpose(2, 0, 1, 3)
    w["mconvb"] = cols(both("conv1d_bias", "conv1db_bias"))
    xp, dp = both("x_proj_w", "x_projb_w"), both("dt_proj_w", "dt_projb_w")
    t, u = z(128, 2, 2, 128), z(128, 2, 2, 128)
    for e in range(2):
        for k in range(2):
            t[:, e, k, 0:32] = xp[e, 64:96, 128 * k:128 * k + 128].T
            t[:, e, k, 64:128] = xp[e, 0:64, 128 * k:128 * k + 128].T
            u[64:128, e, k] = dp[e, 128 * k:128 * k + 128].T
    w["xproj"], w["dtproj"] = t, u
    w["dtb"] = cols(both("dt_proj_b", "dt_projb_b"))
    w["Alog"] = both("A_log", "A_b_log").reshape(2, 2, 128, 16).transpose(2, 0, 1, 3)
    w["Dp"] = cols(both("D", "D_b"))
    w["outp"] = C("out_proj_w").T.reshape(2, 128, 128).transpose(1, 0, 2)
    w["fftb"] = cols(C("fft_conv_b"))
    w["iw"], w["mu"] = E("integration_weight"), E("mu")
    t, u = z(128, 2, 128), z(128)
    t[:, 0, 0:64], t[:, 1, 0:64] = E("shared_w1")[:128], E("shared_w1")[128:]
    t[:, 0, 64:96], t[:, 0, 96:128] = E("halt_w1"), E("router_w1")
    u[0:64], u[64:96], u[96:128] = E("shared_b1"), E("halt_b1"), E("router_b1")
    w["m1"], w["m1b"] = t, u
    t = z(128, 8)
    t[96:128] = E("router_w2")
    w["rw2"], w["rb2"] = t, rows(E("router_b2"))
    t = z(128, 128)
    t[64:96] = np.tile(E("halt_w2"), (1, 128))
    w["hw2"], w["hb2"] = t, rows(E("halt_b2"))
    w["e1"] = E("expert_w1").reshape(8, 2, 128, 64).transpose(2, 1, 0, 3)
    w["e1b"] = E("expert_b1").reshape(4, 128).T
    w["e2"] = E("expert_w2").reshape(4, 128, 384).transpose(1, 0, 2)
    t = z(128, 2, 384)
    t[0:8, 0], t[8:16, 1] = E("expert_b2"), E("expert_b2")
    w["e2b"] = t
    t = z(128, 384)
    t[0:64] = E("shared_w2")
    w["s2"], w["s2b"], w["sw"] = t, cols(E("shared_b2")), rows(E("shared_weight"))
    w["r1"], w["r1b"] = E("refine_w1"), cols(E("refine_b1"))
    w["r2"], w["r2b"] = E("refine_w2").reshape(2, 128, 128).transpose(1, 0, 2), E("refine_b2")
    for name, c in WEIGHTS:
        assert w[name].size == 128 * c, (name, w[name].shape)
    arrays = {"w": np.concatenate([w[name].reshape(128, -1) for name, _ in WEIGHTS], 1)}
    arrays["prep"] = np.concatenate([A("Wq"), A("Wk"), A("Wv"), F("W_r").T, F("W_k").T], 1)
    arrays["taps"] = np.concatenate([rows(A("conv_w_" + n).T) for n in "qkv"], 1)
    arrays["fw"] = C("fft_conv_w").transpose(2, 1, 0).reshape(TAPS, 4, 128, 512).transpose(2, 0, 1, 3).reshape(128, -1)
    arrays["x"] = A("hidden_states").transpose(0, 2, 1)
    arrays["tab"] = np.concatenate(list(shape_tables().values()), 1)
    arrays["sel"] = selector_tables()
    arrays["time"], arrays["fwd"], arrays["inv"] = dft_tables()
    return {k: np.ascontiguousarray(v) for k, v in arrays.items()}


def kernel(**inputs):
    import numpy as _np
    import concourse.bacc as _bacc
    from concourse import mybir as _mybir
    from concourse.bass_utils import run_bass_kernel_spmd as _run

    nc = _bacc.Bacc("TRN2", target_bir_lowering=False, num_devices=1, dynamic_dma_scratch_size=1024)
    arrays, d = {}, {}
    for name, a in lay_out(inputs, _np).items():
        arrays[f"in_{name}_dram"] = a
        d[name] = nc.dram_tensor(f"in_{name}_dram", a.shape, _mybir.dt.from_np(a.dtype), kind="ExternalInput").ap()
    d["folded"] = nc.dram_tensor("folded_dram", (128, TAPS * 2048), F32, kind="Internal").ap()
    out = nc.dram_tensor("out_0_dram", (B, D, L), F32, kind="ExternalOutput").ap()
    build(nc, d, out)
    r = _run(nc, [arrays], core_ids=[0])
    return r.results[0]["out_0_dram"].transpose(0, 2, 1)
```
